# Optimizing a Trainium2 kernel written in Bass

```python
import numpy as np
import jax
import jax.numpy as jnp

def _softmax(x, axis=-1):
    return jax.nn.softmax(x, axis=axis)

def _gelu(x):
    return jax.nn.gelu(x, approximate=True)

def _silu(x):
    return jax.nn.silu(x)

def _sigmoid(x):
    return jax.nn.sigmoid(x)

def _layernorm(x, axis=-1, eps=1e-05):
    m = jnp.mean(x, axis=axis, keepdims=True)
    v = jnp.var(x, axis=axis, keepdims=True)
    return (x - m) / jnp.sqrt(v + eps)

def _scatter_add(tgt, idx, src, axis=0):
    return tgt.at[idx].add(src)

def _segment_sum(src, seg, n):
    return jax.ops.segment_sum(src, seg, n)
kernel_name = 'mk_early_fusion_d2_tok_img1024_r4_6b12f5'

def setup_inputs(seed: int=0):
    np.random.seed(seed)
    _w = jnp.asarray

    def _rec_inputs():
        import jax
        import jax.numpy as jnp
        _rk = jax.random.key(seed)
        x = -4.65018e-05 + 0.999886 * jax.random.normal(jax.random.fold_in(_rk, 1), (64, 3, 96, 96), jnp.float32)
        txt = 0.00060944 + 1.00003 * jax.random.normal(jax.random.fold_in(_rk, 2), (64, 77, 256), jnp.float32)
        return (x, txt)
    x, txt = _rec_inputs()

    def _L0_tok_setup():
        import jax, jax.numpy as jnp
        import numpy as np
        P = 16
        key = jax.random.key(seed)
        k1, k2, k3 = jax.random.split(key, 3)
        B, C, H, W_ = (64, 3, 128, 128)
        D = 256
        x = jax.random.normal(k1, (B, C, H, W_), dtype=jnp.float32)
        W = jax.random.normal(k2, (C * P * P, D), dtype=jnp.float32) * (1.0 / np.sqrt(C * P * P))
        b = jax.random.normal(k3, (D,), dtype=jnp.float32) * 0.01
        return {'x': x, 'W': W, 'b': b}
    _L0_tok_all = _L0_tok_setup()
    _L0_tok_in = {k: v for k, v in _L0_tok_all.items() if k in ('W', 'b')}
    del _L0_tok_all

    def _L0_attn_setup():
        import jax, jax.numpy as jnp
        import numpy as np
        B, S = (2, 512)
        HIDDEN, MLP = (256, 512)
        N_STATE, DT_RANK, CONV_K = (16, 64, 4)

        def _causal_depthwise_conv(u, conv_w, conv_b):
            u_pad = jnp.pad(u, ((0, 0), (CONV_K - 1, 0), (0, 0)))
            seq = u.shape[1]
            y = sum((u_pad[:, k:k + seq, :] * conv_w[:, k] for k in range(CONV_K)))
            return y + conv_b

        def _selective_scan(u, A_log, x_proj_w, dt_proj_w, dt_proj_b, D_skip):
            xp = u @ x_proj_w
            delta = jax.nn.softplus(xp[..., :DT_RANK] @ dt_proj_w + dt_proj_b)
            Bm = xp[..., DT_RANK:DT_RANK + N_STATE]
            Cm = xp[..., DT_RANK + N_STATE:]
            A = -jnp.exp(A_log)
            dA = jnp.exp(delta[..., None] * A)
            dBu = delta[..., None] * Bm[:, :, None, :] * u[..., None]

            def step(h, inp):
                dA_t, dBu_t, C_t = inp
                h = dA_t * h + dBu_t
                y = jnp.einsum('bdn,bn->bd', h, C_t)
                return (h, y)
            h0 = jnp.zeros((u.shape[0], u.shape[2], N_STATE), u.dtype)
            _, ys = jax.lax.scan(step, h0, (dA.transpose(1, 0, 2, 3), dBu.transpose(1, 0, 2, 3), Cm.transpose(1, 0, 2)))
            return ys.transpose(1, 0, 2) + u * D_skip
        key = jax.random.key(seed)
        ks = jax.random.split(key, 14)
        s = 0.02
        return {'x': jax.random.normal(ks[0], (B, S, HIDDEN), jnp.float32), 'W1': jax.random.normal(ks[1], (HIDDEN, MLP), jnp.float32) * s, 'b1': jnp.zeros((MLP,), jnp.float32), 'W2': jax.random.normal(ks[2], (HIDDEN, MLP), jnp.float32) * s, 'b2': jnp.zeros((MLP,), jnp.float32), 'conv_w': jax.random.normal(ks[3], (MLP, CONV_K), jnp.float32) * s, 'conv_b': jnp.zeros((MLP,), jnp.float32), 'A_log': jnp.log(jnp.broadcast_to(jnp.arange(1, N_STATE + 1, dtype=jnp.float32), (MLP, N_STATE))), 'x_proj_w': jax.random.normal(ks[4], (MLP, DT_RANK + 2 * N_STATE), jnp.float32) * s, 'dt_proj_w': jax.random.normal(ks[5], (DT_RANK, MLP), jnp.float32) * s, 'dt_proj_b': jnp.full((MLP,), -4.0, jnp.float32), 'D_skip': jnp.ones((MLP,), jnp.float32), 'Wo': jax.random.normal(ks[6], (MLP, HIDDEN), jnp.float32) * s, 'bo': jnp.zeros((HIDDEN,), jnp.float32)}
    _L0_attn_all = _L0_attn_setup()
    _L0_attn_in = {k: v for k, v in _L0_attn_all.items() if k in ('W1', 'b1', 'W2', 'b2', 'conv_w', 'conv_b', 'A_log', 'x_proj_w', 'dt_proj_w', 'dt_proj_b', 'D_skip', 'Wo', 'bo')}
    del _L0_attn_all

    def _L0_ffn_setup():
        import jax, jax.numpy as jnp
        import numpy as np
        N_HEAD, N_ACTIVE, D_MODEL, D_ATTN = (16, 4, 256, 64)
        key = jax.random.key(seed)
        ks = jax.random.split(key, 12)
        s = 0.02
        B, S = (2, 1024)
        return {'x': jax.random.normal(ks[0], (B, S, D_MODEL), dtype=jnp.float32), 'Wq': jax.random.normal(ks[1], (D_MODEL, N_HEAD * D_ATTN), dtype=jnp.float32) * s, 'bq': jnp.zeros((N_HEAD * D_ATTN,), dtype=jnp.float32), 'Wk': jax.random.normal(ks[2], (D_MODEL, N_HEAD * D_ATTN), dtype=jnp.float32) * s, 'bk': jnp.zeros((N_HEAD * D_ATTN,), dtype=jnp.float32), 'Wv': jax.random.normal(ks[3], (D_MODEL, N_HEAD * D_ATTN), dtype=jnp.float32) * s, 'bv': jnp.zeros((N_HEAD * D_ATTN,), dtype=jnp.float32), 'Wr': jax.random.normal(ks[4], (D_MODEL, N_HEAD), dtype=jnp.float32) * s, 'br': jnp.zeros((N_HEAD,), dtype=jnp.float32), 'Wo': jax.random.normal(ks[5], (N_ACTIVE * D_ATTN, D_MODEL), dtype=jnp.float32) * s, 'bo': jnp.zeros((D_MODEL,), dtype=jnp.float32)}
    _L0_ffn_all = _L0_ffn_setup()
    _L0_ffn_in = {k: v for k, v in _L0_ffn_all.items() if k in ('Wq', 'bq', 'Wk', 'bk', 'Wv', 'bv', 'Wr', 'br', 'Wo', 'bo')}
    del _L0_ffn_all

    def _L1_attn_setup():
        import jax, jax.numpy as jnp
        import numpy as np
        import math
        N_HEAD = 16
        N_KV_HEAD = 4
        HEAD_DIM = 64
        ROPE_THETA = 10000.0

        def _rope_cache(T, D, dtype):
            inv_freq = 1.0 / ROPE_THETA ** (jnp.arange(0, D, 2, dtype=dtype) / D)
            t = jnp.arange(T, dtype=dtype)
            freqs = jnp.einsum('i,j->ij', t, inv_freq)
            return (jnp.cos(freqs)[None, None], jnp.sin(freqs)[None, None])

        def _apply_rope(x, cos, sin):
            x1 = x[..., ::2]
            x2 = x[..., 1::2]
            return jnp.concatenate([x1 * cos - x2 * sin, x1 * sin + x2 * cos], axis=-1)
        key = jax.random.key(seed)
        k0, k1, k2, k3, k4 = jax.random.split(key, 5)
        B, T, C = (4, 512, 256)
        scale = 0.02
        return {'x': jax.random.normal(k0, (B, T, C), dtype=jnp.float32), 'Wq': jax.random.normal(k1, (C, N_HEAD * HEAD_DIM), dtype=jnp.float32) * scale, 'Wk': jax.random.normal(k2, (C, N_KV_HEAD * HEAD_DIM), dtype=jnp.float32) * scale, 'Wv': jax.random.normal(k3, (C, N_KV_HEAD * HEAD_DIM), dtype=jnp.float32) * scale, 'Wo': jax.random.normal(k4, (N_HEAD * HEAD_DIM, C), dtype=jnp.float32) * scale}
    _L1_attn_all = _L1_attn_setup()
    _L1_attn_in = {k: v for k, v in _L1_attn_all.items() if k in ('Wq', 'Wk', 'Wv', 'Wo')}
    del _L1_attn_all

    def _L1_ffn_setup():
        import jax, jax.numpy as jnp
        import numpy as np
        NUM_EXPERTS = 8
        NUM_SELECTED = 2
        EXPERT_CAPACITY = 128
        NUM_GROUPS = 8

        def _routing(xg, w_router):
            G, T, H = xg.shape
            logits = jnp.einsum('gth,he->gte', xg, w_router)
            probs = jax.nn.softmax(logits, axis=-1)
            _gate, idx = jax.lax.top_k(probs, NUM_SELECTED)
            idx_kt = jnp.swapaxes(idx, 1, 2).reshape(G, -1)
            expert_mask = jax.nn.one_hot(idx_kt, NUM_EXPERTS, dtype=jnp.int32)
            priority = jnp.cumsum(expert_mask, axis=1) * expert_mask - 1
            priority = priority.reshape(G, NUM_SELECTED, T, NUM_EXPERTS)
            priority = jnp.swapaxes(priority, 1, 2).max(axis=2)
            dispatch = jax.nn.one_hot(priority, EXPERT_CAPACITY, dtype=xg.dtype)
            combine = probs[..., None] * dispatch
            return (dispatch, combine)
        key = jax.random.key(seed)
        k1, k2, k3, k4 = jax.random.split(key, 4)
        B, S, H, F = (8, 512, 256, 1024)
        return {'x': jax.random.normal(k1, (B, S, H), jnp.float32), 'w_router': jax.random.normal(k2, (H, NUM_EXPERTS), jnp.float32) * 0.02, 'wi': jax.random.normal(k3, (NUM_EXPERTS, H, F), jnp.float32) * 0.02, 'wo': jax.random.normal(k4, (NUM_EXPERTS, F, H), jnp.float32) * 0.02}
    _L1_ffn_all = _L1_ffn_setup()
    _L1_ffn_in = {k: v for k, v in _L1_ffn_all.items() if k in ('w_router', 'wi', 'wo')}
    del _L1_ffn_all
    return {'x': x, 'txt': txt, 'L0_tok_W': _L0_tok_in['W'], 'L0_tok_b': _L0_tok_in['b'], 'L0_attn_W1': _L0_attn_in['W1'], 'L0_attn_b1': _L0_attn_in['b1'], 'L0_attn_W2': _L0_attn_in['W2'], 'L0_attn_b2': _L0_attn_in['b2'], 'L0_attn_conv_w': _L0_attn_in['conv_w'], 'L0_attn_conv_b': _L0_attn_in['conv_b'], 'L0_attn_A_log': _L0_attn_in['A_log'], 'L0_attn_x_proj_w': _L0_attn_in['x_proj_w'], 'L0_attn_dt_proj_w': _L0_attn_in['dt_proj_w'], 'L0_attn_dt_proj_b': _L0_attn_in['dt_proj_b'], 'L0_attn_D_skip': _L0_attn_in['D_skip'], 'L0_attn_Wo': _L0_attn_in['Wo'], 'L0_attn_bo': _L0_attn_in['bo'], 'L0_ffn_Wq': _L0_ffn_in['Wq'], 'L0_ffn_bq': _L0_ffn_in['bq'], 'L0_ffn_Wk': _L0_ffn_in['Wk'], 'L0_ffn_bk': _L0_ffn_in['bk'], 'L0_ffn_Wv': _L0_ffn_in['Wv'], 'L0_ffn_bv': _L0_ffn_in['bv'], 'L0_ffn_Wr': _L0_ffn_in['Wr'], 'L0_ffn_br': _L0_ffn_in['br'], 'L0_ffn_Wo': _L0_ffn_in['Wo'], 'L0_ffn_bo': _L0_ffn_in['bo'], 'L1_attn_Wq': _L1_attn_in['Wq'], 'L1_attn_Wk': _L1_attn_in['Wk'], 'L1_attn_Wv': _L1_attn_in['Wv'], 'L1_attn_Wo': _L1_attn_in['Wo'], 'L1_ffn_w_router': _L1_ffn_in['w_router'], 'L1_ffn_wi': _L1_ffn_in['wi'], 'L1_ffn_wo': _L1_ffn_in['wo']}

def reference(x, txt, L0_tok_W, L0_tok_b, L0_attn_W1, L0_attn_b1, L0_attn_W2, L0_attn_b2, L0_attn_conv_w, L0_attn_conv_b, L0_attn_A_log, L0_attn_x_proj_w, L0_attn_dt_proj_w, L0_attn_dt_proj_b, L0_attn_D_skip, L0_attn_Wo, L0_attn_bo, L0_ffn_Wq, L0_ffn_bq, L0_ffn_Wk, L0_ffn_bk, L0_ffn_Wv, L0_ffn_bv, L0_ffn_Wr, L0_ffn_br, L0_ffn_Wo, L0_ffn_bo, L1_attn_Wq, L1_attn_Wk, L1_attn_Wv, L1_attn_Wo, L1_ffn_w_router, L1_ffn_wi, L1_ffn_wo):
    import jax
    import jax.numpy as jnp

    def _L0_tok_ref(x, W, b):
        import jax, jax.numpy as jnp
        import numpy as np
        P = 16
        B, C, H, W_ = x.shape
        nh, nw = (H // P, W_ // P)
        patches = x.reshape(B, C, nh, P, nw, P)
        patches = patches.transpose(0, 2, 4, 1, 3, 5)
        patches = patches.reshape(B, nh * nw, C * P * P)
        return jnp.einsum('bnk,kd->bnd', patches, W) + b

    def _L0_attn_ref(x, W1, b1, W2, b2, conv_w, conv_b, A_log, x_proj_w, dt_proj_w, dt_proj_b, D_skip, Wo, bo):
        import jax, jax.numpy as jnp
        import numpy as np
        B, S = (2, 512)
        HIDDEN, MLP = (256, 512)
        N_STATE, DT_RANK, CONV_K = (16, 64, 4)

        def _causal_depthwise_conv(u, conv_w, conv_b):
            u_pad = jnp.pad(u, ((0, 0), (CONV_K - 1, 0), (0, 0)))
            seq = u.shape[1]
            y = sum((u_pad[:, k:k + seq, :] * conv_w[:, k] for k in range(CONV_K)))
            return y + conv_b

        def _selective_scan(u, A_log, x_proj_w, dt_proj_w, dt_proj_b, D_skip):
            xp = u @ x_proj_w
            delta = jax.nn.softplus(xp[..., :DT_RANK] @ dt_proj_w + dt_proj_b)
            Bm = xp[..., DT_RANK:DT_RANK + N_STATE]
            Cm = xp[..., DT_RANK + N_STATE:]
            A = -jnp.exp(A_log)
            dA = jnp.exp(delta[..., None] * A)
            dBu = delta[..., None] * Bm[:, :, None, :] * u[..., None]

            def step(h, inp):
                dA_t, dBu_t, C_t = inp
                h = dA_t * h + dBu_t
                y = jnp.einsum('bdn,bn->bd', h, C_t)
                return (h, y)
            h0 = jnp.zeros((u.shape[0], u.shape[2], N_STATE), u.dtype)
            _, ys = jax.lax.scan(step, h0, (dA.transpose(1, 0, 2, 3), dBu.transpose(1, 0, 2, 3), Cm.transpose(1, 0, 2)))
            return ys.transpose(1, 0, 2) + u * D_skip
        gate = jax.nn.sigmoid(x @ W2 + b2)
        u = x @ W1 + b1
        u = jax.nn.sigmoid(_causal_depthwise_conv(u, conv_w, conv_b))
        y = _selective_scan(u, A_log, x_proj_w, dt_proj_w, dt_proj_b, D_skip)
        return y * gate @ Wo + bo

    def _L0_ffn_ref(x, Wq, bq, Wk, bk, Wv, bv, Wr, br, Wo, bo):
        import jax, jax.numpy as jnp
        import numpy as np
        N_HEAD, N_ACTIVE, D_MODEL, D_ATTN = (16, 4, 256, 64)
        B, S, D = x.shape
        H, K, dh = (N_HEAD, N_ACTIVE, D_ATTN)
        dist = jax.nn.softmax(jnp.mean(x @ Wr + br, axis=1), axis=-1)
        top_vals, top_idx = jax.lax.top_k(dist, K)
        sparse = jnp.zeros_like(dist).at[jnp.arange(B)[:, None], top_idx].set(top_vals)
        gates_all = jax.nn.softmax(sparse, axis=1)
        g = jnp.take_along_axis(gates_all, top_idx, axis=1)[:, :, None, None]

        def proj(W, b):
            return (x @ W + b).reshape(B, S, H, dh).transpose(0, 2, 1, 3)
        Q, Kt, V = (proj(Wq, bq), proj(Wk, bk), proj(Wv, bv))
        idx = top_idx[:, :, None, None]
        Qk = jnp.take_along_axis(Q, idx, axis=1) * g
        Kk = jnp.take_along_axis(Kt, idx, axis=1) * g
        Vk = jnp.take_along_axis(V, idx, axis=1) * g
        scores = jnp.einsum('bksd,bktd->bkst', Qk, Kk) / jnp.sqrt(jnp.float32(dh))
        attn = jax.nn.softmax(scores, axis=-1)
        out = jnp.einsum('bkst,bktd->bksd', attn, Vk)
        out = out.transpose(0, 2, 1, 3).reshape(B, S, K * dh)
        return out @ Wo + bo

    def _L1_attn_ref(x, Wq, Wk, Wv, Wo):
        import jax, jax.numpy as jnp
        import numpy as np
        import math
        N_HEAD = 16
        N_KV_HEAD = 4
        HEAD_DIM = 64
        ROPE_THETA = 10000.0

        def _rope_cache(T, D, dtype):
            inv_freq = 1.0 / ROPE_THETA ** (jnp.arange(0, D, 2, dtype=dtype) / D)
            t = jnp.arange(T, dtype=dtype)
            freqs = jnp.einsum('i,j->ij', t, inv_freq)
            return (jnp.cos(freqs)[None, None], jnp.sin(freqs)[None, None])

        def _apply_rope(x, cos, sin):
            x1 = x[..., ::2]
            x2 = x[..., 1::2]
            return jnp.concatenate([x1 * cos - x2 * sin, x1 * sin + x2 * cos], axis=-1)
        B, T, C = x.shape
        H, Hkv, D = (N_HEAD, N_KV_HEAD, HEAD_DIM)
        q = (x @ Wq).reshape(B, T, H, D).transpose(0, 2, 1, 3)
        k = (x @ Wk).reshape(B, T, Hkv, D).transpose(0, 2, 1, 3)
        v = (x @ Wv).reshape(B, T, Hkv, D).transpose(0, 2, 1, 3)
        rep = H // Hkv
        k = jnp.repeat(k, rep, axis=1)
        v = jnp.repeat(v, rep, axis=1)
        cos, sin = _rope_cache(T, D, x.dtype)
        q = _apply_rope(q, cos, sin)
        k = _apply_rope(k, cos, sin)
        att = jnp.einsum('bhtd,bhsd->bhts', q, k) / math.sqrt(D)
        mask = jnp.tril(jnp.ones((T, T), dtype=bool))
        att = jnp.where(mask, att, -jnp.inf)
        att = jax.nn.softmax(att, axis=-1)
        y = jnp.einsum('bhts,bhsd->bhtd', att, v)
        y = y.transpose(0, 2, 1, 3).reshape(B, T, H * D)
        return y @ Wo

    def _L1_ffn_ref(x, w_router, wi, wo):
        import jax, jax.numpy as jnp
        import numpy as np
        NUM_EXPERTS = 8
        NUM_SELECTED = 2
        EXPERT_CAPACITY = 128
        NUM_GROUPS = 8

        def _routing(xg, w_router):
            G, T, H = xg.shape
            logits = jnp.einsum('gth,he->gte', xg, w_router)
            probs = jax.nn.softmax(logits, axis=-1)
            _gate, idx = jax.lax.top_k(probs, NUM_SELECTED)
            idx_kt = jnp.swapaxes(idx, 1, 2).reshape(G, -1)
            expert_mask = jax.nn.one_hot(idx_kt, NUM_EXPERTS, dtype=jnp.int32)
            priority = jnp.cumsum(expert_mask, axis=1) * expert_mask - 1
            priority = priority.reshape(G, NUM_SELECTED, T, NUM_EXPERTS)
            priority = jnp.swapaxes(priority, 1, 2).max(axis=2)
            dispatch = jax.nn.one_hot(priority, EXPERT_CAPACITY, dtype=xg.dtype)
            combine = probs[..., None] * dispatch
            return (dispatch, combine)
        B, S, H = x.shape
        T = B * S // NUM_GROUPS
        xg = x.reshape(NUM_GROUPS, T, H)
        dispatch, combine = _routing(xg, w_router)
        expert_in = jnp.einsum('gth,gtec->gech', xg, dispatch)
        h = jax.nn.gelu(jnp.einsum('gech,ehf->gecf', expert_in, wi))
        expert_out = jnp.einsum('gecf,efh->gech', h, wo)
        out = jnp.einsum('gech,gtec->gth', expert_out, combine)
        return out.reshape(B, S, H)
    h = _L0_tok_ref(x, L0_tok_W, L0_tok_b)
    h = jnp.concatenate([h, txt], axis=1)
    h = h + _L0_attn_ref(_layernorm(h, axis=-1), L0_attn_W1, L0_attn_b1, L0_attn_W2, L0_attn_b2, L0_attn_conv_w, L0_attn_conv_b, L0_attn_A_log, L0_attn_x_proj_w, L0_attn_dt_proj_w, L0_attn_dt_proj_b, L0_attn_D_skip, L0_attn_Wo, L0_attn_bo)
    h = h + _L0_ffn_ref(_layernorm(h, axis=-1), L0_ffn_Wq, L0_ffn_bq, L0_ffn_Wk, L0_ffn_bk, L0_ffn_Wv, L0_ffn_bv, L0_ffn_Wr, L0_ffn_br, L0_ffn_Wo, L0_ffn_bo)
    h = h + _L1_attn_ref(_layernorm(h, axis=-1), L1_attn_Wq, L1_attn_Wk, L1_attn_Wv, L1_attn_Wo)
    h = h + _L1_ffn_ref(_layernorm(h, axis=-1), L1_ffn_w_router, L1_ffn_wi, L1_ffn_wo)
    return h

_drawn_inputs = setup_inputs


def setup_inputs(seed=0):
    import zlib

    import numpy as np

    out = dict(_drawn_inputs(seed))
    spreads = {'L0_attn_b1': (0.0, 0.8),
     'L0_attn_b2': (0.0, 0.8),
     'L0_attn_conv_b': (0.0, 0.8),
     'L0_attn_dt_proj_b': (-4.0, 0.6),
     'L0_attn_D_skip': (1.0, 0.6),
     'L0_attn_bo': (0.0, 0.1),
     'L0_ffn_bq': (0.0, 2.0),
     'L0_ffn_bk': (0.0, 2.0),
     'L0_ffn_bv': (0.0, 0.8),
     'L0_ffn_br': (0.0, 0.8),
     'L0_ffn_bo': (0.0, 0.1)}
    factors = {'L0_tok_b': 8.0,
     'L0_attn_W1': 8.0,
     'L0_attn_W2': 3.045,
     'L0_attn_conv_w': 8.0,
     'L0_attn_A_log': 7.85,
     'L0_attn_x_proj_w': 8.0,
     'L0_attn_dt_proj_w': 8.0,
     'L0_ffn_Wq': 64.0,
     'L0_ffn_Wk': 64.0,
     'L0_ffn_Wv': 8.0,
     'L0_ffn_Wr': 8.0,
     'L0_ffn_Wo': 8.0,
     'L1_attn_Wq': 8.0,
     'L1_attn_Wk': 8.0,
     'L1_ffn_w_router': 8.304,
     'L1_ffn_wi': 2.704}
    for name, (base, spread) in spreads.items():
        noise = np.random.default_rng([zlib.crc32(name.encode()), seed]).standard_normal(out[name].shape)
        drawn = base * np.exp(spread * noise) if base else spread * noise
        out[name] = jnp.asarray(drawn.astype(out[name].dtype))
    for name, factor in factors.items():
        out[name] = (out[name] * factor).astype(out[name].dtype)
    return out
```

```python
from contextlib import ExitStack

import concourse.bass as bass
from concourse import mybir

ALU = mybir.AluOpType
ACT = mybir.ActivationFunctionType
AX_X = mybir.AxisListType.X
F32 = mybir.dt.float32
BF16 = mybir.dt.bfloat16
I32 = mybir.dt.int32
U32 = mybir.dt.uint32

P = 128
SAMPLES = 64
IMG = 36
ROWS = 64
TXT = 77
T = IMG + TXT
D = 256
KD = D // P
QUAD = 4
NQ = SAMPLES // QUAD
C = QUAD * T
KTOK = 768 // P
INNER = 512
J = INNER // P
NS = 16
RANK = 64
TAPS = 4
EPS = 1e-5

COL_B1, COL_B2, COL_CW, COL_CB, COL_DTB, COL_DS, COL_AL = 0, 4, 8, 24, 28, 32, 36
COLS = COL_AL + J * NS


class Memory:

    def __init__(self, nc, ctx, prefix):
        self.nc, self.ctx, self.prefix = nc, ctx, prefix
        self.semaphores = []

    def sb(self, name, shape, dt=F32):
        return self.ctx.enter_context(self.nc.sbuf_tensor(self.prefix + name, shape, dt))

    def ps(self, name, shape, dt=F32):
        return self.ctx.enter_context(self.nc.psum_tensor(self.prefix + name, shape, dt))

    def sem(self, name):
        self.semaphores.append(self.ctx.enter_context(self.nc.semaphore(self.prefix + name)))
        return self.semaphores[-1]


def layer_norm_stats(e, tile, stats, mv, veps, sem, base, spare):
    for s in range(QUAD):
        ins = e.bn_stats(stats[0:T, s, :], tile[0:T, s, :])
    ins.then_inc(sem, 1)
    e.wait_ge(sem, base + 1)
    e.memset(spare, 0.0)
    for s in range(QUAD):
        ins = e.bn_aggr(mv[0:T, s, :], stats[0:T, s, :])
    ins.then_inc(sem, 1)
    e.wait_ge(sem, base + 2)
    e.tensor_scalar(veps[0:T, :], mv[0:T, :, 1], EPS, None, ALU.add).then_inc(sem, 1)


def mixer_phase(nc, io, idf, h_out):
    with ExitStack() as ctx:
        m = Memory(nc, ctx, "m_")
        tokw = m.sb("tokw", [P, KTOK, D])
        w1 = m.sb("w1", [P, KD, INNER])
        w2 = m.sb("w2", [P, KD, INNER])
        xpw = m.sb("xpw", [P, J, 96])
        dtw = m.sb("dtw", [RANK, INNER])
        wo = m.sb("wo", [P, J, D])
        cols = m.sb("cols", [P, COLS])
        brow = m.sb("brow", [1, 2, D])
        nega = m.sb("nega", [P, J * NS])
        ones = m.sb("ones", [1, P])
        sel = m.sb("sel", [96, 2 * NS, P], BF16)
        half = m.sb("half", [P, QUAD])
        patches = [m.sb(f"patches{b}", [P, KTOK, QUAD * ROWS]) for b in (0, 1)]
        h = [m.sb(f"h{b}", [P, QUAD, D]) for b in (0, 1)]
        u = [m.sb(f"u{b}", [P, J, QUAD, T]) for b in (0, 1)]
        gate = [m.sb(f"gate{b}", [P, J, QUAD, T]) for b in (0, 1)]
        delta = [m.sb(f"delta{b}", [P, J, QUAD, T]) for b in (0, 1)]
        du = [m.sb(f"du{b}", [P, J, QUAD, T]) for b in (0, 1)]
        bc = [m.sb(f"bc{b}", [96, C], BF16) for b in (0, 1)]
        stats = m.sb("stats", [P, QUAD, 6])
        mv = m.sb("mv", [P, QUAD, 2])
        spare = m.sb("spare", [1, 1])
        veps = m.sb("veps", [P, QUAD])
        rstd = m.sb("rstd", [P, QUAD])
        xn = m.sb("xn", [P, QUAD, D])
        xnt = m.sb("xnt", [P, KD, C])
        upad = m.sb("upad", [P, J, QUAD, T + TAPS - 1])
        dts = m.sb("dts", [RANK, C])
        rest = m.sb("rest", [P, C])
        absz = m.sb("absz", [P, J, QUAD, T])
        lnw = m.sb("lnw", [P, J, QUAD, T])
        cs = [m.sb(f"cs{b}", [P, C]) for b in range(4)]
        bs = [m.sb(f"bs{b}", [P, C]) for b in range(4)]
        da = [m.sb(f"da{b}", [P, J, QUAD, T]) for b in (0, 1)]
        dbu = [m.sb(f"dbu{b}", [P, J, QUAD, T]) for b in (0, 1)]
        hs = [m.sb(f"hs{b}", [P, J, QUAD, T]) for b in (0, 1)]
        py = m.ps("py", [P, J, 512])
        pb = m.ps("pb", [P, 512])
        pc = m.ps("pc", [P, 512])
        pp = [m.ps(f"pp{b}", [P, 512]) for b in (0, 1)]

        weights = m.sem("weights")
        loaded = [m.sem(f"loaded{b}") for b in (0, 1)]
        stored = [m.sem(f"stored{b}") for b in (0, 1)]
        consts = m.sem("consts")
        dconsts = m.sem("dconsts")
        aconsts = m.sem("aconsts")
        proj = m.sem("proj")
        a_gate = m.sem("a_gate")
        a_dt = m.sem("a_dt")
        d_tok = m.sem("d_tok")
        d_ln = m.sem("d_ln")
        g_rstd = m.sem("g_rstd")
        d_xn = m.sem("d_xn")
        a_xnt = m.sem("a_xnt")
        a_upad = m.sem("a_upad")
        d_conv = m.sem("d_conv")
        a_u = m.sem("a_u")
        d_bc = m.sem("d_bc")
        a_sp = m.sem("a_sp")
        d_sp = m.sem("d_sp")
        t_b = m.sem("t_b")
        t_c = m.sem("t_c")
        a_bs = m.sem("a_bs")
        a_cs = m.sem("a_cs")
        a_da = m.sem("a_da")
        g_dbu = m.sem("g_dbu")
        d_scan = m.sem("d_scan")
        d_hc = m.sem("d_hc")
        t_y = m.sem("t_y")
        d_yg = m.sem("d_yg")
        d_h = m.sem("d_h")

        PRE, POST = 16, 2

        def use(q, k):
            if isinstance(q, int) and q == 0:
                return k
            return q * (PRE + POST) - POST + k

        def out_use(q, r):
            if isinstance(q, int) and q == NQ - 1:
                return NQ * (PRE + POST) - POST + r
            return q * (PRE + POST) + 2 * PRE + r

        TOK, XT, U, G, XP, DT = 0, 1, 3, 7, 11, 12

        block = ctx.enter_context(nc.Block())

        @block.sync
        def _(sp):
            sp.dma_start(tokw[:], io["tokw"].rearrange("(k p) n -> p k n", p=P)).then_inc(weights, 16)
            sp.dma_start(w1[:], io["w1"].rearrange("(k p) n -> p k n", p=P)).then_inc(weights, 16)
            sp.dma_start(w2[:], io["w2"].rearrange("(k p) n -> p k n", p=P)).then_inc(weights, 16)
            sp.dma_start(xpw[:], io["xpw"].rearrange("(k p) n -> p k n", p=P)).then_inc(weights, 16)
            sp.dma_start(dtw[:], io["dtw"]).then_inc(weights, 16)
            sp.dma_start(wo[:], io["wo0"].rearrange("(k p) n -> p k n", p=P)).then_inc(weights, 16)
            sp.dma_start(cols[:], io["cols"]).then_inc(weights, 16)
            sp.dma_start(brow[:], io["brow"][:, 0:2, :]).then_inc(weights, 16)

            def load(q, b, i):
                if i is not None:
                    sp.wait_ge(stored[b], 16 * (i + 1))
                sp.dma_start(patches[b][:], 
                             io["patches"][bass.ds(q, 1), :, :, :].rearrange("a p k n -> (a p) k n"))\
                    .then_inc(loaded[b], 16)
                sp.dma_start(h[b][IMG:T, :, :],
                             io["txt"][bass.ds(q * QUAD, QUAD), :, :].rearrange("s t d -> t s d"))\
                    .then_inc(loaded[b], 16)

            def store(q, b):
                sp.wait_ge(d_h, q * 2 + 2)
                sp.dma_start(h_out[bass.ds(q * QUAD, QUAD), :, :].rearrange("s t d -> t s d"),
                             h[b][0:T, :, :]).then_inc(stored[b], 16)

            load(0, 0, None)
            load(1, 1, None)
            with sp.Fori(0, NQ // 2 - 1) as i:
                for b in (0, 1):
                    store(2 * i + b, b)
                    load(2 * i + (b + 2), b, i)
            for b in (0, 1):
                store(NQ - 2 + b, b)
                sp.wait_ge(stored[b], 16 * (NQ // 2))

        @block.gpsimd
        def _(pool):
            pool.memset(ones[:], 1.0).then_inc(consts, 1)
            pool.memset(half[:], -0.5).then_inc(consts, 1)
            pool.memset(sel[:], 0.0).then_inc(consts, 1)
            for b in (0, 1):
                pool.memset(da[b][:, :, :, 0:1], 0.0).then_inc(consts, 1)
            pool.memset(upad[:, :, :, 0:TAPS - 1], 0.0).then_inc(consts, 1)
            pool.wait_ge(consts, 6)
            for a in range(3):
                part = sel[32 * a:32 * a + 32, :, :]
                pool.affine_select(out=part, in_=part, compare_op=ALU.not_equal, fill=1.0, base=0,
                                   pattern=[[-1, 2 * NS], [0, P]], channel_multiplier=1).then_inc(consts, 1)

            def pre(slot, q, b):
                if slot == 5:
                    pool.wait_ge(d_ln, q * 3 + 3)
                    pool.tensor_tensor(rstd[0:T, :], veps[0:T, :], half[0:T, :], ALU.pow).then_inc(g_rstd, 1)

            def products(n, q, b):
                pool.wait_ge(a_bs, q * NS + (n + 1))
                if n == 0:
                    pool.wait_ge(d_sp, q * 5 + 5)
                if not (first(q) and n < 2):
                    pool.wait_ge(d_scan, q * NS + (n - 1))
                pool.tensor_tensor(dbu[n % 2][:].rearrange("p j s t -> p j (s t)"),
                                   du[b][:].rearrange("p j s t -> p j (s t)"),
                                   bs[n % 4][:, :].unsqueeze(1).to_broadcast([P, J, C]), ALU.mult).then_inc(g_dbu, 1)

            def step(n, q, b, more):
                ahead(products, n, 1, q, b, more)

            run_quads(pool, pre, step, lambda: products(0, 0, 0))

        @block.scalar
        def _(act):
            act.wait_ge(weights, 128)
            act.activation(nega[:], cols[:, COL_AL:COL_AL + J * NS], ACT.Exp).then_inc(aconsts, 1)
            act.wait_ge(aconsts, 1)
            act.activation(nega[:], nega[:], ACT.Copy, scale=-1.0).then_inc(aconsts, 1)
            act.wait_ge(aconsts, 2)
            act.wait_ge(consts, 9)

            def pre(slot, q, b):
                if slot == 7:
                    act.wait_ge(proj, use(q, XT) + KD)
                    for k in range(KD):
                        act.activation(xnt[:, k, :], pp[(XT + k) % 2][:, 0:C], ACT.Copy).then_inc(a_xnt, 1)

                if slot in (8, 9):
                    for j in (2 * slot - 16, 2 * slot - 15):
                        act.wait_ge(proj, use(q, U + j) + 1)
                        if j == 0:
                            act.wait_ge(d_sp, q * 5)
                        act.activation(upad[:, j, :, TAPS - 1:], pp[(U + j) % 2][:, 0:C].rearrange("p (s t) -> p s t", s=QUAD),
                                       ACT.Identity, bias=cols[:, COL_B1 + j:COL_B1 + j + 1])\
                           .then_inc(a_upad, 1)
                if slot in (10, 11):
                    for j in (2 * slot - 20, 2 * slot - 19):
                        act.wait_ge(proj, use(q, G + j) + 1)
                        act.activation(gate[b][:, j, :, :].rearrange("p s t -> p (s t)"), pp[(G + j) % 2][:, 0:C],
                                       ACT.Sigmoid, bias=cols[:, COL_B2 + j:COL_B2 + j + 1]).then_inc(a_gate, 1)

                        act.wait_ge(d_conv, q * 16 + (4 * j + 4))
                        act.activation(u[b][:, j, :, :], u[b][:, j, :, :], ACT.Sigmoid).then_inc(a_u, 1)
                if slot == 13:
                    for j in range(J):
                        act.wait_ge(proj, use(q, DT + j) + 1)
                        zin = pp[(DT + j) % 2][:, 0:C]
                        bias = cols[:, COL_DTB + j:COL_DTB + j + 1]
                        act.activation(absz[:, j, :, :].rearrange("p s t -> p (s t)"), zin, ACT.Abs, bias=bias)
                        act.activation(delta[b][:, j, :, :].rearrange("p s t -> p (s t)"), zin, ACT.Relu, bias=bias)\
                            .then_inc(a_dt, 1)

                if slot == 13:
                    act.wait_ge(a_dt, q * J + J)
                    act.activation(absz[:], absz[:], ACT.Exp, scale=-1.0).then_inc(a_sp, 1)
                    act.wait_ge(a_sp, q * 2 + 1)
                    act.activation(lnw[:], absz[:], ACT.Ln, bias=1.0).then_inc(a_sp, 1)

            def rows(n, q, b):
                act.wait_ge(t_b, q * NS + (n + 1))
                if not (first(q) and n < 4):
                    act.wait_ge(g_dbu, q * NS + (n - 3))
                act.activation(bs[n % 4][:], pb[:, 0:C], ACT.Copy).then_inc(a_bs, 1)
                act.wait_ge(t_c, q * NS + (n + 1))
                if not (first(q) and n < 4):
                    act.wait_ge(d_hc, q * NS + (n - 3))
                act.activation(cs[n % 4][:], pc[:, 0:C], ACT.Copy).then_inc(a_cs, 1)

            def decays(n, q, b):
                if n == 0:
                    act.wait_ge(d_sp, q * 5 + 4)
                if not (first(q) and n < 2):
                    act.wait_ge(d_scan, q * NS + (n - 1))
                for j in range(J):
                    ins = act.activation(da[n % 2][:, j, :, 1:T], delta[b][:, j, :, 1:T], ACT.Exp,
                                         scale=nega[:, j * NS + n:j * NS + n + 1])
                ins.then_inc(a_da, 1)

            def step(n, q, b, more):
                ahead(decays, n, 1, q, b, more)
                ahead(rows, n, 3, q, b, more)

            def start():
                for n in range(3):
                    rows(n, 0, 0)
                decays(0, 0, 0)

            run_quads(act, pre, step, start)

        @block.vector
        def _(dve):
            dve.wait_ge(weights, 128)
            dve.wait_ge(consts, 9)

            def pre(slot, q, b, i):
                if slot == 4:
                    dve.wait_ge(loaded[b], 32 * (i + 1))
                    dve.wait_ge(proj, use(q, TOK) + 1)
                    for r in (0, 1):
                        ins = dve.tensor_copy(h[b][0:IMG, r::2, :],
                                              pp[TOK % 2][64 * r:64 * r + IMG, :].rearrange("p (a d) -> p a d", a=2))
                    ins.then_inc(d_tok, 1)
                    dve.wait_ge(d_tok, q + 1)
                    layer_norm_stats(dve, h[b], stats, mv, veps, d_ln, q * 3, spare[:])
                if slot == 6:
                    dve.wait_ge(g_rstd, q + 1)
                    for s in range(QUAD):
                        ins = dve.tensor_scalar(xn[0:T, s, :], h[b][0:T, s, :], mv[0:T, s, 0:1], rstd[0:T, s:s + 1],
                                                ALU.subtract, ALU.mult)
                    ins.then_inc(d_xn, 1)
                if slot in (8, 9):
                    for j in (2 * slot - 16, 2 * slot - 15):
                        dve.wait_ge(a_upad, q * J + (j + 1))
                        out = u[b][:, j, :, :]
                        for k in range(TAPS):
                            w = cols[:, COL_CW + j * TAPS + k:COL_CW + j * TAPS + k + 1]
                            src = upad[:, j, :, k:k + T]
                            if k == 0:
                                dve.tensor_scalar(out, src, w, cols[:, COL_CB + j:COL_CB + j + 1],
                                                  ALU.mult, ALU.add).then_inc(d_conv, 1)
                            else:
                                dve.wait_ge(d_conv, q * 16 + (4 * j + k))
                                dve.scalar_tensor_tensor(out=out, in0=src, scalar=w, in1=out,
                                                         op0=ALU.mult, op1=ALU.add).then_inc(d_conv, 1)
                if slot == 12:
                    dve.wait_ge(proj, use(q, XP) + 1)
                    src = pp[XP % 2]
                    dve.tensor_copy(dts[:], src[0:RANK, 0:C])
                    dve.tensor_copy(bc[b][0:32, :], src[64:96, 0:C]).then_inc(d_bc, 1)
                    dve.wait_ge(d_bc, q * 4 + 1)
                    dve.tensor_tensor(rest[32:64, :], src[64:96, 0:C], bc[b][0:32, :], ALU.subtract)\
                        .then_inc(d_bc, 1)
                    dve.wait_ge(d_bc, q * 4 + 2)
                    dve.tensor_copy(bc[b][32:64, :], rest[32:64, :]).then_inc(d_bc, 1)
                    dve.wait_ge(d_bc, q * 4 + 3)
                    dve.tensor_tensor(bc[b][64:96, :], rest[32:64, :], bc[b][32:64, :], ALU.subtract).then_inc(d_bc, 1)
                if slot == 14:
                    dve.wait_ge(a_sp, q * 2 + 2)
                    w = upad[:, :, :, TAPS - 1:]
                    dve.tensor_scalar(w, absz[:], 1.0, -1.0, ALU.add, ALU.add).then_inc(d_sp, 1)
                    dve.wait_ge(d_sp, q * 5 + 1)
                    dve.tensor_tensor(w, absz[:], w, ALU.subtract).then_inc(d_sp, 1)
                    dve.wait_ge(d_sp, q * 5 + 2)
                    dve.tensor_tensor(lnw[:], lnw[:], w, ALU.add).then_inc(d_sp, 1)
                    dve.wait_ge(d_sp, q * 5 + 3)
                    dve.tensor_tensor(delta[b][:], delta[b][:], lnw[:], ALU.add).then_inc(d_sp, 1)
                    dve.wait_ge(d_sp, q * 5 + 4)
                    dve.wait_ge(a_u, q * J + J)
                    dve.tensor_tensor(du[b][:], delta[b][:], u[b][:], ALU.mult).then_inc(d_sp, 1)

            def step(n, q, b, more):
                cell = hs[n % 2]
                flat = cell[:].rearrange("p j s t -> p (j s t)")
                dve.wait_ge(a_da, q * NS + (n + 1))
                dve.wait_ge(g_dbu, q * NS + (n + 1))
                if not (first(q) and n < 2):
                    dve.wait_ge(t_y, q * NS + (n - 1))
                dve.tensor_tensor_scan(flat, da[n % 2][:].rearrange("p j s t -> p (j s t)"),
                                       dbu[n % 2][:].rearrange("p j s t -> p (j s t)"), 0.0,
                                       ALU.mult, ALU.add).then_inc(d_scan, 1)
                dve.wait_ge(d_scan, q * NS + (n + 1))
                dve.wait_ge(a_cs, q * NS + (n + 1))
                v = cell[:].rearrange("p j s t -> p j (s t)")
                dve.tensor_tensor(v, v, cs[n % 4][:, :].unsqueeze(1).to_broadcast([P, J, C]), ALU.mult).then_inc(d_hc, 1)
                if n == 1 and not first(q):
                    residual(q - 1, 1 - b)
                if n == NS - 1:
                    gated(q, b)
                    if not more:
                        residual(q, b)

            def gated(q, b):
                dve.wait_ge(t_y, q * NS + NS)
                for j in range(J):
                    flat = u[b][:, j, :, :].rearrange("p s t -> p (s t)")
                    ins = dve.scalar_tensor_tensor(out=flat, in0=flat, scalar=cols[:, COL_DS + j:COL_DS + j + 1],
                                                   in1=py[:, j, 0:C], op0=ALU.mult, op1=ALU.add)
                ins.then_inc(d_yg, 1)
                dve.wait_ge(d_yg, q * 2 + 1)
                dve.tensor_tensor(u[b][:], u[b][:], gate[b][:], ALU.mult).then_inc(d_yg, 1)

            def residual(q, b):
                for r in (0, 1):
                    dve.wait_ge(proj, out_use(q, r) + 1)
                    part = h[b][0:T, 2 * r:2 * r + 2, :]
                    dve.tensor_tensor(part, part, pp[r][0:T, :].rearrange("p (a d) -> p a d", a=2), ALU.add)\
                        .then_inc(d_h, 1)

            run_quads(dve, pre, step, lambda: None, pair_index=True)

        @block.tensor
        def _(pe):
            pe.wait_ge(weights, 128)
            pe.wait_ge(consts, 9)

            def pre(slot, q, b, i):
                if slot == 3:
                    pe.wait_ge(loaded[b], 32 * (i + 1))
                    pe.wait_ge(a_dt, q * J)
                    if not first(q) and not one(q):
                        pe.wait_ge(d_h, (q - 2) * 2 + 2)
                    for a in (0, 1):
                        out = pp[TOK % 2][:, a * D:(a + 1) * D]
                        for k in range(KTOK):
                            pe.matmul(out, patches[b][:, k, a * P:(a + 1) * P], tokw[:, k, :], start=(k == 0), stop=False)
                        ins = pe.matmul(out, ones[:, :], brow[:, 0, :], start=False, stop=True)
                    ins.then_inc(proj, 1)
                if slot == 6:
                    pe.wait_ge(d_xn, q + 1)
                    for k in range(KD):
                        if k == 1:
                            pe.wait_ge(d_tok, q + 1)
                        for s in range(QUAD):
                            ins = pe.transpose(pp[(XT + k) % 2][:, s * T:(s + 1) * T], xn[0:T, s, k * P:(k + 1) * P],
                                               idf[0:T, 0:T])
                        ins.then_inc(proj, 1)
                if slot in (7, 8):
                    project(q, U, w1, slot - 7, (None, a_upad))
                if slot in (9, 10):
                    project(q, G, w2, slot - 9, (a_upad, a_gate))
                if slot == 11:
                    pe.wait_ge(a_gate, q * J + 3)
                    pe.wait_ge(a_u, q * J + J)
                    for j in range(J):
                        ins = pe.matmul(pp[XP % 2][0:96, 0:C], xpw[:, j, :], u[b][:, j, :, :].rearrange("p s t -> p (s t)"),
                                        start=(j == 0), stop=(j == J - 1))
                    ins.then_inc(proj, 1)
                if slot in (12, 13):
                    for j in (2 * slot - 24, 2 * slot - 23):
                        if j == 0:
                            pe.wait_ge(a_gate, q * J + J)
                        elif j == 1:
                            pe.wait_ge(d_bc, q * 4 + 2)
                        else:
                            pe.wait_ge(a_dt, q * J + (j - 1))
                        if j == 0:
                            pe.wait_ge(d_bc, q * 4 + 1)
                        pe.matmul(pp[(DT + j) % 2][:, 0:C], dtw[:, j * P:(j + 1) * P], dts[:],
                                  start=True, stop=True).then_inc(proj, 1)

            def project(q, first, w, part, empties):
                if part == 0:
                    pe.wait_ge(a_xnt, q * KD + KD)
                for j in (2 * part, 2 * part + 1):
                    if empties[part] is not None:
                        pe.wait_ge(empties[part], q * J + (j + 1 if part == 0 else j - 1) + (2 if part == 0 else 0))
                    for k in range(KD):
                        ins = pe.matmul(pp[(first + j) % 2][:, 0:C], w[:, k, j * P:(j + 1) * P], xnt[:, k, :],
                                        start=(k == 0), stop=(k == KD - 1))
                    ins.then_inc(proj, 1)

            def rows(n, q, b):
                if n == 0:
                    pe.wait_ge(d_bc, q * 4 + 4)
                pe.wait_ge(a_bs, q * NS + n)
                pe.matmul(pb[:, 0:C], sel[:, n, :], bc[b][:], start=True, stop=True).then_inc(t_b, 1)
                pe.wait_ge(a_cs, q * NS + n)
                pe.matmul(pc[:, 0:C], sel[:, NS + n, :], bc[b][:], start=True, stop=True).then_inc(t_c, 1)

            def step(n, q, b, more):
                ahead(rows, n, 3, q, b, more)
                if n == 0 and not first(q):
                    output(q - 1, 1 - b)
                pe.wait_ge(d_hc, q * NS + (n + 1))
                for j in range(J):
                    ins = pe.matmul(py[:, j, 0:C], idf[:, :], hs[n % 2][:, j, :, :].rearrange("p s t -> p (s t)"),
                                    start=(n == 0), stop=(n == NS - 1))
                ins.then_inc(t_y, 1)
                if n == NS - 1 and not more:
                    output(q, b)

            def output(q, b):
                pe.wait_ge(d_yg, q * 2 + 2)
                pe.wait_ge(a_dt, min(2 * J, (NQ - q) * J) + q * J if isinstance(q, int) else q * J + 2 * J)
                for r in (0, 1):
                    for a in (0, 1):
                        out = pp[r][0:T, a * D:(a + 1) * D]
                        for j in range(J):
                            pe.matmul(out, u[b][:, j, 2 * r + a, :], wo[:, j, :], start=(j == 0), stop=False)
                        ins = pe.matmul(out, ones[:, 0:T], brow[:, 1, :], start=False, stop=True)
                    ins.then_inc(proj, 1)

            def start():
                for n in range(3):
                    rows(n, 0, 0)

            run_quads(pe, pre, step, start, pair_index=True)
        used = m.semaphores
    return used


def first(q):
    return isinstance(q, int) and q == 0


def one(q):
    return isinstance(q, int) and q == 1


def ahead(work, n, by, q, b, more):
    if n + by < NS:
        work(n + by, q, b)
    elif more:
        work(n + by - NS, q + 1, 1 - b)


def run_quads(eng, pre, step, start, pair_index=False):
    def quad(q, b, next_pair):
        more = next_pair is not None
        for n in range(NS):
            step(n, q, b, more)
            if more:
                before(n, q + 1, 1 - b, next_pair)

    def before(slot, q, b, pair):
        pre(slot, q, b, *((pair,) if pair_index else ()))

    for slot in range(NS):
        before(slot, 0, 0, 0)
    start()
    quad(0, 0, 0)
    with eng.Fori(0, NQ // 2 - 1) as i:
        quad(2 * i + 1, 1, i + 1)
        quad(2 * i + 2, 0, i + 1)
    quad(NQ - 1, 1, None)


def make_identity(nc, idf):
    with ExitStack() as ctx:
        made = ctx.enter_context(nc.semaphore("identity_made"))
        block = ctx.enter_context(nc.Block())

        @block.gpsimd
        def _(pool):
            pool.memset(idf[:], 0.0).then_inc(made, 1)
            pool.wait_ge(made, 1)
            pool.affine_select(out=idf[:], in_=idf[:], compare_op=ALU.not_equal, fill=1.0, base=0,
                               pattern=[[-1, P]], channel_multiplier=1).then_inc(made, 1)
            pool.wait_ge(made, 2)
    return [made]



def in_steps(eng, stages, items, lead, unroll=4, base=0):
    tail = max(lag for lag, _ in stages)

    def step(i, t):
        for lag, work in stages:
            if not isinstance(i, int) or 0 <= i - lag < items:
                work(i + (base - lag), (t - lag) % unroll)

    for i in range(lead):
        step(i, i % unroll)
    with eng.Fori(0, (items - lead) // unroll) as m:
        for t in range(unroll):
            step(unroll * m + (lead + t), t)
    for i in range(items, items + tail):
        step(i, i % unroll)


def wait(eng, sem, value):
    if not isinstance(value, int) or value > 0:
        eng.wait_ge(sem, value)


class Norm:

    def __init__(self, m, xnt, pt, sums=None, kept=None):
        self.h = [m.sb(f"nh{b}", [P, QUAD, D]) for b in (0, 1)]
        self.xn = [m.sb(f"nxn{b}", [P, QUAD, D]) for b in (0, 1)]
        self.stats = m.sb("nstats", [P, QUAD, 6])
        self.mv = [m.sb(f"nmv{b}", [P, QUAD, 2]) for b in (0, 1)]
        self.veps = [m.sb(f"nveps{b}", [P, QUAD]) for b in (0, 1)]
        self.rstd = [m.sb(f"nrstd{b}", [P, QUAD]) for b in (0, 1)]
        self.spare = m.sb("nspare", [1, 1])
        self.half = m.sb("nhalf", [P, QUAD])
        self.ones = m.sb("nones", [P, 1])
        self.xnt, self.pt, self.sums = xnt, pt, sums
        if kept is not None:
            self.kept = kept
        self.loaded = [m.sem(f"nloaded{b}") for b in (0, 1)]
        self.made = m.sem("nmade")
        self.d_st = m.sem("nd_st")
        self.g_rstd = m.sem("ng_rstd")
        self.d_xn = m.sem("nd_xn")
        self.t_xt = m.sem("nt_xt")
        self.a_xt = m.sem("na_xt")
        self.t_lg = m.sem("nt_lg")
        self.d_lg = m.sem("nd_lg")

    def xt_out(self, q, t, k):
        return self.xnt[:, k, bass.ds(q * C, C)]

    def source(self, b):
        return self.sums[b][:]

    def sync(self, sp, h_in):
        def load(q, t):
            b = t % 2
            wait(sp, self.d_xn, q - 1)
            sp.dma_start(self.h[b][0:T, :, :], h_in[bass.ds(q * QUAD, QUAD), :, :].rearrange("s t d -> t s d"))\
                .then_inc(self.loaded[b], 16)
        in_steps(sp, [(0, load)], NQ, 4)

    def gpsimd(self, pool):
        pool.memset(self.half[:], -0.5).then_inc(self.made, 1)
        pool.memset(self.ones[:], 1.0).then_inc(self.made, 1)
        pool.wait_ge(self.made, 2)

        def power(q, t):
            b = t % 2
            pool.wait_ge(self.d_st, q * 3 + 3)
            pool.tensor_tensor(self.rstd[b][0:T, :], self.veps[b][0:T, :], self.half[0:T, :], ALU.pow)\
                .then_inc(self.g_rstd, 1)
        in_steps(pool, [(0, power)], NQ, 4)

    def vector(self, dve):
        def stats(q, t):
            b = t % 2
            if isinstance(q, int):
                dve.wait_ge(self.loaded[b], 16 * (q // 2 + 1))
            else:
                dve.wait_ge(self.loaded[b], (q - b) * 8 + 16)
            layer_norm_stats(dve, self.h[b], self.stats, self.mv[b], self.veps[b], self.d_st, q * 3, self.spare[:])

        def normal(q, t):
            b = t % 2
            dve.wait_ge(self.g_rstd, q + 1)
            wait(dve, self.t_xt, q - 1)
            if self.sums is not None:
                wait(dve, self.t_lg, q - 1)
            for s in range(QUAD):
                ins = dve.tensor_scalar(self.xn[b][0:T, s, :], self.h[b][0:T, s, :], self.mv[b][0:T, s, 0:1],
                                        self.rstd[b][0:T, s:s + 1], ALU.subtract, ALU.mult)
            ins.then_inc(self.d_xn, 1)
        def keep(q, t):
            b = t % 2
            dve.wait_ge(self.t_lg, q + 1)
            dve.tensor_scalar(self.kept(q), self.source(b), 1.0, None, ALU.mult).then_inc(self.d_lg, 1)

        stages = [(2, keep)] if self.sums is not None else []
        in_steps(dve, stages + [(1, normal), (0, stats)], NQ, 4)

    def tensor(self, pe, idf):
        pe.wait_ge(self.made, 2)

        def turn(q, t):
            b = t % 2
            pe.wait_ge(self.d_xn, q + 1)
            wait(pe, self.a_xt, (q - 1) * KD)
            for k in range(KD):
                for s in range(QUAD):
                    ins = pe.transpose(self.pt[b][:, k, s * T:(s + 1) * T], self.xn[b][0:T, s, k * P:(k + 1) * P],
                                       idf[0:T, 0:T])
            ins.then_inc(self.t_xt, 1)
            if self.sums is not None:
                wait(pe, self.d_lg, q - 1)
                for k in range(KD):
                    for s in range(QUAD):
                        ins = pe.matmul(self.sums[b][:, k, s:s + 1], self.xn[b][0:T, s, k * P:(k + 1) * P],
                                        self.ones[0:T, :], start=True, stop=True)
                ins.then_inc(self.t_lg, 1)
        in_steps(pe, [(0, turn)], NQ, 4)

    def scalar(self, act, xs=None):
        def empty(q, t):
            b = t % 2
            act.wait_ge(self.t_xt, q + 1)
            for k in range(KD):
                act.activation(self.xt_out(q, t, k), self.pt[b][:, k, 0:C], ACT.Copy)\
                    .then_inc(self.a_xt, 1)
        in_steps(act, [(0, empty)], NQ, 4)


HEADS = 16
ACTIVE = 4
DH = 64
HEAD_W = 3 * DH
KB = KD + 1


def routed_phase(nc, io, idf, h_in, h_out):
    with ExitStack() as ctx:
        m = Memory(nc, ctx, "r_")
        xnt = m.sb("xnt", [P, KD, SAMPLES * T])
        wqkv = m.sb("wqkv", [P, KB, HEADS, HEAD_W])
        wr = m.sb("wr", [P, KD, HEADS])
        wo = m.sb("wo", [P, KD, D])
        br = m.sb("br", [SAMPLES, HEADS])
        brow = m.sb("brow", [1, D])
        xs = m.sb("xs", [P, KD, SAMPLES])
        ones = m.sb("ones", [P, P])
        picks = m.sb("picks", [P, SAMPLES, 2 * ACTIVE])
        heads = m.sb("heads", [P, SAMPLES, ACTIVE], I32)
        weights = m.sem("weights")
        consts = m.sem("consts")
        with ExitStack() as inner:
            n = Memory(nc, inner, "rn_")
            pt = [n.ps(f"pt{b}", [P, KD, 512]) for b in (0, 1)]
            sums = [n.ps(f"sums{b}", [P, KD, QUAD]) for b in (0, 1)]
            norm = Norm(n, xnt, pt, sums, lambda q: xs[:, :, bass.ds(q * QUAD, QUAD)])
            block = inner.enter_context(nc.Block())

            @block.sync
            def _(sp):
                sp.dma_start(wqkv[:, 0:KD, :, :], io["rwqkv"].rearrange("(k p) h d -> p k (h d)", p=P))\
                    .then_inc(weights, 16)
                sp.dma_start(wr[:], io["rwr"].rearrange("(k p) h -> p k h", p=P)).then_inc(weights, 16)
                sp.dma_start(wo[:], io["rwo"].rearrange("(k p) n -> p k n", p=P)).then_inc(weights, 16)
                sp.dma_start(br[:], io["rbr"]).then_inc(weights, 16)
                sp.dma_start(brow[:], io["brow"][:, 2, :]).then_inc(weights, 16)
                sp.wait_ge(consts, 2)
                sp.dma_start(wqkv[0:1, KD, :, :], io["rbias"]).then_inc(weights, 16)
                norm.sync(sp, h_in)

            @block.gpsimd
            def _(pool):
                pool.memset(wqkv[:, KD, :, :], 0.0).then_inc(consts, 1)
                pool.memset(ones[:], 1.0).then_inc(consts, 1)
                norm.gpsimd(pool)

            @block.scalar
            def _(act):
                norm.scalar(act)

            @block.tensor
            def _(pe):
                norm.tensor(pe, idf)

            @block.vector
            def _(dve):
                norm.vector(dve)

        with ExitStack() as inner:
            n = Memory(nc, inner, "rr_")
            route(nc, n, inner, idf, xs, wr, br, ones, picks, heads, weights)
        with ExitStack() as inner:
            n = Memory(nc, inner, "ra_")
            routed_attention(nc, n, inner, idf, xnt, wqkv, wo, brow, ones, picks, heads, h_in, h_out)


def route(nc, m, ctx, idf, xs, wr, br, ones, picks, heads, weights):
    S = SAMPLES
    lg = m.sb("lg", [S, HEADS])
    top = m.sb("top", [S, 8])
    neg = m.sb("neg", [S, 2])
    ex = m.sb("ex", [S, HEADS])
    tot = m.sb("tot", [S, 4])
    dist = m.sb("dist", [S, HEADS])
    best = m.sb("best", [S, 8])
    index = m.sb("index", [S, 8], U32)
    ev = m.sb("ev", [S, ACTIVE + 1])
    pick = m.sb("pick", [S, 2 * ACTIVE])
    spread = m.sb("spread", [S, S, 2 * ACTIVE])
    pl = m.ps("pl", [P, 512])
    pp = m.ps("pp", [P, 512])
    t_l = m.sem("t_l")
    t_p = m.sem("t_p")
    d = m.sem("d")
    a = m.sem("a")
    block = ctx.enter_context(nc.Block())

    @block.tensor
    def _(pe):
        pe.wait_ge(weights, 6 * 16)
        for k in range(KD):
            ins = pe.matmul(pl[0:S, 0:HEADS], xs[:, k, :], wr[:, k, :], start=(k == 0), stop=(k == KD - 1))
        ins.then_inc(t_l, 1)
        pe.wait_ge(d, 13)
        pe.matmul(pp[:, :], ones[0:S, :], spread[:].rearrange("p s k -> p (s k)"), start=True, stop=True)\
            .then_inc(t_p, 1)

    @block.scalar
    def _(act):
        act.wait_ge(d, 3)
        act.activation(ex[:], lg[:], ACT.Exp, bias=neg[:, 0:1], accum_out=tot[:, 0:1]).then_inc(a, 1)
        act.wait_ge(d, 8)
        act.activation(ev[:, 0:ACTIVE], best[:, 0:ACTIVE], ACT.Exp, bias=neg[:, 1:2],
                       accum_out=tot[:, 2:3]).then_inc(a, 1)
        act.activation(ev[:, ACTIVE:], neg[:, 1:2], ACT.Exp).then_inc(a, 1)

    @block.vector
    def _(dve):
        count = [0]

        def then(ins):
            count[0] += 1
            ins.then_inc(d, 1)
            dve.wait_ge(d, count[0])

        dve.wait_ge(t_l, 1)
        dve.wait_ge(weights, 6 * 16)
        then(dve.scalar_tensor_tensor(out=lg[:], in0=pl[0:S, 0:HEADS], scalar=1.0 / T, in1=br[:],
                                      op0=ALU.mult, op1=ALU.add))
        then(dve.max(top[:], lg[:]))
        then(dve.tensor_scalar(neg[:, 0:1], top[:, 0:1], -1.0, None, ALU.mult))
        dve.wait_ge(a, 1)
        then(dve.reciprocal(tot[:, 1:2], tot[:, 0:1]))
        then(dve.tensor_scalar(dist[:], ex[:], tot[:, 1:2], None, ALU.mult))
        then(dve.max(best[:], dist[:]))
        then(dve.max_index(index[:], best[:], dist[:]))
        then(dve.tensor_scalar(neg[:, 1:2], best[:, 0:1], -1.0, None, ALU.mult))
        dve.wait_ge(a, 3)
        then(dve.scalar_tensor_tensor(out=tot[:, 3:4], in0=ev[:, ACTIVE:], scalar=float(HEADS - ACTIVE),
                                      in1=tot[:, 2:3], op0=ALU.mult, op1=ALU.add))
        then(dve.reciprocal(tot[:, 0:1], tot[:, 3:4]))
        then(dve.tensor_scalar(pick[:, 0:ACTIVE], ev[:, 0:ACTIVE], tot[:, 0:1], None, ALU.mult))
        then(dve.tensor_copy(pick[:, ACTIVE:], index[:, 0:ACTIVE]))
        then(dve.tensor_tensor(spread[:], idf[0:S, 0:S].unsqueeze(2).to_broadcast([S, S, 2 * ACTIVE]),
                               pick[:].unsqueeze(1).to_broadcast([S, S, 2 * ACTIVE]), ALU.mult))
        dve.wait_ge(t_p, 1)
        then(dve.tensor_copy(picks[:].rearrange("p s k -> p (s k)"), pp[:, :]))
        then(dve.tensor_copy(heads[:], picks[:, :, ACTIVE:]))


def routed_attention(nc, m, ctx, idf, xnt, wqkv, wo, brow, ones, picks, heads, h_in, h_out):
    A = ACTIVE
    wsel = [m.sb(f"wsel{b}", [P, KB, 3, A, DH]) for b in (0, 1)]
    xcur = [m.sb(f"xcur{b}", [P, KD, T]) for b in (0, 1)]
    qk = [m.sb(f"qk{b}", [P, 4, T]) for b in (0, 1)]
    v = [m.sb(f"v{b}", [P, A, DH + 1]) for b in range(4)]
    sh = [m.sb(f"sh{b}", [P, A, T]) for b in (0, 1)]
    pr = [m.sb(f"pr{b}", [P, A, T]) for b in (0, 1)]
    prt = [m.sb(f"prt{b}", [P, A, T]) for b in (0, 1)]
    o = [m.sb(f"o{b}", [P, A, DH]) for b in (0, 1)]
    ot = [m.sb(f"ot{b}", [P, KD, T]) for b in (0, 1)]
    top = m.sb("top", [P, A])
    rec = m.sb("rec", [P, A])
    h = [m.sb(f"h{b}", [P, D]) for b in range(4)]
    pqk = m.ps("pqk", [P, 512])
    pv = m.ps("pv", [P, 512])
    psc = m.ps("psc", [P, 2, 512])
    ptr = m.ps("ptr", [P, 512])
    po = m.ps("po", [P, 512])
    pot = m.ps("pot", [P, 512])
    pout = m.ps("pout", [P, 512])

    g_one = m.sem("g_one")
    g_x = m.sem("g_x")
    d_sel = m.sem("d_sel")
    t_qkv = m.sem("t_qkv")
    a_qk = m.sem("a_qk")
    a_v = m.sem("a_v")
    t_sc = m.sem("t_sc")
    d_mx = m.sem("d_mx")
    d_sh = m.sem("d_sh")
    a_ex = m.sem("a_ex")
    t_tr = m.sem("t_tr")
    a_tr = m.sem("a_tr")
    t_o = m.sem("t_o")
    d_rec = m.sem("d_rec")
    d_o = m.sem("d_o")
    t_ot = m.sem("t_ot")
    a_ot = m.sem("a_ot")
    t_out = m.sem("t_out")
    d_h = m.sem("d_h")
    loaded = [m.sem(f"loaded{b}") for b in range(4)]
    stored = [m.sem(f"stored{b}") for b in range(4)]
    N = SAMPLES
    SEL, QKV, SC, TR, O, OT, OUT = range(7)
    LEAD = 8
    block = ctx.enter_context(nc.Block())

    @block.sync
    def _(sp):
        def load(s, t):
            if not isinstance(s, int):
                sp.wait_ge(stored[t], (s - t) * 4)
            elif s >= 4:
                sp.wait_ge(stored[t], 16 * (s // 4))
            sp.dma_start(h[t][0:T, :], h_in[bass.ds(s, 1), :, :].rearrange("s t d -> (s t) d")).then_inc(loaded[t], 16)

        def store(s, t):
            sp.wait_ge(d_h, s + 1)
            sp.dma_start(h_out[bass.ds(s, 1), :, :].rearrange("s t d -> (s t) d"), h[t][0:T, :]).then_inc(stored[t], 16)

        in_steps(sp, [(O, load), (OUT + 1, store)], N, LEAD)
        for t in range(4):
            sp.wait_ge(stored[t], 16 * (N // 4))

    @block.gpsimd
    def _(pool):
        for b in range(4):
            pool.memset(v[b][:, :, DH:], 1.0).then_inc(g_one, 1)

        def current(s, t):
            wait(pool, t_qkv, (s - 1) * 2)
            pool.tensor_copy(xcur[t % 2][:], xnt[:, :, bass.ds(s * T, T)]).then_inc(g_x, 1)

        in_steps(pool, [(SEL, current)], N, LEAD)

    @block.scalar
    def _(act):
        act.wait_ge(g_one, 4)

        def project(s, t):
            act.wait_ge(t_qkv, s * 2 + 1)
            wait(act, t_sc, s - 1)
            act.activation(qk[t % 2][:].rearrange("p x t -> p (x t)"), pqk[:, 0:C], ACT.Copy).then_inc(a_qk, 1)
            act.wait_ge(t_qkv, s * 2 + 2)
            wait(act, t_o, s - 3)
            act.activation(v[t][0:T, :, 0:DH], pv[0:T, 0:D].rearrange("p (a d) -> p a d", a=A), ACT.Copy)\
                .then_inc(a_v, 1)

        def weights(s, t):
            act.wait_ge(d_sh, s + 1)
            wait(act, t_tr, s - 1)
            act.activation(pr[t % 2][0:T, :, :], sh[t % 2][0:T, :, :], ACT.Exp, scale=DH ** -0.5).then_inc(a_ex, 1)

        def turned(s, t):
            act.wait_ge(t_tr, s + 1)
            wait(act, t_o, s - 1)
            act.activation(prt[t % 2][0:T, :, :].rearrange("p a t -> p (a t)"), ptr[0:T, 0:C], ACT.Copy)\
                .then_inc(a_tr, 1)

        def out_turned(s, t):
            act.wait_ge(t_ot, s + 1)
            wait(act, t_out, s - 1)
            act.activation(ot[t % 2][:].rearrange("p k t -> p (k t)"), pot[:, 0:KD * T], ACT.Copy).then_inc(a_ot, 1)

        in_steps(act, [(OT, out_turned), (TR, turned), (SC, weights), (QKV, project)], N, LEAD)

    @block.vector
    def _(dve):
        def select(s, t):
            wait(dve, t_qkv, (s - 1) * 2)
            for a in range(A):
                head = dve.value_load(heads[0:1, bass.ds(s, 1), a:a + 1].rearrange("p s a -> p (s a)"), min_val=0, max_val=HEADS - 1)
                ins = dve.tensor_scalar(wsel[t % 2][:, :, :, a, :],
                                        wqkv[:, :, bass.ds(head, 1), :].rearrange("p k h (x d) -> p k (h x) d", x=3),
                                        picks[:, bass.ds(s, 1), a:a + 1].rearrange("p s a -> p (s a)"), None, ALU.mult)
            ins.then_inc(d_sel, 1)

        def shift(s, t):
            dve.wait_ge(t_sc, s + 1)
            sc = psc[0:T, :, 0:2 * T].rearrange("p x (y t) -> p x y t", y=2)
            best = top[0:T, :].rearrange("p (x y) -> p x y", x=2)
            dve.tensor_reduce(best, sc, AX_X, ALU.max).then_inc(d_mx, 1)
            dve.wait_ge(d_mx, s + 1)
            wait(dve, a_ex, s - 1)
            dve.tensor_tensor(sh[t % 2][0:T, :, :].rearrange("p (x y) t -> p x y t", x=2), sc,
                              best.unsqueeze(3).to_broadcast([T, 2, 2, T]),
                              ALU.subtract).then_inc(d_sh, 1)

        def normal(s, t):
            dve.wait_ge(t_o, s + 1)
            po3 = po[0:T, 0:A * (DH + 1)].rearrange("p (a d) -> p a d", a=A)
            dve.reciprocal(rec[0:T, :], po3[:, :, DH]).then_inc(d_rec, 1)
            dve.wait_ge(d_rec, s + 1)
            wait(dve, t_ot, s - 1)
            dve.tensor_tensor(o[t % 2][0:T, :, :], po3[:, :, 0:DH],
                              rec[0:T, :].unsqueeze(2).to_broadcast([T, A, DH]), ALU.mult).then_inc(d_o, 1)

        def residual(s, t):
            if isinstance(s, int):
                dve.wait_ge(loaded[t], 16 * (s // 4 + 1))
            else:
                dve.wait_ge(loaded[t], (s - t) * 4 + 16)
            dve.wait_ge(t_out, s + 1)
            dve.tensor_tensor(h[t][0:T, :], h[t][0:T, :], pout[0:T, 0:D], ALU.add).then_inc(d_h, 1)

        in_steps(dve, [(OUT, residual), (O, normal), (SC, shift), (SEL, select)], N, LEAD)

    @block.tensor
    def _(pe):
        pe.wait_ge(g_one, 4)

        def project(s, t):
            w = wsel[t % 2]
            x = xcur[t % 2]
            pe.wait_ge(g_x, s + 1)
            pe.wait_ge(d_sel, s + 1)
            wait(pe, a_qk, s)
            for c in range(4):
                out = pqk[:, c * T:(c + 1) * T]
                part = w[:, :, c // 2, 2 * (c % 2):2 * (c % 2) + 2, :].rearrange("p k a d -> p k (a d)")
                pe.matmul(out, part[0:1, KD, :], ones[0:1, 0:T], start=True, stop=False)
                for k in range(KD):
                    ins = pe.matmul(out, part[:, k, :], x[:, k, :], start=False, stop=(k == KD - 1))
            ins.then_inc(t_qkv, 1)
            wait(pe, a_v, s)
            part = w[:, :, 2, :, :].rearrange("p k a d -> p k (a d)")
            pe.matmul(pv[0:T, 0:D], ones[0:1, 0:T], part[0:1, KD, :], start=True, stop=False)
            for k in range(KD):
                ins = pe.matmul(pv[0:T, 0:D], x[:, k, :], part[:, k, :], start=False, stop=(k == KD - 1))
            ins.then_inc(t_qkv, 1)

        def scores(s, t):
            pe.wait_ge(a_qk, s + 1)
            wait(pe, d_sh, s)
            for a in range(A):
                rows = slice(DH * (a % 2), DH * (a % 2) + DH)
                ins = pe.matmul(psc[0:T, a % 2, (a // 2) * T:(a // 2 + 1) * T], qk[t % 2][rows, a // 2, :], qk[t % 2][rows, 2 + a // 2, :],
                                start=True, stop=True)
            ins.then_inc(t_sc, 1)

        def turn_weights(s, t):
            pe.wait_ge(a_ex, s + 1)
            wait(pe, a_tr, s)
            for a in range(A):
                ins = pe.transpose(ptr[0:T, a * T:(a + 1) * T], pr[t % 2][0:T, 2 * (a % 2) + a // 2, :], idf[0:T, 0:T])
            ins.then_inc(t_tr, 1)

        def weighted(s, t):
            pe.wait_ge(a_tr, s + 1)
            pe.wait_ge(a_v, s + 1)
            wait(pe, d_o, s)
            for a in range(A):
                ins = pe.matmul(po[0:T, a * (DH + 1):(a + 1) * (DH + 1)], prt[t % 2][0:T, a, :], v[t][0:T, a, :],
                                start=True, stop=True)
            ins.then_inc(t_o, 1)

        def turn_out(s, t):
            pe.wait_ge(d_o, s + 1)
            wait(pe, a_ot, s)
            for k in range(KD):
                ins = pe.transpose(pot[:, k * T:(k + 1) * T],
                                   o[t % 2][0:T, 2 * k:2 * k + 2, :].rearrange("p a d -> p (a d)"), idf[0:T, 0:T])
            ins.then_inc(t_ot, 1)

        def output(s, t):
            pe.wait_ge(a_ot, s + 1)
            wait(pe, d_h, s)
            for k in range(KD):
                pe.matmul(pout[0:T, 0:D], ot[t % 2][:, k, :], wo[:, k, :], start=(k == 0), stop=False)
            pe.matmul(pout[0:T, 0:D], ones[0:1, 0:T], brow[:], start=False, stop=True).then_inc(t_out, 1)

        in_steps(pe, [(OUT, output), (OT, turn_out), (O, weighted), (TR, turn_weights), (SC, scores), (QKV, project)],
                 N, LEAD)


KV = 4
REP = HEADS // KV
FR = DH // 2


def grouped_phase(nc, io, idf, h_in, h_out):
    with ExitStack() as ctx:
        m = Memory(nc, ctx, "g_")
        xnt = m.sb("xnt", [P, KD, SAMPLES * T])
        with ExitStack() as inner:
            n = Memory(nc, inner, "gn_")
            pt = [n.ps(f"pt{b}", [P, KD, 512]) for b in (0, 1)]
            norm = Norm(n, xnt, pt)
            block = inner.enter_context(nc.Block())

            @block.sync
            def _(sp):
                norm.sync(sp, h_in)

            @block.gpsimd
            def _(pool):
                norm.gpsimd(pool)

            @block.scalar
            def _(act):
                norm.scalar(act)

            @block.tensor
            def _(pe):
                norm.tensor(pe, idf)

            @block.vector
            def _(dve):
                norm.vector(dve)

        with ExitStack() as inner:
            grouped_attention(nc, Memory(nc, inner, "ga_"), inner, io, idf, xnt, h_in, h_out)


def grouped_attention(nc, m, ctx, io, idf, xnt, h_in, h_out):
    wq = m.sb("wq", [P, KD, REP, 2, P])
    wk = m.sb("wk", [P, KD, 2, P])
    wv = m.sb("wv", [P, KD, KV * DH])
    wo = m.sb("wo", [P, HEADS // 2, D])
    cos = m.sb("cos", [P, T])
    sin = m.sb("sin", [P, T])
    idb = m.sb("idb", [P, P], BF16)
    mask = m.sb("mask", [P, KV, T], BF16)
    turned_q = [m.sb(f"turned_q{b}", [P, REP, 2, QUAD, T]) for b in (0, 1)]
    keys = [m.sb(f"keys{b}", [P, 2, QUAD, KV, T]) for b in (0, 1)]
    qm = [m.sb(f"qm{b}", [P, 4, QUAD, T]) for b in (0, 1)]
    km = m.sb("km", [P, 4, QUAD, T])
    turned_k = m.sb("turned_k", [P, 2, QUAD, T])
    xcur = [m.sb(f"xcur{b}", [P, KD, T]) for b in (0, 1)]
    v = [m.sb(f"v{b}", [P, KV, DH + 1]) for b in (0, 1)]
    sh = [m.sb(f"sh{b}", [P, KV, T]) for b in (0, 1)]
    pr = [m.sb(f"pr{b}", [P, KV, T]) for b in (0, 1)]
    prt = [m.sb(f"prt{b}", [P, KV, T]) for b in (0, 1)]
    o = [m.sb(f"o{b}", [P, HEADS, DH]) for b in (0, 1)]
    ot = [m.sb(f"ot{b}", [P, HEADS // 2, T]) for b in (0, 1)]
    top = m.sb("top", [P, KV])
    rec = m.sb("rec", [P, KV])
    h = [m.sb(f"h{b}", [P, D]) for b in range(4)]
    pq = [m.ps(f"pq{b}", [P, 512]) for b in (0, 1)]
    pv = m.ps("pv", [P, 512])
    psc = m.ps("psc", [P, 512])
    ptr = m.ps("ptr", [P, 512])
    po = m.ps("po", [P, 512])
    pot = m.ps("pot", [P, 512])
    pout = m.ps("pout", [P, 512])

    weights = m.sem("weights")
    g_made = m.sem("g_made")
    t_k = m.sem("t_k")
    d_km = m.sem("d_km")
    g_k = m.sem("g_k")
    a_k = m.sem("a_k")
    t_q = m.sem("t_q")
    d_qm = m.sem("d_qm")
    g_q = m.sem("g_q")
    g_x = m.sem("g_x")
    t_v = m.sem("t_v")
    a_v = m.sem("a_v")
    t_sc = m.sem("t_sc")
    d_mx = m.sem("d_mx")
    d_sh = m.sem("d_sh")
    a_ex = m.sem("a_ex")
    t_tr = m.sem("t_tr")
    a_tr = m.sem("a_tr")
    t_o = m.sem("t_o")
    d_rec = m.sem("d_rec")
    d_o = m.sem("d_o")
    t_ot = m.sem("t_ot")
    a_ot = m.sem("a_ot")
    t_out = m.sem("t_out")
    d_h = m.sem("d_h")
    loaded = [m.sem(f"loaded{b}") for b in range(4)]
    stored = [m.sem(f"stored{b}") for b in range(4)]
    N, LEAD, UNROLL = SAMPLES, 16, 8
    CORE, LATE, OUT = 5, 6, 7
    block = ctx.enter_context(nc.Block())

    def per_quad(p, t):
        return (p - t % QUAD) // QUAD

    @block.sync
    def _(sp):
        for tile, name in ((wq, "gwq"), (wk, "gwk"), (wv, "gwv"), (wo, "gwo")):
            flat = tile[:].rearrange({4: "p k n c -> p k (n c)", 5: "p k r a c -> p k (r a c)"}.get(len(tile.shape), "p k n -> p k n")) \
                if len(tile.shape) > 3 else tile[:]
            sp.dma_start(flat, io[name].rearrange("(k p) n -> p k n", p=P)).then_inc(weights, 16)
        sp.dma_start(cos[:], io["cos"]).then_inc(weights, 16)
        sp.dma_start(sin[:], io["sin"]).then_inc(weights, 16)

        def load(s, t):
            if not isinstance(s, int):
                sp.wait_ge(stored[t % 4], (s - t % 4) * 4)
            elif s >= 4:
                sp.wait_ge(stored[t % 4], 16 * (s // 4))
            sp.dma_start(h[t % 4][0:T, :], h_in[bass.ds(s, 1), :, :].rearrange("s t d -> (s t) d"))\
                .then_inc(loaded[t % 4], 16)

        def store(s, t):
            sp.wait_ge(d_h, s + 1)
            sp.dma_start(h_out[bass.ds(s, 1), :, :].rearrange("s t d -> (s t) d"), h[t % 4][0:T, :])\
                .then_inc(stored[t % 4], 16)

        in_steps(sp, [(CORE, load), (OUT + 1, store)], N, LEAD, UNROLL)
        for t in range(4):
            sp.wait_ge(stored[t], 16 * (N // 4))

    @block.gpsimd
    def _(pool):
        for b in (0, 1):
            pool.memset(v[b][:, :, DH:], 1.0).then_inc(g_made, 1)
            pool.memset(keys[b][:].rearrange("p a s g t -> p (a s g t)"), 0.0).then_inc(g_made, 1)
        pool.memset(idb[:], 0.0).then_inc(g_made, 1)
        pool.memset(mask[:], 0.0).then_inc(g_made, 1)
        pool.wait_ge(g_made, 6)
        pool.affine_select(out=idb[:], in_=idb[:], compare_op=ALU.not_equal, fill=1.0, base=0,
                           pattern=[[-1, P]], channel_multiplier=1).then_inc(g_made, 1)
        pool.affine_select(out=mask[:], in_=mask[:], compare_op=ALU.is_ge, fill=-1e30, base=0,
                           pattern=[[0, KV], [-1, T]], channel_multiplier=1).then_inc(g_made, 1)

        def rotate_keys(p, t):
            if t % QUAD:
                return
            wait(pool, d_km, per_quad(p, t) + 1)
            wait(pool, a_k, per_quad(p, t))
            pool.tensor_tensor(turned_k[:, 0, :, :], km[:, 0, :, :], km[:, 1, :, :], ALU.subtract)
            pool.tensor_tensor(turned_k[:, 1, :, :], km[:, 2, :, :], km[:, 3, :, :], ALU.add).then_inc(g_k, 1)

        def rotate_queries(p, t):
            b, r = t // QUAD, t % QUAD
            pool.wait_ge(d_qm, p + 1)
            wait(pool, t_sc, (p - r - 8) * 4 + 16)
            q = qm[t % 2]
            pool.tensor_tensor(turned_q[b][:, r, 0, :, :], q[:, 0, :, :], q[:, 1, :, :], ALU.subtract)
            pool.tensor_tensor(turned_q[b][:, r, 1, :, :], q[:, 2, :, :], q[:, 3, :, :], ALU.add).then_inc(g_q, 1)

        def current(s, t):
            wait(pool, t_v, s - 1)
            pool.tensor_copy(xcur[t % 2][:], xnt[:, :, bass.ds(s * T, T)]).then_inc(g_x, 1)

        in_steps(pool, [(1, rotate_keys), (1, rotate_queries), (CORE - 1, current)], N, LEAD, UNROLL)

    @block.scalar
    def _(act):
        act.wait_ge(g_made, 8)

        def values(s, t):
            act.wait_ge(t_v, s + 1)
            wait(act, t_o, (s - 1) * 4)
            act.activation(v[t % 2][0:T, :, 0:DH], pv[0:T, 0:KV * DH].rearrange("p (a d) -> p a d", a=KV), ACT.Copy)\
                .then_inc(a_v, 1)

        def place_keys(p, t):
            if t % QUAD:
                return
            act.wait_ge(g_k, per_quad(p, t) + 1)
            wait(act, t_sc, (p - 8) * 4 + 16)
            for g in range(KV):
                rows = slice(32 * g, 32 * g + 32)
                for a in (0, 1):
                    ins = act.activation(keys[t // QUAD][rows, a, :, g, :], turned_k[rows, a, :, :], ACT.Copy)
            ins.then_inc(a_k, 1)

        def weigh(r):
            def work(s, t):
                act.wait_ge(d_sh, s * 4 + (r + 1))
                wait(act, t_tr, s * 4 + (r - 1))
                act.activation(pr[r % 2][0:T, :, :], sh[r % 2][0:T, :, :], ACT.Exp, scale=DH ** -0.5).then_inc(a_ex, 1)
            return work

        def turned(r):
            def work(s, t):
                act.wait_ge(t_tr, s * 4 + (r + 1))
                wait(act, t_o, s * 4 + (r - 1))
                act.activation(prt[r % 2][0:T, :, :].rearrange("p a t -> p (a t)"), ptr[0:T, 0:C], ACT.Copy)\
                    .then_inc(a_tr, 1)
            return work

        def out_turned(x):
            def work(s, t):
                act.wait_ge(t_ot, s * 2 + (x + 1))
                wait(act, t_out, s - 1)
                act.activation(ot[t % 2][:, 4 * x:4 * x + 4, :].rearrange("p k t -> p (k t)"), pot[:, 0:C], ACT.Copy)\
                    .then_inc(a_ot, 1)
            return work

        in_steps(act, [(CORE, values), (CORE, weigh(0)), (LATE, turned(3)), (2, place_keys), (CORE, weigh(1)), (CORE, turned(0)),
                       (CORE, weigh(2)), (CORE, turned(1)), (LATE, out_turned(0)),
                       (CORE, weigh(3)), (CORE, turned(2)), (LATE, out_turned(1))], N, LEAD, UNROLL)

    @block.vector
    def _(dve):
        dve.wait_ge(weights, 96)

        def rotation(out, sem):
            a, b = (pq[x][:, 0:C].rearrange("p (s t) -> p s t", s=QUAD) for x in (0, 1))
            c, s = (x[:].unsqueeze(1).to_broadcast([P, QUAD, T]) for x in (cos, sin))
            dve.tensor_tensor(out[:, 0, :, :], a, c, ALU.mult)
            dve.tensor_tensor(out[:, 1, :, :], b, s, ALU.mult)
            dve.tensor_tensor(out[:, 2, :, :], a, s, ALU.mult)
            dve.tensor_tensor(out[:, 3, :, :], b, c, ALU.mult).then_inc(sem, 1)

        def rope_keys(p, t):
            if t % QUAD:
                return
            wait(dve, t_k, per_quad(p, t) + 1)
            wait(dve, g_k, per_quad(p, t))
            rotation(km, d_km)

        def rope_queries(p, t):
            dve.wait_ge(t_q, p + 1)
            wait(dve, g_q, p - 1)
            rotation(qm[t % 2], d_qm)

        def shift(r):
            def work(s, t):
                dve.wait_ge(t_sc, s * 4 + (r + 1))
                sc = psc[0:T, 0:C].rearrange("p (a t) -> p a t", a=KV)
                dve.tensor_reduce(top[0:T, :], sc, AX_X, ALU.max).then_inc(d_mx, 1)
                dve.wait_ge(d_mx, s * 4 + (r + 1))
                wait(dve, a_ex, s * 4 + (r - 1))
                dve.tensor_tensor(sh[r % 2][0:T, :, :], sc, top[0:T, :].unsqueeze(2).to_broadcast([T, KV, T]),
                                  ALU.subtract).then_inc(d_sh, 1)
            return work

        def normal(r):
            def work(s, t):
                dve.wait_ge(t_o, s * 4 + (r + 1))
                po3 = po[0:T, 0:KV * (DH + 1)].rearrange("p (a d) -> p a d", a=KV)
                dve.reciprocal(rec[0:T, :], po3[:, :, DH]).then_inc(d_rec, 1)
                dve.wait_ge(d_rec, s * 4 + (r + 1))
                wait(dve, t_ot, (s - 1) * 2)
                dve.tensor_tensor(o[t % 2][0:T, r::REP, :], po3[:, :, 0:DH],
                                  rec[0:T, :].unsqueeze(2).to_broadcast([T, KV, DH]), ALU.mult).then_inc(d_o, 1)
            return work

        def residual(s, t):
            if isinstance(s, int):
                dve.wait_ge(loaded[t % 4], 16 * (s // 4 + 1))
            else:
                dve.wait_ge(loaded[t % 4], (s - t % 4) * 4 + 16)
            dve.wait_ge(t_out, s + 1)
            tile = h[t % 4][0:T, :]
            dve.tensor_tensor(tile, tile, pout[0:T, 0:D], ALU.add).then_inc(d_h, 1)

        in_steps(dve, [(0, rope_keys), (CORE, shift(0)), (LATE, normal(2)), (OUT, residual), (CORE, shift(1)),
                       (LATE, normal(3)), (0, rope_queries),
                       (CORE, shift(2)), (CORE, normal(0)), (CORE, shift(3)), (CORE, normal(1))], N, LEAD, UNROLL)

    @block.tensor
    def _(pe):
        pe.wait_ge(weights, 96)
        pe.wait_ge(g_made, 8)

        def project(w, cols):
            for a in (0, 1):
                for k in range(KD):
                    ins = pe.matmul(pq[a][:, 0:C], w[:, k, a, :], xnt[:, k, cols], start=(k == 0), stop=(k == KD - 1))
            return ins

        def project_keys(p, t):
            if t % QUAD:
                return
            wait(pe, d_qm, p)
            project(wk, bass.ds(p * T, C)).then_inc(t_k, 1)

        def project_queries(p, t):
            r = t % QUAD
            if r == 0:
                wait(pe, d_km, per_quad(p, t) + 1)
            wait(pe, d_qm, p)
            project(wq[:, :, r, :, :], bass.ds((p - r) * T, C)).then_inc(t_q, 1)

        def project_values(s, t):
            pe.wait_ge(g_x, s + 1)
            wait(pe, a_v, s)
            for k in range(KD):
                ins = pe.matmul(pv[0:T, 0:KV * DH], xcur[t % 2][:, k, :], wv[:, k, :], start=(k == 0), stop=(k == KD - 1))
            ins.then_inc(t_v, 1)

        def scores(r):
            def work(s, t):
                b, x = t // QUAD, t % QUAD
                if r == 0:
                    if x == 0:
                        wait(pe, a_k, per_quad(s, t) + 1)
                    wait(pe, g_q, (s - x) + 4)
                wait(pe, d_sh, s * 4 + r)
                out = psc[0:T, 0:C]
                for a in (0, 1):
                    pe.matmul(out, turned_q[b][:, r, a, x, :], keys[b][:, a, x, :, :].rearrange("p g t -> p (g t)"),
                              start=(a == 0), stop=False)
                pe.matmul(out, idb[0:T, 0:T], mask[0:T, :, :].rearrange("p g t -> p (g t)"), start=False, stop=True)\
                    .then_inc(t_sc, 1)
            return work

        def turn_weights(r):
            def work(s, t):
                pe.wait_ge(a_ex, s * 4 + (r + 1))
                wait(pe, a_tr, s * 4 + r)
                for g in range(KV):
                    ins = pe.transpose(ptr[0:T, g * T:(g + 1) * T], pr[r % 2][0:T, g, :], idf[0:T, 0:T])
                ins.then_inc(t_tr, 1)
            return work

        def weighted(r):
            def work(s, t):
                pe.wait_ge(a_tr, s * 4 + (r + 1))
                pe.wait_ge(a_v, s + 1)
                wait(pe, d_o, s * 4 + r)
                for g in range(KV):
                    ins = pe.matmul(po[0:T, g * (DH + 1):(g + 1) * (DH + 1)], prt[r % 2][0:T, g, :], v[t % 2][0:T, g, :],
                                    start=True, stop=True)
                ins.then_inc(t_o, 1)
            return work

        def turn_out(x):
            def work(s, t):
                pe.wait_ge(d_o, s * 4 + 4)
                wait(pe, a_ot, s * 2 + x)
                for k in range(4):
                    c = 4 * x + k
                    ins = pe.transpose(pot[:, k * T:(k + 1) * T], o[t % 2][0:T, 2 * c:2 * c + 2, :].rearrange("p a d -> p (a d)"),
                                       idf[0:T, 0:T])
                ins.then_inc(t_ot, 1)
            return work

        def output(s, t):
            pe.wait_ge(a_ot, s * 2 + 2)
            wait(pe, d_h, s)
            for k in range(HEADS // 2):
                ins = pe.matmul(pout[0:T, 0:D], ot[t % 2][:, k, :], wo[:, k, :], start=(k == 0), stop=(k == HEADS // 2 - 1))
            ins.then_inc(t_out, 1)

        in_steps(pe, [(OUT, output), (CORE, project_values), (0, project_keys),
                      (CORE, scores(0)), (LATE, turn_weights(3)), (LATE, weighted(2)),
                      (CORE, scores(1)), (CORE, turn_weights(0)), (LATE, weighted(3)),
                      (0, project_queries),
                      (CORE, scores(2)), (CORE, turn_weights(1)), (CORE, weighted(0)), (LATE, turn_out(0)),
                      (CORE, scores(3)), (CORE, turn_weights(2)), (CORE, weighted(1)), (LATE, turn_out(1))],
                 N, LEAD, UNROLL)


EXPERTS = 8
FFN = 1024
CAP = 128
GROUPS = 8
IN_GROUP = SAMPLES // GROUPS
HALF_GROUPS = GROUPS // 2
CHUNK = HALF_GROUPS * CAP
CHUNKS = 2 * EXPERTS
SLOTS = CHUNKS * CHUNK
SPARE = SLOTS


class RouterNorm(Norm):

    def __init__(self, m, pt, plg, wr, logits, x_out):
        xt = [m.sb(f"rxt{b}", [P, KD, C]) for b in (0, 1)]
        super().__init__(m, xt, pt, plg, None)
        self.wr, self.all_logits, self.x_out = wr, logits, x_out
        self.written = [m.sem(f"written{b}") for b in (0, 1)]
        self.wr_in = m.sem("wr_in")

    def xt_out(self, q, t, k):
        return self.xnt[t % 2][:, k, :]

    def kept(self, q):
        return self.all_logits[0:T, bass.ds(q * QUAD, QUAD), :]

    def source(self, b):
        return self.sums[b][0:T, :, :]

    def sync_and_write(self, sp, h_in):
        def load(q, t):
            b = t % 2
            wait(sp, self.d_xn, q - 1)
            sp.dma_start(self.h[b][0:T, :, :], h_in[bass.ds(q * QUAD, QUAD), :, :].rearrange("s t d -> t s d"))\
                .then_inc(self.loaded[b], 16)

        def write(q, t):
            b = t % 2
            sp.wait_ge(self.d_xn, q + 1)
            sp.dma_start(self.x_out[bass.ds(q * QUAD, QUAD), :, :].rearrange("s t d -> t s d"), self.xn[b][0:T, :, :])\
                .then_inc(self.written[b], 16)
        in_steps(sp, [(0, load), (1, write)], NQ, 4)
        for b in (0, 1):
            sp.wait_ge(self.written[b], 16 * (NQ // 2))

    def tensor(self, pe, idf):
        pe.wait_ge(self.wr_in, 16)

        def turn(q, t):
            b = t % 2
            pe.wait_ge(self.d_xn, q + 1)
            wait(pe, self.a_xt, (q - 1) * KD)
            for k in range(KD):
                for s in range(QUAD):
                    ins = pe.transpose(self.pt[b][:, k, s * T:(s + 1) * T], self.xn[b][0:T, s, k * P:(k + 1) * P],
                                       idf[0:T, 0:T])
            ins.then_inc(self.t_xt, 1)

        def logits(q, t):
            b = t % 2
            pe.wait_ge(self.a_xt, q * KD + KD)
            wait(pe, self.d_lg, q - 1)
            for s in range(QUAD):
                for k in range(KD):
                    ins = pe.matmul(self.sums[b][0:T, s, :], self.xnt[b][:, k, s * T:(s + 1) * T], self.wr[:, k, :],
                                    start=(k == 0), stop=(k == KD - 1))
            ins.then_inc(self.t_lg, 1)
        in_steps(pe, [(1, logits), (0, turn)], NQ, 4)


def expert_phase(nc, io, idf, h_in, out, x_dram, places, answers):
    with ExitStack() as ctx:
        m = Memory(nc, ctx, "e_")
        logits = m.sb("logits", [P, SAMPLES, EXPERTS])
        gates = m.sb("gates", [P, 2, SAMPLES])
        put = m.sb("put", [P, SAMPLES, 2], I32)
        get = m.sb("get", [P, SAMPLES, 2], I32)
        with ExitStack() as inner:
            n = Memory(nc, inner, "en_")
            wr = n.sb("wr", [P, KD, EXPERTS])
            zero = n.sb("zero", [P, SLOTS * D // P // 4])
            pt = [n.ps(f"pt{b}", [P, KD, 512]) for b in (0, 1)]
            plg = [n.ps(f"plg{b}", [P, QUAD, EXPERTS]) for b in (0, 1)]
            norm = RouterNorm(n, pt, plg, wr, logits, x_dram)
            zeroed = n.sem("zeroed")
            cleared = n.sem("cleared")
            block = inner.enter_context(nc.Block())

            @block.sync
            def _(sp):
                sp.dma_start(wr[:], io["ewr"].rearrange("(k p) n -> p k n", p=P)).then_inc(norm.wr_in, 16)
                norm.sync_and_write(sp, h_in)
                sp.wait_ge(cleared, 16 * 4)

            @block.gpsimd
            def _(pool):
                norm.gpsimd(pool)

            @block.scalar
            def _(act):
                act.wait_ge(zeroed, 1)
                rows = places[0:SLOTS, :].rearrange("(a p r) d -> a p (r d)", a=4, p=P)
                for a in range(4):
                    act.dma_start(rows[a], zero[:]).then_inc(cleared, 16)
                norm.scalar(act)

            @block.tensor
            def _(pe):
                norm.tensor(pe, idf)

            @block.vector
            def _(dve):
                dve.memset(zero[:], 0.0).then_inc(zeroed, 1)
                norm.vector(dve)

        with ExitStack() as inner:
            choose(nc, Memory(nc, inner, "ec_"), inner, logits, gates, put, get)
        with ExitStack() as inner:
            experts(nc, Memory(nc, inner, "ex_"), inner, io, idf, gates, put, get, h_in, out, x_dram, places, answers)


def choose(nc, m, ctx, logits, gates, put, get):
    S, E = SAMPLES, EXPERTS
    FULL = [P, S, E]
    shifted = m.sb("shifted", FULL)
    probs = m.sb("probs", FULL)
    left = m.sb("left", FULL)
    rank = m.sb("rank", FULL)
    order = m.sb("order", FULL, I32)
    orderf = m.sb("orderf", FULL)
    base = m.sb("base", FULL, I32)
    basef = m.sb("basef", FULL)
    spare = m.sb("spare", [P, 2, S], I32)
    sparef = m.sb("sparef", [P, 2, S])
    small = m.sb("small", [P, 8, S])
    mask = [m.sb(f"mask{k}", FULL, BF16) for k in (0, 1)]
    upto = m.sb("upto", [P, T], BF16)
    every = m.sb("every", [P, T], BF16)
    before = m.sb("before", [P, 2, GROUPS, IN_GROUP + 1, E])
    pos = m.sb("pos", FULL)
    work = m.sb("work", FULL)
    keep = m.sb("keep", [P, 2, S])
    row = m.sb("row", [P, 2, S])
    pc = [m.ps(f"pc{k}", [P, 512]) for k in (0, 1)]
    pa = [m.ps(f"pa{k}", [P, 512]) for k in (0, 1)]
    d = m.sem("d")
    g = m.sem("g")
    a = m.sem("a")
    masks = m.sem("masks")
    t_c = m.sem("t_c")
    block = ctx.enter_context(nc.Block())

    @block.gpsimd
    def _(pool):
        pool.iota(order[:], [[0, S], [-1, E]], base=E, channel_multiplier=0).then_inc(g, 1)
        for half in (0, 1):
            part = base[:, half * S // 2:(half + 1) * S // 2, :]
            pool.iota(part, [[CAP, HALF_GROUPS], [0, IN_GROUP], [CHUNK, E]], base=half * EXPERTS * CHUNK - 1,
                      channel_multiplier=0).then_inc(g, 1)
        pool.iota(spare[:], [[P * S, 2], [P, S]], base=SPARE, channel_multiplier=1).then_inc(g, 1)
        pool.memset(upto[:], 1.0).then_inc(g, 1)
        pool.memset(every[:], 1.0).then_inc(g, 1)
        pool.wait_ge(g, 6)
        pool.affine_select(out=upto[:], in_=upto[:], compare_op=ALU.is_ge, fill=0.0, base=0,
                           pattern=[[1, T]], channel_multiplier=-1).then_inc(g, 1)

    @block.scalar
    def _(act):
        act.wait_ge(d, 5)
        act.activation(shifted[0:T, :, :], shifted[0:T, :, :], ACT.Exp).then_inc(a, 1)

    @block.tensor
    def _(pe):
        pe.wait_ge(g, 7)
        for k in (0, 1):
            pe.wait_ge(masks, k + 1)
            flat = mask[k][0:T, :, :].rearrange("p s e -> p (s e)")
            pe.matmul(pc[k][0:T, :], upto[0:T, :], flat, start=True, stop=True)
            pe.matmul(pa[k][0:T, :], every[0:T, :], flat, start=True, stop=True).then_inc(t_c, 1)

    @block.vector
    def _(dve):
        count = [0]

        def then(ins):
            count[0] += 1
            ins.then_inc(d, 1)
            dve.wait_ge(d, count[0])

        def wide(x):
            return x.unsqueeze(2).to_broadcast([T, S, E])

        full = (slice(0, T), slice(None), slice(None))
        dve.wait_ge(g, 7)
        then(dve.tensor_copy(orderf[:], order[:]))
        then(dve.tensor_copy(basef[:], base[:]))
        then(dve.tensor_copy(sparef[:], spare[:]))
        top, total, recip, best = (small[0:T, x, :] for x in range(4))
        then(dve.tensor_reduce(top, logits[full], AX_X, ALU.max))
        then(dve.tensor_tensor(shifted[full], logits[full], wide(top), ALU.subtract))
        dve.wait_ge(a, 1)
        then(dve.tensor_reduce(total, shifted[full], AX_X, ALU.add))
        then(dve.reciprocal(recip, total))
        then(dve.tensor_tensor(probs[full], shifted[full], wide(recip), ALU.mult))
        for k in (0, 1):
            src = (probs, left)[k]
            gate = small[0:T, 4 + k, :]
            then(dve.tensor_reduce(gate, src[full], AX_X, ALU.max))
            then(dve.tensor_tensor(rank[full], src[full], wide(gate), ALU.is_equal))
            then(dve.tensor_tensor(rank[full], rank[full], orderf[full], ALU.mult))
            then(dve.tensor_reduce(best, rank[full], AX_X, ALU.max))
            then(dve.tensor_tensor(work[full], rank[full], wide(best), ALU.is_equal))
            dve.tensor_copy(mask[k][full], work[full]).then_inc(masks, 1)
            if k == 0:
                then(dve.scalar_tensor_tensor(out=left[full], in0=work[full], scalar=-2.0, in1=probs[full],
                                              op0=ALU.mult, op1=ALU.add))
        then(dve.memset(before[0:T, 0, :, 0, :], 0.0))
        for k in (0, 1):
            dve.wait_ge(t_c, k + 1)
            sums = pa[k][0:T, :].rearrange("p (g s e) -> p g s e", g=GROUPS, s=IN_GROUP)
            for s in range(IN_GROUP):
                then(dve.tensor_tensor(before[0:T, k, :, s + 1, :], before[0:T, k, :, s, :], sums[:, :, s, :], ALU.add))
            if k == 0:
                then(dve.tensor_copy(before[0:T, 1, :, 0, :], before[0:T, 0, :, IN_GROUP, :]))
            then(dve.tensor_tensor(pos[full].rearrange("p (g s) e -> p g s e", g=GROUPS),
                                   pc[k][0:T, :].rearrange("p (g s e) -> p g s e", g=GROUPS, s=IN_GROUP),
                                   before[0:T, k, :, 0:IN_GROUP, :], ALU.add))
            then(dve.scalar_tensor_tensor(out=work[full], in0=pos[full], scalar=float(CAP), in1=mask[k][full],
                                          op0=ALU.is_le, op1=ALU.mult))
            then(dve.tensor_reduce(keep[0:T, k, :], work[full], AX_X, ALU.add))
            then(dve.tensor_tensor(pos[full], pos[full], basef[full], ALU.add))
            then(dve.tensor_tensor(work[full], work[full], pos[full], ALU.mult))
            then(dve.tensor_reduce(row[0:T, k, :], work[full], AX_X, ALU.add))
            then(dve.tensor_tensor(gates[0:T, k, :], small[0:T, 4 + k, :], keep[0:T, k, :], ALU.mult))
            S2 = S // 2
            then(dve.tensor_copy(get[0:T, 0:S2, k], row[0:T, k, 0:S2]))
            then(dve.scalar_tensor_tensor(out=small[0:T, 6, S2:S], in0=keep[0:T, k, S2:S], scalar=-float(SLOTS // 2),
                                          in1=row[0:T, k, S2:S], op0=ALU.mult, op1=ALU.add))
            then(dve.tensor_copy(get[0:T, S2:S, k], small[0:T, 6, S2:S]))
            then(dve.tensor_scalar(keep[0:T, k, :], keep[0:T, k, :], -1.0, 1.0, ALU.mult, ALU.add))
            then(dve.tensor_tensor(keep[0:T, k, :], keep[0:T, k, :], sparef[0:T, k, :], ALU.mult))
            then(dve.tensor_tensor(put[0:T, :, k], row[0:T, k, :], keep[0:T, k, :], ALU.add))


def experts(nc, m, ctx, io, idf, gates, put, get, h_in, out, x_dram, places, answers):
    FT = FFN // P
    wi = [m.sb(f"wi{b}", [P, KD, FFN]) for b in (0, 1)]
    wo = [m.sb(f"wo{b}", [P, FT, D]) for b in (0, 1)]
    tok = [m.sb(f"tok{b}", [P, HALF_GROUPS, D]) for b in (0, 1)]
    xt = [m.sb(f"xt{b}", [P, KD, CHUNK]) for b in (0, 1)]
    hid = [m.sb(f"hid{b}", [P, FT, CHUNK]) for b in (0, 1)]
    ans = [m.sb(f"ans{b}", [P, HALF_GROUPS, D]) for b in (0, 1)]
    index = [m.sb(f"index{b}", [P, 2], I32) for b in range(4)]
    index2 = [m.sb(f"index2{b}", [P, 2], I32) for b in range(4)]
    x = [m.sb(f"x{b}", [P, D]) for b in range(4)]
    h = [m.sb(f"h{b}", [P, D]) for b in range(4)]
    got = [m.sb(f"got{b}", [P, 2, D]) for b in range(4)]
    pt = m.ps("pt", [P, KD, 512])
    pu = [m.ps(f"pu{b}", [P, 512]) for b in (0, 1)]
    pd = [m.ps(f"pd{b}", [P, 2, D]) for b in (0, 1)]

    idle = m.sb("idle", [1, 6])
    g_idle = m.sem("g_idle")
    g_met = [m.sem(f"g_met{i}") for i in range(5)]
    x_in = [m.sem(f"x_in{b}") for b in range(4)]
    sent = [m.sem(f"sent{b}") for b in range(4)]
    g_put = m.sem("g_put")
    loaded = [m.sem(f"loaded{b}") for b in (0, 1)]
    kept = [m.sem(f"kept{b}") for b in (0, 1)]
    t_t = m.sem("t_t")
    a_t = m.sem("a_t")
    t_u = m.sem("t_u")
    a_u = m.sem("a_u")
    t_d = m.sem("t_d")
    d_a = m.sem("d_a")
    g_get = m.sem("g_get")
    back = [m.sem(f"back{b}") for b in range(4)]
    d_c = m.sem("d_c")
    done = [m.sem(f"done{b}") for b in range(4)]
    HALF = SAMPLES // 2
    block = ctx.enter_context(nc.Block())

    def slot_uses(s, t, each):
        return (s - t) * (each // 4) if not isinstance(s, int) else each * (s // 4)

    @block.gpsimd
    def _(pool):
        pool.memset(idle[:], 0.0).then_inc(g_idle, 1)
        pool.wait_ge(g_idle, 1)

        def met(site, n):
            wait(pool, g_met[site], n)
            pool.tensor_tensor(idle[:, site + 1:site + 2], idle[:, 0:1], idle[:, 0:1], ALU.add).then_inc(g_met[site], 1)

        def take(s, t):
            wait(pool, sent[t], slot_uses(s, t, 32))
            met(0, s)
            pool.dma_start(x[t][0:T, :], x_dram[bass.ds(s, 1), :, :].rearrange("s t d -> (s t) d")).then_inc(x_in[t], 16)
            pool.tensor_copy(index[t][0:T, :], put[0:T, bass.ds(s, 1), :].rearrange("p s k -> p (s k)")).then_inc(g_put, 1)

        def send(s, t):
            pool.wait_ge(g_put, s + 1)
            pool.wait_ge(x_in[t], slot_uses(s, t, 16) + 16)
            met(1, s)
            for k in (0, 1):
                pool.indirect_dma_start(out=places[:, :], out_offset=bass.IndirectOffsetOnAxis(ap=index[t][0:T, k:k + 1], axis=0),
                                        in_=x[t][0:T, :], in_offset=None).then_inc(sent[t], 16)

        in_steps(pool, [(0, take), (2, send)], SAMPLES, 8)

        half_now = [0]

        def fetch(s, t):
            if isinstance(s, int) and s % HALF == 0:
                for b in (0, 1):
                    pool.wait_ge(kept[b], 16 * EXPERTS // 2 * (s // HALF + 1))
            wait(pool, d_c, (s - 3) * 2)
            wait(pool, done[t], slot_uses(s, t, 16))
            met(2, s)
            pool.dma_start(h[t][0:T, :], h_in[bass.ds(s, 1), :, :].rearrange("s t d -> (s t) d")).then_inc(back[t], 16)
            pool.tensor_copy(index2[t][0:T, :], get[0:T, bass.ds(s, 1), :].rearrange("p s k -> p (s k)")).then_inc(g_get, 1)
            pool.wait_ge(g_get, s + 1)
            met(3, s)
            for k in (0, 1):
                pool.indirect_dma_start(out=got[t][0:T, k, :], out_offset=None, in_=answers[half_now[0]][:, :],
                                        in_offset=bass.IndirectOffsetOnAxis(ap=index2[t][0:T, k:k + 1], axis=0))\
                    .then_inc(back[t], 16)

        def write(s, t):
            pool.wait_ge(d_c, s * 2 + 2)
            met(4, s)
            pool.dma_start(out[bass.ds(s, 1), :, :].rearrange("s t d -> (s t) d"), h[t][0:T, :]).then_inc(done[t], 16)

        for half in (0, 1):
            half_now[0] = half
            in_steps(pool, [(0, fetch), (2, write)], HALF, 8, base=half * HALF)
        for t in range(4):
            pool.wait_ge(done[t], 16 * SAMPLES // 4)

    @block.sync
    def _(sp):
        def chunk(c, t):
            b = t % 2
            if isinstance(c, int) and c % EXPERTS == 0:
                for i in range(4):
                    sp.wait_ge(sent[i], 32 * HALF // 4 * (c // EXPERTS + 1))
            wait(sp, t_d, (c - 1) * 2)
            e = c % EXPERTS if isinstance(c, int) else c - half_start[0]
            sp.dma_start(wi[b][:], io["ewi"][bass.ds(e, 1), :, :].rearrange("e (k p) f -> p (e k) f", p=P)).then_inc(loaded[b], 16)
            sp.dma_start(wo[b][:], io["ewo"][bass.ds(e, 1), :, :].rearrange("e (k p) n -> p (e k) n", p=P)).then_inc(loaded[b], 16)
            sp.dma_start(tok[b][:], places[bass.ds(c * CHUNK, CHUNK), :].rearrange("(g p) d -> p g d", p=P))\
                .then_inc(loaded[b], 16)

        def keep(c, t):
            b = t % 2
            sp.wait_ge(d_a, c * 2 + 2)
            e = c - half_start[0]
            sp.dma_start(answers[half_start[0] // EXPERTS][bass.ds(e * CHUNK, CHUNK), :].rearrange("(g p) d -> p g d", p=P), ans[b][:])\
                .then_inc(kept[b], 16)

        half_start = [0]
        for half in (0, 1):
            half_start[0] = half * EXPERTS
            in_steps(sp, [(0, chunk), (2, keep)], EXPERTS, 4, 2, base=half * EXPERTS)
        for b in (0, 1):
            sp.wait_ge(kept[b], 16 * CHUNKS // 2)

    def halves(eng, stages, second=()):
        for half in (0, 1):
            in_steps(eng, stages + (list(second) if half else []), EXPERTS, 4, 2, base=half * EXPERTS)

    @block.scalar
    def _(act):
        def empty(c, t):
            act.wait_ge(t_t, c + 1)
            for k in range(KD):
                act.activation(xt[t % 2][:, k, :], pt[:, k, :], ACT.Copy).then_inc(a_t, 1)

        def gelu(c, t):
            for f in range(FT):
                act.wait_ge(t_u, c * FT + (f + 1))
                act.activation(hid[t % 2][:, f, :], pu[f % 2][:], ACT.Gelu_apprx_tanh).then_inc(a_u, 1)

        halves(act, [(1, gelu), (0, empty)])

    @block.vector
    def _(dve):
        def answer(c, t):
            b = t % 2
            for r in (0, 1):
                dve.wait_ge(t_d, c * 2 + (r + 1))
                if r == 0:
                    wait(dve, kept[b], 16 * (c // 2) if isinstance(c, int) else (c - b) * 8)
                dve.tensor_copy(ans[b][:, 2 * r:2 * r + 2, :], pd[r][:]).then_inc(d_a, 1)

        def combine(s, t):
            dve.wait_ge(back[t], slot_uses(s, t, 48) + 48)
            tile = h[t][0:T, :]
            for k in (0, 1):
                if k:
                    dve.wait_ge(d_c, s * 2 + 1)
                dve.scalar_tensor_tensor(out=tile, in0=got[t][0:T, k, :],
                                         scalar=gates[0:T, k, bass.ds(s, 1)], in1=tile,
                                         op0=ALU.mult, op1=ALU.add).then_inc(d_c, 1)

        def combine_first(c, t):
            for i in range(4):
                combine((c - EXPERTS) * 4 + i, i)

        halves(dve, [(1, answer)], [(1, combine_first)])
        in_steps(dve, [(0, combine)], HALF, 8, base=HALF)

    @block.tensor
    def _(pe):
        def turn(c, t):
            b = t % 2
            if isinstance(c, int):
                pe.wait_ge(loaded[b], 48 * (c // 2 + 1))
            else:
                pe.wait_ge(loaded[b], (c - b) * 24 + 48)
            wait(pe, a_t, c * 2)
            for k in range(KD):
                for g in range(HALF_GROUPS):
                    ins = pe.transpose(pt[:, k, g * P:(g + 1) * P], tok[b][:, g, k * P:(k + 1) * P], idf[:, :])
            ins.then_inc(t_t, 1)

        def up(c, t):
            b = t % 2
            pe.wait_ge(a_t, c * 2 + 2)
            for f in range(FT):
                wait(pe, a_u, c * FT + (f - 1))
                for k in range(KD):
                    ins = pe.matmul(pu[f % 2][:], wi[b][:, k, f * P:(f + 1) * P], xt[b][:, k, :],
                                    start=(k == 0), stop=(k == KD - 1))
                ins.then_inc(t_u, 1)

        def down(c, t):
            b = t % 2
            pe.wait_ge(a_u, c * FT + FT)
            for r in (0, 1):
                wait(pe, d_a, (c - 1) * 2 + (r + 1))
                for g in (2 * r, 2 * r + 1):
                    for f in range(FT):
                        ins = pe.matmul(pd[r][:, g % 2, :], hid[b][:, f, g * P:(g + 1) * P], wo[b][:, f, :],
                                        start=(f == 0), stop=(f == FT - 1))
                ins.then_inc(t_d, 1)

        halves(pe, [(1, up), (0, turn), (1, down)])


def clear_semaphores(nc, used):
    with ExitStack() as ctx:
        block = ctx.enter_context(nc.Block())

        @block.gpsimd
        def _(pool):
            for semaphore in used:
                pool.sem_clear(semaphore)


def build(nc, io, out, scratch, rows):
    with ExitStack() as ctx:
        idf = ctx.enter_context(nc.sbuf_tensor("idf", [P, P], F32))
        used = make_identity(nc, idf)
        used = used + mixer_phase(nc, io, idf, scratch[0])
        clear_semaphores(nc, used)
        routed_phase(nc, io, idf, scratch[0], scratch[1])
        grouped_phase(nc, io, idf, scratch[1], scratch[2])
        expert_phase(nc, io, idf, scratch[2], out, *rows)


def kernel(**inputs):
    import numpy as _np
    import concourse.bacc as _bacc
    from concourse import mybir as _mybir
    from concourse.bass_utils import run_bass_kernel_spmd as _run

    a = {k: _np.ascontiguousarray(v) for k, v in inputs.items()}
    x = a["x"].reshape(16, 4, 3, 6, 16, 6, 16).transpose(0, 2, 4, 6, 1, 3, 5)
    x = _np.pad(x.reshape(16, 6, 128, 4, 36), ((0, 0),) * 4 + ((0, 28),))
    x = x.reshape(16, 6, 128, 256).transpose(0, 2, 1, 3)

    def cols(v, n):
        return v.reshape(4, 128, n).transpose(1, 0, 2).reshape(128, 4 * n)

    data = {
        "patches": x,
        "txt": a["txt"],
        "tokw": a["L0_tok_W"],
        "w1": a["L0_attn_W1"], "w2": a["L0_attn_W2"],
        "xpw": a["L0_attn_x_proj_w"], "dtw": a["L0_attn_dt_proj_w"], "wo0": a["L0_attn_Wo"],
        "cols": _np.concatenate([cols(a["L0_attn_b1"], 1), cols(a["L0_attn_b2"], 1), cols(a["L0_attn_conv_w"], 4),
                                 cols(a["L0_attn_conv_b"], 1), cols(a["L0_attn_dt_proj_b"], 1),
                                 cols(a["L0_attn_D_skip"], 1), cols(a["L0_attn_A_log"], 16)], axis=1),
        "brow": _np.concatenate([a["L0_tok_b"], a["L0_attn_bo"], a["L0_ffn_bo"]]).reshape(1, 3, 256),
    }
    data["rwqkv"] = _np.stack([a["L0_ffn_W" + w].reshape(256, 16, 64) for w in "qkv"], axis=2).reshape(256, 16, 192)
    data["rbias"] = _np.stack([a["L0_ffn_b" + w].reshape(16, 64) for w in "qkv"], axis=1).reshape(1, 16, 192)
    data["rwr"] = a["L0_ffn_Wr"]
    data["rwo"] = a["L0_ffn_Wo"]
    data["rbr"] = _np.broadcast_to(a["L0_ffn_br"], (64, 16))
    data["gwq"] = a["L1_attn_Wq"].reshape(256, 4, 4, 32, 2).transpose(0, 2, 4, 1, 3).reshape(256, 1024)
    data["gwk"] = a["L1_attn_Wk"].reshape(256, 4, 32, 2).transpose(0, 3, 1, 2).reshape(256, 256)
    data["gwv"], data["gwo"] = a["L1_attn_Wv"], a["L1_attn_Wo"]
    rate = (1.0 / 10000.0 ** (_np.arange(0, 64, 2, dtype=_np.float32) / _np.float32(64))).astype(_np.float32)
    angle = _np.arange(113, dtype=_np.float32)[None, :] * rate[:, None]
    data["cos"] = _np.tile(_np.cos(angle).astype(_np.float32), (4, 1))
    data["sin"] = _np.tile(_np.sin(angle).astype(_np.float32), (4, 1))
    data["ewr"], data["ewi"], data["ewo"] = a["L1_ffn_w_router"], a["L1_ffn_wi"], a["L1_ffn_wo"]
    nc = _bacc.Bacc("TRN2", target_bir_lowering=False, num_devices=1)
    arrays, io = {}, {}
    for name, v in data.items():
        v = _np.ascontiguousarray(v)
        arrays[f"in_{name}"] = v
        io[name] = nc.dram_tensor(f"in_{name}", v.shape, _mybir.dt.from_np(v.dtype), kind="ExternalInput").ap()
    out = nc.dram_tensor("out_h", (64, 113, 256), _mybir.dt.float32, kind="ExternalOutput").ap()
    scratch = [nc.dram_tensor(f"h{i}", (64, 113, 256), _mybir.dt.float32, kind="Internal").ap() for i in range(3)]
    rows = [nc.dram_tensor("normal", (64, 113, 256), _mybir.dt.float32, kind="Internal").ap(),
            nc.dram_tensor("places", (SLOTS + 2 * P * SAMPLES, 256), _mybir.dt.float32, kind="Internal").ap(),
            [nc.dram_tensor(f"answers{i}", (SLOTS // 2, 256), _mybir.dt.float32, kind="Internal").ap() for i in (0, 1)]]
    build(nc, io, out, scratch, rows)
    r = _run(nc, [arrays], core_ids=[0])
    return r.results[0]["out_h"]
```

```python
from contextlib import ExitStack
from functools import partial

import concourse.bass as bass
from concourse import mybir

ALU = mybir.AluOpType
ACT = mybir.ActivationFunctionType
AX_X = mybir.AxisListType.X
F32 = mybir.dt.float32
BF16 = mybir.dt.bfloat16
I32 = mybir.dt.int32
U32 = mybir.dt.uint32

P = 128
SAMPLES = 64
IMG = 36
ROWS = 64
TXT = 77
T = IMG + TXT
D = 256
KD = D // P
QUAD = 4
NQ = SAMPLES // QUAD
C = QUAD * T
KTOK = 768 // P
INNER = 512
J = INNER // P
NS = 16
RANK = 64
TAPS = 4
EPS = 1e-5

COL_B1, COL_B2, COL_CW, COL_CB, COL_DTB, COL_DS, COL_AL = 0, 4, 8, 24, 28, 32, 36
COLS = COL_AL + J * NS


class Memory:

    def __init__(self, nc, ctx, prefix):
        self.nc, self.ctx, self.prefix = nc, ctx, prefix
        self.semaphores = []

    def sb(self, name, shape, dt=F32):
        return self.ctx.enter_context(self.nc.sbuf_tensor(self.prefix + name, shape, dt))

    def ps(self, name, shape, dt=F32):
        return self.ctx.enter_context(self.nc.psum_tensor(self.prefix + name, shape, dt))

    def sem(self, name):
        self.semaphores.append(self.ctx.enter_context(self.nc.semaphore(self.prefix + name)))
        return self.semaphores[-1]


def layer_norm_stats(e, tile, stats, mv, veps, sem, base, spare):
    for s in range(QUAD):
        ins = e.bn_stats(stats[0:T, s, :], tile[0:T, s, :])
    ins.then_inc(sem, 1)
    e.wait_ge(sem, base + 1)
    e.memset(spare, 0.0)
    for s in range(QUAD):
        ins = e.bn_aggr(mv[0:T, s, :], stats[0:T, s, :])
    ins.then_inc(sem, 1)
    e.wait_ge(sem, base + 2)
    e.tensor_scalar(veps[0:T, :], mv[0:T, :, 1], EPS, None, ALU.add).then_inc(sem, 1)


def mixer_phase(nc, io, idf, h_out):
    with ExitStack() as ctx:
        m = Memory(nc, ctx, "m_")
        tokw = m.sb("tokw", [P, KTOK, D])
        w1 = m.sb("w1", [P, KD, INNER])
        w2 = m.sb("w2", [P, KD, INNER])
        xpw = m.sb("xpw", [P, J, 96])
        dtw = m.sb("dtw", [RANK, INNER])
        wo = m.sb("wo", [P, J, D])
        cols = m.sb("cols", [P, COLS])
        brow = m.sb("brow", [1, 2, D])
        nega = m.sb("nega", [P, J * NS])
        ones = m.sb("ones", [1, P])
        sel = m.sb("sel", [96, 2 * NS, P], BF16)
        half = m.sb("half", [P, QUAD])
        patches = m.sb("patches", [P, KTOK, QUAD * ROWS])
        fresh = m.sb("fresh", [P, QUAD, D])
        h = m.sb("h", [P, QUAD, D])
        u = [m.sb(f"u{b}", [P, J, QUAD, T]) for b in (0, 1)]
        gate = [m.sb(f"gate{b}", [P, J, QUAD, T]) for b in (0, 1)]
        delta = [m.sb(f"delta{b}", [P, J, QUAD, T]) for b in (0, 1)]
        du = [m.sb(f"du{b}", [P, J, QUAD, T]) for b in (0, 1)]
        bc = [m.sb(f"bc{b}", [96, C], BF16) for b in (0, 1)]
        stats = m.sb("stats", [P, QUAD, 6])
        mv = m.sb("mv", [P, QUAD, 2])
        spare = m.sb("spare", [1, 1])
        veps = m.sb("veps", [P, QUAD])
        rstd = m.sb("rstd", [P, QUAD])
        xn = m.sb("xn", [P, QUAD, D])
        xnt = m.sb("xnt", [P, KD, C])
        upad = m.sb("upad", [P, J, QUAD, T + TAPS - 1])
        absz = m.sb("absz", [P, J, QUAD, T])
        lnw = m.sb("lnw", [P, J, QUAD, T])
        rest = lnw[:, 2, :, :].rearrange("p s t -> p (s t)")
        dts = lnw[0:RANK, 3, :, :].rearrange("p s t -> p (s t)")
        cs = [m.sb(f"cs{b}", [P, C]) for b in range(4)]
        bs = [m.sb(f"bs{b}", [P, C]) for b in range(4)]
        da = [m.sb(f"da{b}", [P, J, QUAD, T]) for b in (0, 1)]
        dbu = [m.sb(f"dbu{b}", [P, J, QUAD, T]) for b in (0, 1)]
        hs = [m.sb(f"hs{b}", [P, J, QUAD, T]) for b in range(3)]
        py = m.ps("py", [P, J, 512])
        pb = m.ps("pb", [P, 512])
        pc = m.ps("pc", [P, 512])
        pp = [m.ps(f"pp{b}", [P, 512]) for b in (0, 1)]

        weights = m.sem("weights")
        patch_in = m.sem("patch_in")
        text_in = m.sem("text_in")
        kept = m.sem("kept")
        back = m.sem("back")
        stored = m.sem("stored")
        consts = m.sem("consts")
        dconsts = m.sem("dconsts")
        aconsts = m.sem("aconsts")
        proj = m.sem("proj")
        a_gate = m.sem("a_gate")
        a_dt = m.sem("a_dt")
        d_tok = m.sem("d_tok")
        d_ln = m.sem("d_ln")
        g_rstd = m.sem("g_rstd")
        d_xn = m.sem("d_xn")
        a_xnt = m.sem("a_xnt")
        a_upad = m.sem("a_upad")
        a_tap = m.sem("a_tap")
        d_du = m.sem("d_du")
        d_conv = m.sem("d_conv")
        a_u = m.sem("a_u")
        d_bc = m.sem("d_bc")
        a_sp = m.sem("a_sp")
        d_sp = m.sem("d_sp")
        t_b = m.sem("t_b")
        t_c = m.sem("t_c")
        a_bs = m.sem("a_bs")
        a_cs = m.sem("a_cs")
        a_da = m.sem("a_da")
        g_dbu = m.sem("g_dbu")
        d_scan = m.sem("d_scan")
        d_hc = m.sem("d_hc")
        t_y = m.sem("t_y")
        d_yg = m.sem("d_yg")
        d_h = m.sem("d_h")

        U, G, TOK, XP, DT, XT = 0, 4, 8, 9, 10, 14
        PRE, POST = 16, 2

        def state_buffer(n, b):
            return (b * NS + n) % 3

        def during(q):
            if not isinstance(q, int):
                return q * (PRE + POST) + (3 + PRE - POST)
            if q < 1:
                return {-2: 0, -1: 3, 0: 3 + PRE}[q]
            return q * (PRE + POST) + (3 + PRE - POST) - (3 if q == NQ - 1 else 0)

        def use(q, k):
            at = q - (2 if k in (TOK, XT, XT + 1) else 1)
            if isinstance(at, int) and at == -2:
                return (TOK, XT, XT + 1).index(k)
            if isinstance(at, int) and at < 1:
                return during(at) + k
            late = isinstance(at, int) and at == NQ - 2 and k > TOK
            return during(at) + (POST + k - (1 if late else 0))

        def out_use(q, r):
            if isinstance(q, int) and q == NQ - 1:
                return during(NQ - 1) + POST + r
            return during(q + 1) + r

        block = ctx.enter_context(nc.Block())

        @block.sync
        def _(sp):
            sp.dma_start(tokw[:], io["tokw"].rearrange("(k p) n -> p k n", p=P)).then_inc(weights, 16)
            sp.dma_start(w1[:], io["w1"].rearrange("(k p) n -> p k n", p=P)).then_inc(weights, 16)
            sp.dma_start(w2[:], io["w2"].rearrange("(k p) n -> p k n", p=P)).then_inc(weights, 16)
            sp.dma_start(xpw[:], io["xpw"].rearrange("(k p) n -> p k n", p=P)).then_inc(weights, 16)
            sp.dma_start(dtw[:], io["dtw"]).then_inc(weights, 16)
            sp.dma_start(wo[:], io["wo0"].rearrange("(k p) n -> p k n", p=P)).then_inc(weights, 16)
            sp.dma_start(cols[:], io["cols"]).then_inc(weights, 16)
            sp.dma_start(brow[:], io["brow"][:, 0:2, :]).then_inc(weights, 16)

            def quad_of(tensor, q):
                return tensor[bass.ds(q * QUAD, QUAD), :, :].rearrange("s t d -> t s d")

            def load(q):
                if not first(q):
                    sp.wait_ge(proj, use(q - 1, TOK) + 1)
                sp.dma_start(patches[:], io["patches"][bass.ds(q, 1), :, :, :].rearrange("q p k n -> p (q k) n"))\
                    .then_inc(patch_in, 16)
                if not first(q):
                    sp.wait_ge(kept, 16 * q)
                    sp.wait_ge(d_xn, q)
                sp.dma_start(fresh[IMG:T, :, :], quad_of(io["txt"], q)).then_inc(text_in, 16)

            def keep(q):
                sp.wait_ge(d_tok, q + 1)
                sp.dma_start(quad_of(h_out, q), fresh[0:T, :, :]).then_inc(kept, 16)

            def fetch(q):
                if not first(q):
                    sp.wait_ge(stored, 16 * q)
                sp.wait_ge(kept, 16 * (q + 1))
                sp.dma_start(h[0:T, :, :], quad_of(h_out, q)).then_inc(back, 16)

            def store(q):
                sp.wait_ge(d_h, 2 * q + 2)
                sp.dma_start(quad_of(h_out, q), h[0:T, :, :]).then_inc(stored, 16)

            load(0)
            for q in (0, 1):
                keep(q)
                load(q + 1)
            fetch(0)
            keep(2)
            load(3)
            with sp.Fori(1, NQ - 3) as q:
                store(q - 1)
                fetch(q)
                keep(q + 2)
                load(q + 3)
            for q in range(NQ - 3, NQ):
                store(q - 1)
                fetch(q)
                if q + 2 < NQ:
                    keep(q + 2)
            store(NQ - 1)
            sp.wait_ge(stored, 16 * NQ)

        @block.gpsimd
        def _(pool):
            pool.memset(ones[:], 1.0).then_inc(consts, 1)
            pool.memset(half[:], -0.5).then_inc(consts, 1)
            pool.memset(sel[:], 0.0).then_inc(consts, 1)
            for b in (0, 1):
                pool.memset(da[b][:, :, :, 0:1], 0.0).then_inc(consts, 1)
            pool.memset(upad[:, :, :, 0:TAPS - 1], 0.0).then_inc(consts, 1)
            pool.wait_ge(consts, 6)
            for a in range(3):
                part = sel[32 * a:32 * a + 32, :, :]
                pool.affine_select(out=part, in_=part, compare_op=ALU.not_equal, fill=1.0, base=0,
                                   pattern=[[-1, 2 * NS], [0, P]], channel_multiplier=1).then_inc(consts, 1)

            def pre_a(slot, q):
                if slot == 11:
                    pool.wait_ge(d_ln, q * 3 + 3)
                    pool.tensor_tensor(rstd[0:T, :], veps[0:T, :], half[0:T, :], ALU.pow).then_inc(g_rstd, 1)

            def products(n, q, b):
                pool.wait_ge(a_bs, q * NS + (n + 1))
                if n == 0:
                    pool.wait_ge(d_du, q + 1)
                if not (first(q) and n < 2):
                    pool.wait_ge(d_scan, q * NS + (n - 1))
                pool.tensor_tensor(dbu[n % 2][:].rearrange("p j s t -> p j (s t)"),
                                   du[b][:].rearrange("p j s t -> p j (s t)"),
                                   bs[n % 4][:, :].unsqueeze(1).to_broadcast([P, J, C]), ALU.mult).then_inc(g_dbu, 1)

            def step(n, q, b, more):
                ahead(products, n, 1, q, b, more)

            run_quads(pool, lambda slot, q, b: None, pre_a, step, lambda: products(0, 0, 0))

        @block.scalar
        def _(act):
            act.wait_ge(weights, 128)
            act.activation(nega[:], cols[:, COL_AL:COL_AL + J * NS], ACT.Exp).then_inc(aconsts, 1)
            act.wait_ge(aconsts, 1)
            act.activation(nega[:], nega[:], ACT.Copy, scale=-1.0).then_inc(aconsts, 1)
            act.wait_ge(aconsts, 2)
            act.wait_ge(consts, 9)
            act.preload_act_table_set("natural_log_exp_and_others")

            def pre_a(slot, q):
                if slot == 15:
                    act.wait_ge(proj, use(q, XT) + KD)
                    for k in range(KD):
                        act.activation(xnt[:, k, :], pp[(XT + k) % 2][:, 0:C], ACT.Copy).then_inc(a_xnt, 1)

            def pre_b(slot, q, b):
                if slot in (5, 6):
                    for j in (2 * slot - 10, 2 * slot - 9):
                        act.wait_ge(proj, use(q, U + j) + 1)
                        if j == 0:
                            act.wait_ge(d_sp, q * 3)
                        act.activation(upad[:, j, :, TAPS - 1:], pp[(U + j) % 2][:, 0:C].rearrange("p (s t) -> p s t", s=QUAD),
                                       ACT.Identity, bias=cols[:, COL_B1 + j:COL_B1 + j + 1])\
                           .then_inc(a_upad, 1)
                        act.wait_ge(a_upad, q * J + (j + 1))
                        act.activation(u[b][:, j, :, :], upad[:, j, :, 0:T], ACT.Identity,
                                       scale=cols[:, COL_CW + j * TAPS:COL_CW + j * TAPS + 1],
                                       bias=cols[:, COL_CB + j:COL_CB + j + 1]).then_inc(a_tap, 1)
                if slot in (7, 8):
                    for j in (2 * slot - 14, 2 * slot - 13):
                        act.wait_ge(proj, use(q, G + j) + 1)
                        act.activation(gate[b][:, j, :, :].rearrange("p s t -> p (s t)"), pp[(G + j) % 2][:, 0:C],
                                       ACT.Identity, bias=cols[:, COL_B2 + j:COL_B2 + j + 1]).then_inc(a_gate, 1)
                if slot == 8:
                    act.wait_ge(d_conv, q * 3 * J + 3 * J)
                    act.activation(u[b][:], u[b][:], ACT.Sigmoid).then_inc(a_u, 1)
                    act.wait_ge(a_gate, q * J + J)
                    act.activation(gate[b][:], gate[b][:], ACT.Sigmoid)
                    act.preload_act_table_set("natural_log_exp_and_others")
                if slot in (12, 13):
                    for j in (2 * slot - 24, 2 * slot - 23):
                        act.wait_ge(proj, use(q, DT + j) + 1)
                        zin = pp[(DT + j) % 2][:, 0:C]
                        bias = cols[:, COL_DTB + j:COL_DTB + j + 1]
                        act.activation(absz[:, j, :, :].rearrange("p s t -> p (s t)"), zin, ACT.Abs, bias=bias)
                        act.activation(delta[b][:, j, :, :].rearrange("p s t -> p (s t)"), zin, ACT.Relu, bias=bias)\
                            .then_inc(a_dt, 1)
                    part = slice(2 * slot - 24, 2 * slot - 22)
                    w = upad[:, part, :, TAPS - 1:]
                    at = q * 6 + (slot - 12) * 3
                    act.wait_ge(a_dt, q * J + (2 * slot - 22))
                    act.activation(absz[:, part], absz[:, part], ACT.Exp, scale=-1.0).then_inc(a_sp, 1)
                    act.wait_ge(a_sp, at + 1)
                    act.activation(w, absz[:, part], ACT.Identity, bias=1.0).then_inc(a_sp, 1)
                    act.wait_ge(a_sp, at + 2)
                    if slot == 13:
                        act.wait_ge(d_bc, q * 4 + 4)
                    act.activation(lnw[:, part], w, ACT.Ln).then_inc(a_sp, 1)

            def rows(n, q, b):
                act.wait_ge(t_b, q * NS + (n + 1))
                if not (first(q) and n < 4):
                    act.wait_ge(g_dbu, q * NS + (n - 3))
                act.activation(bs[n % 4][:], pb[:, 0:C], ACT.Copy).then_inc(a_bs, 1)
                act.wait_ge(t_c, q * NS + (n + 1))
                if not (first(q) and n < 4):
                    act.wait_ge(d_hc, q * NS + (n - 3))
                act.activation(cs[n % 4][:], pc[:, 0:C], ACT.Copy).then_inc(a_cs, 1)

            def decays(n, q, b):
                if n == 0:
                    act.wait_ge(d_sp, q * 3 + 3)
                if not (first(q) and n < 2):
                    act.wait_ge(d_scan, q * NS + (n - 1))
                for j in range(J):
                    ins = act.activation(da[n % 2][:, j, :, 1:T], delta[b][:, j, :, 1:T], ACT.Exp,
                                         scale=nega[:, j * NS + n:j * NS + n + 1])
                ins.then_inc(a_da, 1)

            def step(n, q, b, more):
                ahead(rows, n, 2, q, b, more)
                ahead(decays, n, 1, q, b, more)

            def start():
                for n in range(2):
                    rows(n, 0, 0)
                decays(0, 0, 0)

            run_quads(act, pre_b, pre_a, step, start)

        @block.vector
        def _(dve):
            dve.wait_ge(weights, 128)
            dve.wait_ge(consts, 9)

            def pre_a(slot, q):
                if slot == 9:
                    dve.wait_ge(text_in, 16 * (q + 1))
                    dve.wait_ge(proj, use(q, TOK) + 1)
                    for r in (0, 1):
                        ins = dve.tensor_copy(fresh[0:IMG, r::2, :],
                                              pp[TOK % 2][64 * r:64 * r + IMG, :].rearrange("p (a d) -> p a d", a=2))
                    ins.then_inc(d_tok, 1)
                    dve.wait_ge(d_tok, q + 1)
                    layer_norm_stats(dve, fresh, stats, mv, veps, d_ln, q * 3, spare[:])
                if slot == 12:
                    dve.wait_ge(g_rstd, q + 1)
                    for s in range(QUAD):
                        ins = dve.tensor_scalar(xn[0:T, s, :], fresh[0:T, s, :], mv[0:T, s, 0:1], rstd[0:T, s:s + 1],
                                                ALU.subtract, ALU.mult)
                    ins.then_inc(d_xn, 1)

            def pre_b(slot, q, b):
                if slot in (5, 6, 7):
                    for j in {5: (0,), 6: (1, 2), 7: (3,)}[slot]:
                        dve.wait_ge(a_tap, q * J + (j + 1))
                        for k in range(1, TAPS):
                            if k > 1:
                                dve.wait_ge(d_conv, q * 3 * J + (3 * j + k - 1))
                            dve.scalar_tensor_tensor(out=u[b][:, j, :, :], in0=upad[:, j, :, k:k + T],
                                                     scalar=cols[:, COL_CW + j * TAPS + k:COL_CW + j * TAPS + k + 1],
                                                     in1=u[b][:, j, :, :], op0=ALU.mult, op1=ALU.add).then_inc(d_conv, 1)
                if slot == 10:
                    dve.wait_ge(proj, use(q, XP) + 1)
                    src = pp[XP % 2]
                    dve.tensor_copy(dts, src[0:RANK, 0:C])
                    dve.tensor_copy(bc[b][0:32, :], src[64:96, 0:C]).then_inc(d_bc, 1)
                    dve.wait_ge(d_bc, q * 4 + 1)
                    dve.tensor_tensor(rest[32:64, :], src[64:96, 0:C], bc[b][0:32, :], ALU.subtract)\
                        .then_inc(d_bc, 1)
                    dve.wait_ge(d_bc, q * 4 + 2)
                    dve.tensor_copy(bc[b][32:64, :], rest[32:64, :]).then_inc(d_bc, 1)
                    dve.wait_ge(d_bc, q * 4 + 3)
                    dve.tensor_tensor(bc[b][64:96, :], rest[32:64, :], bc[b][32:64, :], ALU.subtract).then_inc(d_bc, 1)
                if slot == 14:
                    dve.wait_ge(a_sp, q * 6 + 6)
                    w = upad[:, :, :, TAPS - 1:]
                    dve.scalar_tensor_tensor(out=absz[:], in0=w, scalar=-1.0, in1=absz[:],
                                             op0=ALU.add, op1=ALU.subtract).then_inc(d_sp, 1)
                    dve.wait_ge(d_sp, q * 3 + 1)
                    dve.tensor_tensor(lnw[:], lnw[:], absz[:], ALU.subtract).then_inc(d_sp, 1)
                    dve.wait_ge(d_sp, q * 3 + 2)
                    dve.tensor_tensor(delta[b][:], delta[b][:], lnw[:], ALU.add).then_inc(d_sp, 1)
                    dve.wait_ge(d_sp, q * 3 + 3)
                    dve.wait_ge(a_u, q + 1)
                    dve.tensor_tensor(du[b][:], delta[b][:], u[b][:], ALU.mult).then_inc(d_du, 1)

            def step(n, q, b, more):
                cell = hs[state_buffer(n, b)]
                flat = cell[:].rearrange("p j s t -> p (j s t)")
                dve.wait_ge(a_da, q * NS + (n + 1))
                dve.wait_ge(g_dbu, q * NS + (n + 1))
                back_by = 2 if b == 0 and n < 2 else 3
                if not (first(q) and n < 3):
                    dve.wait_ge(t_y, q * NS + (n + 1 - back_by))
                dve.tensor_tensor_scan(flat, da[n % 2][:].rearrange("p j s t -> p (j s t)"),
                                       dbu[n % 2][:].rearrange("p j s t -> p (j s t)"), 0.0,
                                       ALU.mult, ALU.add).then_inc(d_scan, 1)
                dve.wait_ge(d_scan, q * NS + (n + 1))
                dve.wait_ge(a_cs, q * NS + (n + 1))
                v = cell[:].rearrange("p j s t -> p j (s t)")
                dve.tensor_tensor(v, v, cs[n % 4][:, :].unsqueeze(1).to_broadcast([P, J, C]), ALU.mult).then_inc(d_hc, 1)
                if n == 0 and not first(q):
                    gated(q - 1, 1 - b)
                if n in (2, 3) and not first(q):
                    residual(q - 1, n - 2)
                if n == NS - 1 and not more:
                    gated(q, b)
                    residual(q, 0)
                    residual(q, 1)

            def gated(q, b):
                dve.wait_ge(t_y, q * NS + NS)
                for j in range(J):
                    flat = u[b][:, j, :, :].rearrange("p s t -> p (s t)")
                    ins = dve.scalar_tensor_tensor(out=flat, in0=flat, scalar=cols[:, COL_DS + j:COL_DS + j + 1],
                                                   in1=py[:, j, 0:C], op0=ALU.mult, op1=ALU.add)
                ins.then_inc(d_yg, 1)
                dve.wait_ge(d_yg, q * 2 + 1)
                dve.tensor_tensor(u[b][:], u[b][:], gate[b][:], ALU.mult).then_inc(d_yg, 1)

            def residual(q, r):
                if r == 0:
                    dve.wait_ge(back, 16 * (q + 1))
                dve.wait_ge(proj, out_use(q, r) + 1)
                part = h[0:T, 2 * r:2 * r + 2, :]
                dve.tensor_tensor(part, part, pp[r][0:T, :].rearrange("p (a d) -> p a d", a=2), ALU.add).then_inc(d_h, 1)

            run_quads(dve, pre_b, pre_a, step, lambda: None)

        @block.tensor
        def _(pe):
            pe.wait_ge(weights, 128)
            pe.wait_ge(consts, 9)

            def pre_a(slot, q):
                if slot == 7:
                    pe.wait_ge(patch_in, 16 * (q + 1))
                    if not first(q):
                        pe.wait_ge(a_gate, (q - 1) * J + 3)
                    for a in (0, 1):
                        out = pp[TOK % 2][:, a * D:(a + 1) * D]
                        for k in range(KTOK):
                            pe.matmul(out, patches[:, k, a * P:(a + 1) * P], tokw[:, k, :], start=(k == 0), stop=False)
                        ins = pe.matmul(out, ones[:, :], brow[:, 0, :], start=False, stop=True)
                    ins.then_inc(proj, 1)
                if slot == 13:
                    pe.wait_ge(d_xn, q + 1)
                    for k in range(KD):
                        if not first(q):
                            pe.wait_ge(a_dt, (q - 1) * J + 3 + k)
                        elif k == 0:
                            pe.wait_ge(d_tok, 1)
                        for s in range(QUAD):
                            ins = pe.transpose(pp[(XT + k) % 2][:, s * T:(s + 1) * T], xn[0:T, s, k * P:(k + 1) * P],
                                               idf[0:T, 0:T])
                        ins.then_inc(proj, 1)

            def pre_b(slot, q, b):
                if slot in (3, 4):
                    for j in (2 * slot - 6, 2 * slot - 5):
                        if slot == 4:
                            pe.wait_ge(a_upad, q * J + (j - 1))
                        else:
                            pe.wait_ge(a_xnt, q * KD + KD)
                            if not first(q) and not one(q):
                                pe.wait_ge(d_h, (q - 2) * 2 + j + 1)
                        project(U, w1, j)
                if slot in (5, 6):
                    for j in (2 * slot - 10, 2 * slot - 9):
                        if slot == 5:
                            pe.wait_ge(a_upad, q * J + (j + 3))
                        else:
                            pe.wait_ge(a_gate, q * J + (j - 1))
                        project(G, w2, j)
                if slot == 8:
                    pe.wait_ge(a_gate, q * J + J)
                    pe.wait_ge(a_u, q + 1)
                    for j in range(J):
                        ins = pe.matmul(pp[XP % 2][0:96, 0:C], xpw[:, j, :], u[b][:, j, :, :].rearrange("p s t -> p (s t)"),
                                        start=(j == 0), stop=(j == J - 1))
                    ins.then_inc(proj, 1)
                if slot in (10, 11):
                    for j in (2 * slot - 20, 2 * slot - 19):
                        if j == 0:
                            if not (isinstance(q, int) and q == NQ - 1):
                                pe.wait_ge(d_tok, q + 2)
                            pe.wait_ge(d_bc, q * 4 + 1)
                        elif j == 1:
                            pe.wait_ge(d_bc, q * 4 + 2)
                        else:
                            pe.wait_ge(a_dt, q * J + (j - 1))
                        pe.matmul(pp[(DT + j) % 2][:, 0:C], dtw[:, j * P:(j + 1) * P], dts,
                                  start=True, stop=True).then_inc(proj, 1)

            def project(at, w, j):
                for k in range(KD):
                    ins = pe.matmul(pp[(at + j) % 2][:, 0:C], w[:, k, j * P:(j + 1) * P], xnt[:, k, :],
                                    start=(k == 0), stop=(k == KD - 1))
                ins.then_inc(proj, 1)

            def rows(n, q, b):
                if n == 0:
                    pe.wait_ge(d_bc, q * 4 + 4)
                pe.wait_ge(a_bs, q * NS + n)
                pe.matmul(pb[:, 0:C], sel[:, n, :], bc[b][:], start=True, stop=True).then_inc(t_b, 1)
                pe.wait_ge(a_cs, q * NS + n)
                pe.matmul(pc[:, 0:C], sel[:, NS + n, :], bc[b][:], start=True, stop=True).then_inc(t_c, 1)

            def step(n, q, b, more):
                ahead(rows, n, 3, q, b, more)
                if n == 0 and not first(q):
                    pe.wait_ge(d_yg, q * 2 - 1)
                pe.wait_ge(d_hc, q * NS + (n + 1))
                for j in range(J):
                    ins = pe.matmul(py[:, j, 0:C], idf[:, :], hs[state_buffer(n, b)][:, j, :, :].rearrange("p s t -> p (s t)"),
                                    start=(n == 0), stop=(n == NS - 1))
                ins.then_inc(t_y, 1)
                if n in (0, 1) and not first(q):
                    output(q - 1, 1 - b, n)
                if n == NS - 1 and not more:
                    output(q, b, 0)
                    output(q, b, 1)

            def output(q, b, r):
                if r == 0:
                    pe.wait_ge(d_yg, q * 2 + 2)
                    if isinstance(q, int) and q == NQ - 1:
                        pe.wait_ge(d_h, 2 * q)
                    elif isinstance(q, int) and q == NQ - 2:
                        pe.wait_ge(a_dt, NQ * J)
                    else:
                        pe.wait_ge(a_xnt, (q + 3) * KD)
                for a in (0, 1):
                    out = pp[r][0:T, a * D:(a + 1) * D]
                    for j in range(J):
                        pe.matmul(out, u[b][:, j, 2 * r + a, :], wo[:, j, :], start=(j == 0), stop=False)
                    ins = pe.matmul(out, ones[:, 0:T], brow[:, 1, :], start=False, stop=True)
                ins.then_inc(proj, 1)

            def start():
                for n in range(3):
                    rows(n, 0, 0)

            run_quads(pe, pre_b, pre_a, step, start)
        used = m.semaphores
    return used


def first(q):
    return isinstance(q, int) and q == 0


def one(q):
    return isinstance(q, int) and q == 1


def ahead(work, n, by, q, b, more):
    if n + by < NS:
        work(n + by, q, b)
    elif more:
        work(n + by - NS, q + 1, 1 - b)


def run_quads(eng, pre_b, pre_a, step, start):
    def slots(slot, q, b):
        if not isinstance(q, int) or -1 <= q < NQ - 1:
            pre_b(slot, q + 1, 1 - b)
        if not isinstance(q, int) or q < NQ - 2:
            pre_a(slot, q + 2)

    def quad(q, b):
        for n in range(NS):
            step(n, q, b, not (isinstance(q, int) and q == NQ - 1))
            slots(n, q, b)

    for q in (-2, -1):
        for slot in range(NS):
            slots(slot, q, q % 2)
    start()
    quad(0, 0)
    with eng.Fori(0, (NQ - 4) // 2) as i:
        quad(2 * i + 1, 1)
        quad(2 * i + 2, 0)
    for q in range(NQ - 3, NQ):
        quad(q, q % 2)


def make_identity(nc, idf):
    with ExitStack() as ctx:
        made = ctx.enter_context(nc.semaphore("identity_made"))
        block = ctx.enter_context(nc.Block())

        @block.gpsimd
        def _(pool):
            pool.memset(idf[:], 0.0).then_inc(made, 1)
            pool.wait_ge(made, 1)
            pool.affine_select(out=idf[:], in_=idf[:], compare_op=ALU.not_equal, fill=1.0, base=0,
                               pattern=[[-1, P]], channel_multiplier=1).then_inc(made, 1)
            pool.wait_ge(made, 2)
    return [made]



def in_steps(eng, stages, items, lead, unroll=4, base=0):
    tail = max(lag for lag, _ in stages)

    def step(i, t):
        for lag, work in stages:
            if not isinstance(i, int) or 0 <= i - lag < items:
                work(i + (base - lag), (t - lag) % unroll)

    for i in range(lead):
        step(i, i % unroll)
    with eng.Fori(0, (items - lead) // unroll) as m:
        for t in range(unroll):
            step(unroll * m + (lead + t), t)
    for i in range(items, items + tail):
        step(i, i % unroll)


def wait(eng, sem, value):
    if not isinstance(value, int) or value > 0:
        eng.wait_ge(sem, value)


class Norm:

    def __init__(self, m, xnt, pt, sums=None, kept=None):
        self.h = [m.sb(f"nh{b}", [P, QUAD, D]) for b in range(4)]
        self.xn = [m.sb(f"nxn{b}", [P, QUAD, D]) for b in (0, 1)]
        self.stats = m.sb("nstats", [P, QUAD, 6])
        self.mv = [m.sb(f"nmv{b}", [P, QUAD, 2]) for b in (0, 1)]
        self.veps = [m.sb(f"nveps{b}", [P, QUAD]) for b in (0, 1)]
        self.rstd = [m.sb(f"nrstd{b}", [P, QUAD]) for b in (0, 1)]
        self.spare = m.sb("nspare", [1, 1])
        self.half = m.sb("nhalf", [P, QUAD])
        self.ones = m.sb("nones", [P, 1])
        self.xnt, self.pt, self.sums, self.written = xnt, pt, sums, None
        if kept is not None:
            self.kept = kept
        self.loaded = [m.sem(f"nloaded{b}") for b in range(4)]
        self.made = m.sem("nmade")
        self.d_st = m.sem("nd_st")
        self.g_rstd = m.sem("ng_rstd")
        self.d_xn = m.sem("nd_xn")
        self.t_xt = m.sem("nt_xt")
        self.a_xt = m.sem("na_xt")
        self.t_lg = m.sem("nt_lg")
        self.d_lg = m.sem("nd_lg")

    def xt_out(self, q, t, k):
        return self.xnt[:, k, bass.ds(q * C, C)]

    def source(self, b):
        return self.sums[b][:]

    def sync(self, sp, h_in):
        def load(q, t):
            wait(sp, self.d_xn, q - 3)
            sp.dma_start(self.h[t][0:T, :, :], h_in[bass.ds(q * QUAD, QUAD), :, :].rearrange("s t d -> t s d"))\
                .then_inc(self.loaded[t], 16)
        in_steps(sp, [(0, load)], NQ, 4)

    def gpsimd(self, pool):
        pool.memset(self.half[:], -0.5).then_inc(self.made, 1)
        pool.memset(self.ones[:], 1.0).then_inc(self.made, 1)
        pool.wait_ge(self.made, 2)

        def power(q, t):
            b = t % 2
            pool.wait_ge(self.d_st, q * 3 + 3)
            pool.tensor_tensor(self.rstd[b][0:T, :], self.veps[b][0:T, :], self.half[0:T, :], ALU.pow)\
                .then_inc(self.g_rstd, 1)
        in_steps(pool, [(0, power)], NQ, 4)

    def vector(self, dve):
        def stats(q, t):
            b = t % 2
            if isinstance(q, int):
                dve.wait_ge(self.loaded[t], 16 * (q // 4 + 1))
            else:
                dve.wait_ge(self.loaded[t], (q - t) * 4 + 16)
            layer_norm_stats(dve, self.h[t], self.stats, self.mv[b], self.veps[b], self.d_st, q * 3, self.spare[:])

        def normal(q, t):
            b = t % 2
            dve.wait_ge(self.g_rstd, q + 1)
            wait(dve, self.t_xt, q - 1)
            if self.sums is not None:
                wait(dve, self.t_lg, q - 1)
            if self.written is not None:
                wait(dve, self.written[b], 16 * (q // 2) if isinstance(q, int) else (q - b) * 8)
            for s in range(QUAD):
                ins = dve.tensor_scalar(self.xn[b][0:T, s, :], self.h[t][0:T, s, :], self.mv[b][0:T, s, 0:1],
                                        self.rstd[b][0:T, s:s + 1], ALU.subtract, ALU.mult)
            ins.then_inc(self.d_xn, 1)

        def keep(q, t):
            b = t % 2
            dve.wait_ge(self.t_lg, q + 1)
            dve.tensor_scalar(self.kept(q), self.source(b), 1.0, None, ALU.mult).then_inc(self.d_lg, 1)

        stages = [(3, keep)] if self.sums is not None else []
        in_steps(dve, stages + [(0, stats), (1, normal)], NQ, 4)

    def tensor(self, pe, idf):
        pe.wait_ge(self.made, 2)

        def turn(q, t):
            b = t % 2
            pe.wait_ge(self.d_xn, q + 1)
            wait(pe, self.a_xt, (q - 1) * KD)
            for k in range(KD):
                for s in range(QUAD):
                    ins = pe.transpose(self.pt[b][:, k, s * T:(s + 1) * T], self.xn[b][0:T, s, k * P:(k + 1) * P],
                                       idf[0:T, 0:T])
            ins.then_inc(self.t_xt, 1)
            if self.sums is not None:
                wait(pe, self.d_lg, q - 1)
                for k in range(KD):
                    for s in range(QUAD):
                        ins = pe.matmul(self.sums[b][:, k, s:s + 1], self.xn[b][0:T, s, k * P:(k + 1) * P],
                                        self.ones[0:T, :], start=True, stop=True)
                ins.then_inc(self.t_lg, 1)
        in_steps(pe, [(0, turn)], NQ, 4)

    def scalar(self, act, beside=None):
        def empty(q, t):
            b = t % 2
            if beside is not None:
                beside(q)
            act.wait_ge(self.t_xt, q + 1)
            for k in range(KD):
                act.activation(self.xt_out(q, t, k), self.pt[b][:, k, 0:C], ACT.Copy)\
                    .then_inc(self.a_xt, 1)
        in_steps(act, [(0, empty)], NQ, 4)


HEADS = 16
ACTIVE = 4
DH = 64
HEAD_W = 3 * DH
KB = KD + 1


def routed_phase(nc, io, idf, h_in, h_out):
    with ExitStack() as ctx:
        m = Memory(nc, ctx, "r_")
        xnt = m.sb("xnt", [P, KD, SAMPLES * T])
        wqkv = m.sb("wqkv", [P, KB, HEADS, HEAD_W])
        wr = m.sb("wr", [P, KD, HEADS])
        wo = m.sb("wo", [P, KD, D])
        br = m.sb("br", [SAMPLES, HEADS])
        brow = m.sb("brow", [1, D])
        xs = m.sb("xs", [P, KD, SAMPLES])
        ones = m.sb("ones", [P, P])
        picks = m.sb("picks", [P, SAMPLES, 2 * ACTIVE])
        heads = m.sb("heads", [P, SAMPLES, ACTIVE], I32)
        weights = m.sem("weights")
        consts = m.sem("consts")
        with ExitStack() as inner:
            n = Memory(nc, inner, "rn_")
            pt = [n.ps(f"pt{b}", [P, KD, 512]) for b in (0, 1)]
            sums = [n.ps(f"sums{b}", [P, KD, QUAD]) for b in (0, 1)]
            norm = Norm(n, xnt, pt, sums, lambda q: xs[:, :, bass.ds(q * QUAD, QUAD)])
            block = inner.enter_context(nc.Block())

            @block.sync
            def _(sp):
                norm.sync(sp, h_in)

            @block.gpsimd
            def _(pool):
                pool.memset(wqkv[:, KD, :, :], 0.0).then_inc(consts, 1)
                pool.memset(ones[:], 1.0).then_inc(consts, 1)
                norm.gpsimd(pool)

            @block.scalar
            def _(act):
                act.dma_start(wqkv[:, 0:KD, :, :], io["rwqkv"].rearrange("(k p) h d -> p k (h d)", p=P))\
                    .then_inc(weights, 16)
                act.dma_start(wr[:], io["rwr"].rearrange("(k p) h -> p k h", p=P)).then_inc(weights, 16)
                act.dma_start(wo[:], io["rwo"].rearrange("(k p) n -> p k n", p=P)).then_inc(weights, 16)
                act.dma_start(br[:], io["rbr"]).then_inc(weights, 16)
                act.dma_start(brow[:], io["brow"][:, 2, :]).then_inc(weights, 16)
                act.wait_ge(consts, 2)
                act.dma_start(wqkv[0:1, KD, :, :], io["rbias"]).then_inc(weights, 16)
                norm.scalar(act)

            @block.tensor
            def _(pe):
                norm.tensor(pe, idf)

            @block.vector
            def _(dve):
                norm.vector(dve)

        with ExitStack() as inner:
            n = Memory(nc, inner, "rr_")
            route(nc, n, inner, idf, xs, wr, br, ones, picks, heads, weights)
        with ExitStack() as inner:
            n = Memory(nc, inner, "ra_")
            routed_attention(nc, n, inner, idf, xnt, wqkv, wo, brow, ones, picks, heads, h_in, h_out)


def route(nc, m, ctx, idf, xs, wr, br, ones, picks, heads, weights):
    S = SAMPLES
    lg = m.sb("lg", [S, HEADS])
    top = m.sb("top", [S, 8])
    neg = m.sb("neg", [S, 2])
    ex = m.sb("ex", [S, HEADS])
    tot = m.sb("tot", [S, 4])
    dist = m.sb("dist", [S, HEADS])
    best = m.sb("best", [S, 8])
    index = m.sb("index", [S, 8], U32)
    ev = m.sb("ev", [S, ACTIVE + 1])
    pick = m.sb("pick", [S, 2 * ACTIVE])
    spread = m.sb("spread", [S, S, 2 * ACTIVE])
    pl = m.ps("pl", [P, 512])
    pp = m.ps("pp", [P, 512])
    t_l = m.sem("t_l")
    t_p = m.sem("t_p")
    d = m.sem("d")
    a = m.sem("a")
    block = ctx.enter_context(nc.Block())

    @block.tensor
    def _(pe):
        pe.wait_ge(weights, 6 * 16)
        for k in range(KD):
            ins = pe.matmul(pl[0:S, 0:HEADS], xs[:, k, :], wr[:, k, :], start=(k == 0), stop=(k == KD - 1))
        ins.then_inc(t_l, 1)
        pe.wait_ge(d, 13)
        pe.matmul(pp[:, :], ones[0:S, :], spread[:].rearrange("p s k -> p (s k)"), start=True, stop=True)\
            .then_inc(t_p, 1)

    @block.scalar
    def _(act):
        act.wait_ge(d, 3)
        act.activation(ex[:], lg[:], ACT.Exp, bias=neg[:, 0:1], accum_out=tot[:, 0:1]).then_inc(a, 1)
        act.wait_ge(d, 8)
        act.activation(ev[:, 0:ACTIVE], best[:, 0:ACTIVE], ACT.Exp, bias=neg[:, 1:2],
                       accum_out=tot[:, 2:3]).then_inc(a, 1)
        act.activation(ev[:, ACTIVE:], neg[:, 1:2], ACT.Exp).then_inc(a, 1)

    @block.vector
    def _(dve):
        count = [0]

        def then(ins):
            count[0] += 1
            ins.then_inc(d, 1)
            dve.wait_ge(d, count[0])

        dve.wait_ge(t_l, 1)
        dve.wait_ge(weights, 6 * 16)
        then(dve.scalar_tensor_tensor(out=lg[:], in0=pl[0:S, 0:HEADS], scalar=1.0 / T, in1=br[:],
                                      op0=ALU.mult, op1=ALU.add))
        then(dve.max(top[:], lg[:]))
        then(dve.tensor_scalar(neg[:, 0:1], top[:, 0:1], -1.0, None, ALU.mult))
        dve.wait_ge(a, 1)
        then(dve.reciprocal(tot[:, 1:2], tot[:, 0:1]))
        then(dve.tensor_scalar(dist[:], ex[:], tot[:, 1:2], None, ALU.mult))
        then(dve.max(best[:], dist[:]))
        then(dve.max_index(index[:], best[:], dist[:]))
        then(dve.tensor_scalar(neg[:, 1:2], best[:, 0:1], -1.0, None, ALU.mult))
        dve.wait_ge(a, 3)
        then(dve.scalar_tensor_tensor(out=tot[:, 3:4], in0=ev[:, ACTIVE:], scalar=float(HEADS - ACTIVE),
                                      in1=tot[:, 2:3], op0=ALU.mult, op1=ALU.add))
        then(dve.reciprocal(tot[:, 0:1], tot[:, 3:4]))
        then(dve.tensor_scalar(pick[:, 0:ACTIVE], ev[:, 0:ACTIVE], tot[:, 0:1], None, ALU.mult))
        then(dve.tensor_copy(pick[:, ACTIVE:], index[:, 0:ACTIVE]))
        then(dve.tensor_tensor(spread[:], idf[0:S, 0:S].unsqueeze(2).to_broadcast([S, S, 2 * ACTIVE]),
                               pick[:].unsqueeze(1).to_broadcast([S, S, 2 * ACTIVE]), ALU.mult))
        dve.wait_ge(t_p, 1)
        then(dve.tensor_copy(picks[:].rearrange("p s k -> p (s k)"), pp[:, :]))
        then(dve.tensor_copy(heads[:], picks[:, :, ACTIVE:]))


def routed_attention(nc, m, ctx, idf, xnt, wqkv, wo, brow, ones, picks, heads, h_in, h_out):
    A = ACTIVE
    wsel = [m.sb(f"wsel{b}", [P, KB, 3, A, DH]) for b in (0, 1)]
    xcur = [m.sb(f"xcur{b}", [P, KD, T]) for b in (0, 1)]
    qk = [m.sb(f"qk{b}", [P, 4, T]) for b in (0, 1)]
    v = [m.sb(f"v{b}", [P, A, DH + 1]) for b in range(4)]
    sh = [m.sb(f"sh{b}", [P, A, T]) for b in (0, 1)]
    pr = [m.sb(f"pr{b}", [P, A, T]) for b in (0, 1)]
    prt = [m.sb(f"prt{b}", [P, A, T]) for b in (0, 1)]
    o = [m.sb(f"o{b}", [P, A, DH]) for b in (0, 1)]
    ot = [m.sb(f"ot{b}", [P, KD, T]) for b in (0, 1)]
    top = m.sb("top", [P, A])
    rec = m.sb("rec", [P, A])
    h = [m.sb(f"h{b}", [P, D]) for b in range(4)]
    pqk = m.ps("pqk", [P, 512])
    pv = m.ps("pv", [P, 512])
    psc = m.ps("psc", [P, 2, 512])
    ptr = m.ps("ptr", [P, 512])
    po = m.ps("po", [P, 512])
    pot = m.ps("pot", [P, 512])
    pout = m.ps("pout", [P, 512])

    g_one = m.sem("g_one")
    g_x = m.sem("g_x")
    d_sel = m.sem("d_sel")
    t_qkv = m.sem("t_qkv")
    a_qk = m.sem("a_qk")
    a_v = m.sem("a_v")
    t_sc = m.sem("t_sc")
    d_mx = m.sem("d_mx")
    d_sh = m.sem("d_sh")
    a_ex = m.sem("a_ex")
    t_tr = m.sem("t_tr")
    a_tr = m.sem("a_tr")
    t_o = m.sem("t_o")
    d_rec = m.sem("d_rec")
    d_o = m.sem("d_o")
    t_ot = m.sem("t_ot")
    a_ot = m.sem("a_ot")
    t_out = m.sem("t_out")
    d_h = m.sem("d_h")
    loaded = [m.sem(f"loaded{b}") for b in range(4)]
    stored = [m.sem(f"stored{b}") for b in range(4)]
    N = SAMPLES
    SEL, QKV, SC, TR, O, OT, OUT = range(7)
    LEAD = 8
    block = ctx.enter_context(nc.Block())

    @block.sync
    def _(sp):
        def load(s, t):
            if not isinstance(s, int):
                sp.wait_ge(stored[t], (s - t) * 4)
            elif s >= 4:
                sp.wait_ge(stored[t], 16 * (s // 4))
            sp.dma_start(h[t][0:T, :], h_in[bass.ds(s, 1), :, :].rearrange("s t d -> (s t) d")).then_inc(loaded[t], 16)

        def store(s, t):
            sp.wait_ge(d_h, s + 1)
            sp.dma_start(h_out[bass.ds(s, 1), :, :].rearrange("s t d -> (s t) d"), h[t][0:T, :]).then_inc(stored[t], 16)

        in_steps(sp, [(O, load), (OUT + 1, store)], N, LEAD)
        for t in range(4):
            sp.wait_ge(stored[t], 16 * (N // 4))

    @block.gpsimd
    def _(pool):
        for b in range(4):
            pool.memset(v[b][:, :, DH:], 1.0).then_inc(g_one, 1)

        def current(s, t):
            wait(pool, t_qkv, (s - 1) * 2)
            pool.tensor_copy(xcur[t % 2][:], xnt[:, :, bass.ds(s * T, T)]).then_inc(g_x, 1)

        in_steps(pool, [(SEL, current)], N, LEAD)

    @block.scalar
    def _(act):
        act.wait_ge(g_one, 4)

        def project(s, t):
            act.wait_ge(t_qkv, s * 2 + 1)
            wait(act, t_sc, s - 1)
            act.activation(qk[t % 2][:].rearrange("p x t -> p (x t)"), pqk[:, 0:C], ACT.Copy).then_inc(a_qk, 1)
            act.wait_ge(t_qkv, s * 2 + 2)
            wait(act, t_o, s - 3)
            act.activation(v[t][0:T, :, 0:DH], pv[0:T, 0:D].rearrange("p (a d) -> p a d", a=A), ACT.Copy)\
                .then_inc(a_v, 1)

        def weights(s, t):
            act.wait_ge(d_sh, s + 1)
            wait(act, t_tr, s - 1)
            act.activation(pr[t % 2][0:T, :, :], sh[t % 2][0:T, :, :], ACT.Exp, scale=DH ** -0.5).then_inc(a_ex, 1)

        def turned(s, t):
            act.wait_ge(t_tr, s + 1)
            wait(act, t_o, s - 1)
            act.activation(prt[t % 2][0:T, :, :].rearrange("p a t -> p (a t)"), ptr[0:T, 0:C], ACT.Copy)\
                .then_inc(a_tr, 1)

        def out_turned(s, t):
            act.wait_ge(t_ot, s + 1)
            wait(act, t_out, s - 1)
            act.activation(ot[t % 2][:].rearrange("p k t -> p (k t)"), pot[:, 0:KD * T], ACT.Copy).then_inc(a_ot, 1)

        in_steps(act, [(OT, out_turned), (TR, turned), (SC, weights), (QKV, project)], N, LEAD)

    @block.vector
    def _(dve):
        def select(s, t):
            wait(dve, t_qkv, (s - 1) * 2)
            for a in range(A):
                head = dve.value_load(heads[0:1, bass.ds(s, 1), a:a + 1].rearrange("p s a -> p (s a)"), min_val=0, max_val=HEADS - 1)
                ins = dve.tensor_scalar(wsel[t % 2][:, :, :, a, :],
                                        wqkv[:, :, bass.ds(head, 1), :].rearrange("p k h (x d) -> p k (h x) d", x=3),
                                        picks[:, bass.ds(s, 1), a:a + 1].rearrange("p s a -> p (s a)"), None, ALU.mult)
            ins.then_inc(d_sel, 1)

        def shift(s, t):
            dve.wait_ge(t_sc, s + 1)
            sc = psc[0:T, :, 0:2 * T].rearrange("p x (y t) -> p x y t", y=2)
            best = top[0:T, :].rearrange("p (x y) -> p x y", x=2)
            dve.tensor_reduce(best, sc, AX_X, ALU.max).then_inc(d_mx, 1)
            dve.wait_ge(d_mx, s + 1)
            wait(dve, a_ex, s - 1)
            dve.tensor_tensor(sh[t % 2][0:T, :, :].rearrange("p (x y) t -> p x y t", x=2), sc,
                              best.unsqueeze(3).to_broadcast([T, 2, 2, T]),
                              ALU.subtract).then_inc(d_sh, 1)

        def normal(s, t):
            dve.wait_ge(t_o, s + 1)
            po3 = po[0:T, 0:A * (DH + 1)].rearrange("p (a d) -> p a d", a=A)
            dve.reciprocal(rec[0:T, :], po3[:, :, DH]).then_inc(d_rec, 1)
            dve.wait_ge(d_rec, s + 1)
            wait(dve, t_ot, s - 1)
            dve.tensor_tensor(o[t % 2][0:T, :, :], po3[:, :, 0:DH],
                              rec[0:T, :].unsqueeze(2).to_broadcast([T, A, DH]), ALU.mult).then_inc(d_o, 1)

        def residual(s, t):
            if isinstance(s, int):
                dve.wait_ge(loaded[t], 16 * (s // 4 + 1))
            else:
                dve.wait_ge(loaded[t], (s - t) * 4 + 16)
            dve.wait_ge(t_out, s + 1)
            dve.tensor_tensor(h[t][0:T, :], h[t][0:T, :], pout[0:T, 0:D], ALU.add).then_inc(d_h, 1)

        in_steps(dve, [(OUT, residual), (O, normal), (SC, shift), (SEL, select)], N, LEAD)

    @block.tensor
    def _(pe):
        pe.wait_ge(g_one, 4)

        def project(s, t):
            w = wsel[t % 2]
            x = xcur[t % 2]
            pe.wait_ge(g_x, s + 1)
            pe.wait_ge(d_sel, s + 1)
            wait(pe, a_qk, s)
            for c in range(4):
                out = pqk[:, c * T:(c + 1) * T]
                part = w[:, :, c // 2, 2 * (c % 2):2 * (c % 2) + 2, :].rearrange("p k a d -> p k (a d)")
                pe.matmul(out, part[0:1, KD, :], ones[0:1, 0:T], start=True, stop=False)
                for k in range(KD):
                    ins = pe.matmul(out, part[:, k, :], x[:, k, :], start=False, stop=(k == KD - 1))
            ins.then_inc(t_qkv, 1)
            wait(pe, a_v, s)
            part = w[:, :, 2, :, :].rearrange("p k a d -> p k (a d)")
            pe.matmul(pv[0:T, 0:D], ones[0:1, 0:T], part[0:1, KD, :], start=True, stop=False)
            for k in range(KD):
                ins = pe.matmul(pv[0:T, 0:D], x[:, k, :], part[:, k, :], start=False, stop=(k == KD - 1))
            ins.then_inc(t_qkv, 1)

        def scores(s, t):
            pe.wait_ge(a_qk, s + 1)
            wait(pe, d_sh, s)
            for a in range(A):
                rows = slice(DH * (a % 2), DH * (a % 2) + DH)
                ins = pe.matmul(psc[0:T, a % 2, (a // 2) * T:(a // 2 + 1) * T], qk[t % 2][rows, a // 2, :], qk[t % 2][rows, 2 + a // 2, :],
                                start=True, stop=True)
            ins.then_inc(t_sc, 1)

        def turn_weights(s, t):
            pe.wait_ge(a_ex, s + 1)
            wait(pe, a_tr, s)
            for a in range(A):
                ins = pe.transpose(ptr[0:T, a * T:(a + 1) * T], pr[t % 2][0:T, 2 * (a % 2) + a // 2, :], idf[0:T, 0:T])
            ins.then_inc(t_tr, 1)

        def weighted(s, t):
            pe.wait_ge(a_tr, s + 1)
            pe.wait_ge(a_v, s + 1)
            wait(pe, d_o, s)
            for a in range(A):
                ins = pe.matmul(po[0:T, a * (DH + 1):(a + 1) * (DH + 1)], prt[t % 2][0:T, a, :], v[t][0:T, a, :],
                                start=True, stop=True)
            ins.then_inc(t_o, 1)

        def turn_out(s, t):
            pe.wait_ge(d_o, s + 1)
            wait(pe, a_ot, s)
            for k in range(KD):
                ins = pe.transpose(pot[:, k * T:(k + 1) * T],
                                   o[t % 2][0:T, 2 * k:2 * k + 2, :].rearrange("p a d -> p (a d)"), idf[0:T, 0:T])
            ins.then_inc(t_ot, 1)

        def output(s, t):
            pe.wait_ge(a_ot, s + 1)
            wait(pe, d_h, s)
            for k in range(KD):
                pe.matmul(pout[0:T, 0:D], ot[t % 2][:, k, :], wo[:, k, :], start=(k == 0), stop=False)
            pe.matmul(pout[0:T, 0:D], ones[0:1, 0:T], brow[:], start=False, stop=True).then_inc(t_out, 1)

        in_steps(pe, [(OUT, output), (OT, turn_out), (O, weighted), (TR, turn_weights), (SC, scores), (QKV, project)],
                 N, LEAD)


KV = 4
REP = HEADS // KV
FR = DH // 2


def grouped_phase(nc, io, idf, h_in, h_out):
    with ExitStack() as ctx:
        m = Memory(nc, ctx, "g_")
        xnt = m.sb("xnt", [P, KD, SAMPLES * T])
        with ExitStack() as inner:
            n = Memory(nc, inner, "gn_")
            pt = [n.ps(f"pt{b}", [P, KD, 512]) for b in (0, 1)]
            norm = Norm(n, xnt, pt)
            block = inner.enter_context(nc.Block())

            @block.sync
            def _(sp):
                norm.sync(sp, h_in)

            @block.gpsimd
            def _(pool):
                norm.gpsimd(pool)

            @block.scalar
            def _(act):
                norm.scalar(act)

            @block.tensor
            def _(pe):
                norm.tensor(pe, idf)

            @block.vector
            def _(dve):
                norm.vector(dve)

        with ExitStack() as inner:
            grouped_attention(nc, Memory(nc, inner, "ga_"), inner, io, idf, xnt, h_in, h_out)


def grouped_attention(nc, m, ctx, io, idf, xnt, h_in, h_out):
    wq = m.sb("wq", [P, KD, REP, 2, P])
    wk = m.sb("wk", [P, KD, 2, P])
    wv = m.sb("wv", [P, KD, KV * DH])
    wo = m.sb("wo", [P, HEADS // 2, D])
    cos = m.sb("cos", [P, T])
    sin = m.sb("sin", [P, T])
    idb = m.sb("idb", [P, P], BF16)
    mask = m.sb("mask", [P, KV, T], BF16)
    turned_q = [m.sb(f"turned_q{b}", [P, REP, 2, QUAD, T]) for b in (0, 1)]
    keys = [m.sb(f"keys{b}", [P, 2, QUAD, KV, T]) for b in (0, 1)]
    qm = [m.sb(f"qm{b}", [P, 4, QUAD, T]) for b in (0, 1)]
    km = m.sb("km", [P, 4, QUAD, T])
    turned_k = m.sb("turned_k", [P, 2, QUAD, T])
    xcur = [m.sb(f"xcur{b}", [P, KD, T]) for b in (0, 1)]
    v = [m.sb(f"v{b}", [P, KV, DH + 1]) for b in (0, 1)]
    sh = [m.sb(f"sh{b}", [P, KV, T]) for b in (0, 1)]
    pr = [m.sb(f"pr{b}", [P, KV, T]) for b in (0, 1)]
    prt = [m.sb(f"prt{b}", [P, KV, T]) for b in (0, 1)]
    o = [m.sb(f"o{b}", [P, HEADS, DH]) for b in (0, 1)]
    ot = [m.sb(f"ot{b}", [P, HEADS // 2, T]) for b in (0, 1)]
    top = m.sb("top", [P, KV])
    rec = m.sb("rec", [P, KV])
    h = [m.sb(f"h{b}", [P, D]) for b in range(4)]
    pq = [m.ps(f"pq{b}", [P, 512]) for b in (0, 1)]
    pv = m.ps("pv", [P, 512])
    psc = m.ps("psc", [P, 512])
    ptr = m.ps("ptr", [P, 512])
    po = m.ps("po", [P, 512])
    pot = m.ps("pot", [P, 512])
    pout = m.ps("pout", [P, 512])

    weights = m.sem("weights")
    g_made = m.sem("g_made")
    t_k = m.sem("t_k")
    d_km = m.sem("d_km")
    g_k = m.sem("g_k")
    a_k = m.sem("a_k")
    t_q = m.sem("t_q")
    d_qm = m.sem("d_qm")
    g_q = m.sem("g_q")
    g_x = m.sem("g_x")
    t_v = m.sem("t_v")
    a_v = m.sem("a_v")
    t_sc = m.sem("t_sc")
    d_mx = m.sem("d_mx")
    d_sh = m.sem("d_sh")
    a_ex = m.sem("a_ex")
    t_tr = m.sem("t_tr")
    a_tr = m.sem("a_tr")
    t_o = m.sem("t_o")
    d_rec = m.sem("d_rec")
    d_o = m.sem("d_o")
    t_ot = m.sem("t_ot")
    a_ot = m.sem("a_ot")
    t_out = m.sem("t_out")
    d_h = m.sem("d_h")
    loaded = [m.sem(f"loaded{b}") for b in range(4)]
    stored = [m.sem(f"stored{b}") for b in range(4)]
    N, LEAD, UNROLL = SAMPLES, 16, 8
    CORE, LATE, OUT = 5, 6, 7
    block = ctx.enter_context(nc.Block())

    def per_quad(p, t):
        return (p - t % QUAD) // QUAD

    @block.sync
    def _(sp):
        for tile, name in ((wq[:].rearrange("p k r a c -> p k (r a c)"), "gwq"),
                           (wk[:].rearrange("p k a c -> p k (a c)"), "gwk"), (wv[:], "gwv"), (wo[:], "gwo")):
            sp.dma_start(tile, io[name].rearrange("(k p) n -> p k n", p=P)).then_inc(weights, 16)
        sp.dma_start(cos[:], io["cos"]).then_inc(weights, 16)
        sp.dma_start(sin[:], io["sin"]).then_inc(weights, 16)

        def load(s, t):
            if not isinstance(s, int):
                sp.wait_ge(stored[t % 4], (s - t % 4) * 4)
            elif s >= 4:
                sp.wait_ge(stored[t % 4], 16 * (s // 4))
            sp.dma_start(h[t % 4][0:T, :], h_in[bass.ds(s, 1), :, :].rearrange("s t d -> (s t) d"))\
                .then_inc(loaded[t % 4], 16)

        def store(s, t):
            sp.wait_ge(d_h, s + 1)
            sp.dma_start(h_out[bass.ds(s, 1), :, :].rearrange("s t d -> (s t) d"), h[t % 4][0:T, :])\
                .then_inc(stored[t % 4], 16)

        in_steps(sp, [(CORE, load), (OUT + 1, store)], N, LEAD, UNROLL)
        for t in range(4):
            sp.wait_ge(stored[t], 16 * (N // 4))

    @block.gpsimd
    def _(pool):
        for b in (0, 1):
            pool.memset(v[b][:, :, DH:], 1.0).then_inc(g_made, 1)
            pool.memset(keys[b][:].rearrange("p a s g t -> p (a s g t)"), 0.0).then_inc(g_made, 1)
        pool.memset(idb[:], 0.0).then_inc(g_made, 1)
        pool.memset(mask[:], 0.0).then_inc(g_made, 1)
        pool.wait_ge(g_made, 6)
        pool.affine_select(out=idb[:], in_=idb[:], compare_op=ALU.not_equal, fill=1.0, base=0,
                           pattern=[[-1, P]], channel_multiplier=1).then_inc(g_made, 1)
        pool.affine_select(out=mask[:], in_=mask[:], compare_op=ALU.is_ge, fill=-1e30, base=0,
                           pattern=[[0, KV], [-1, T]], channel_multiplier=1).then_inc(g_made, 1)

        def rotate_keys(p, t):
            if t % QUAD:
                return
            wait(pool, d_km, per_quad(p, t) + 1)
            wait(pool, a_k, per_quad(p, t))
            pool.tensor_tensor(turned_k[:, 0, :, :], km[:, 0, :, :], km[:, 1, :, :], ALU.subtract)
            pool.tensor_tensor(turned_k[:, 1, :, :], km[:, 2, :, :], km[:, 3, :, :], ALU.add).then_inc(g_k, 1)

        def rotate_queries(p, t):
            b, r = t // QUAD, t % QUAD
            pool.wait_ge(d_qm, p + 1)
            wait(pool, t_sc, (p - r - 8) * 4 + 16)
            q = qm[t % 2]
            pool.tensor_tensor(turned_q[b][:, r, 0, :, :], q[:, 0, :, :], q[:, 1, :, :], ALU.subtract)
            pool.tensor_tensor(turned_q[b][:, r, 1, :, :], q[:, 2, :, :], q[:, 3, :, :], ALU.add).then_inc(g_q, 1)

        def current(s, t):
            wait(pool, t_v, s - 1)
            pool.tensor_copy(xcur[t % 2][:], xnt[:, :, bass.ds(s * T, T)]).then_inc(g_x, 1)

        in_steps(pool, [(1, rotate_keys), (1, rotate_queries), (CORE - 1, current)], N, LEAD, UNROLL)

    @block.scalar
    def _(act):
        act.wait_ge(g_made, 8)

        def values(s, t):
            act.wait_ge(t_v, s + 1)
            wait(act, t_o, (s - 1) * 4)
            act.activation(v[t % 2][0:T, :, 0:DH], pv[0:T, 0:KV * DH].rearrange("p (a d) -> p a d", a=KV), ACT.Copy)\
                .then_inc(a_v, 1)

        def place_keys(p, t):
            if t % QUAD:
                return
            act.wait_ge(g_k, per_quad(p, t) + 1)
            wait(act, t_sc, (p - 8) * 4 + 16)
            for g in range(KV):
                rows = slice(32 * g, 32 * g + 32)
                for a in (0, 1):
                    ins = act.activation(keys[t // QUAD][rows, a, :, g, :], turned_k[rows, a, :, :], ACT.Copy)
            ins.then_inc(a_k, 1)

        def weigh(r):
            def work(s, t):
                act.wait_ge(d_sh, s * 4 + (r + 1))
                wait(act, t_tr, s * 4 + (r - 1))
                act.activation(pr[r % 2][0:T, :, :], sh[r % 2][0:T, :, :], ACT.Exp, scale=DH ** -0.5).then_inc(a_ex, 1)
            return work

        def turned(r):
            def work(s, t):
                act.wait_ge(t_tr, s * 4 + (r + 1))
                wait(act, t_o, s * 4 + (r - 1))
                act.activation(prt[r % 2][0:T, :, :].rearrange("p a t -> p (a t)"), ptr[0:T, 0:C], ACT.Copy)\
                    .then_inc(a_tr, 1)
            return work

        def out_turned(x):
            def work(s, t):
                act.wait_ge(t_ot, s * 2 + (x + 1))
                wait(act, t_out, s - 1)
                act.activation(ot[t % 2][:, 4 * x:4 * x + 4, :].rearrange("p k t -> p (k t)"), pot[:, 0:C], ACT.Copy)\
                    .then_inc(a_ot, 1)
            return work

        in_steps(act, [(CORE, values), (CORE, weigh(0)), (LATE, turned(3)), (2, place_keys), (CORE, weigh(1)), (CORE, turned(0)),
                       (CORE, weigh(2)), (CORE, turned(1)), (LATE, out_turned(0)),
                       (CORE, weigh(3)), (CORE, turned(2)), (LATE, out_turned(1))], N, LEAD, UNROLL)

    @block.vector
    def _(dve):
        dve.wait_ge(weights, 96)

        def rotation(out, sem):
            a, b = (pq[x][:, 0:C].rearrange("p (s t) -> p s t", s=QUAD) for x in (0, 1))
            c, s = (x[:].unsqueeze(1).to_broadcast([P, QUAD, T]) for x in (cos, sin))
            dve.tensor_tensor(out[:, 0, :, :], a, c, ALU.mult)
            dve.tensor_tensor(out[:, 1, :, :], b, s, ALU.mult)
            dve.tensor_tensor(out[:, 2, :, :], a, s, ALU.mult)
            dve.tensor_tensor(out[:, 3, :, :], b, c, ALU.mult).then_inc(sem, 1)

        def rope_keys(p, t):
            if t % QUAD:
                return
            wait(dve, t_k, per_quad(p, t) + 1)
            wait(dve, g_k, per_quad(p, t))
            rotation(km, d_km)

        def rope_queries(p, t):
            dve.wait_ge(t_q, p + 1)
            wait(dve, g_q, p - 1)
            rotation(qm[t % 2], d_qm)

        def shift(r):
            def work(s, t):
                dve.wait_ge(t_sc, s * 4 + (r + 1))
                sc = psc[0:T, 0:C].rearrange("p (a t) -> p a t", a=KV)
                dve.tensor_reduce(top[0:T, :], sc, AX_X, ALU.max).then_inc(d_mx, 1)
                dve.wait_ge(d_mx, s * 4 + (r + 1))
                wait(dve, a_ex, s * 4 + (r - 1))
                dve.tensor_tensor(sh[r % 2][0:T, :, :], sc, top[0:T, :].unsqueeze(2).to_broadcast([T, KV, T]),
                                  ALU.subtract).then_inc(d_sh, 1)
            return work

        def normal(r):
            def work(s, t):
                dve.wait_ge(t_o, s * 4 + (r + 1))
                po3 = po[0:T, 0:KV * (DH + 1)].rearrange("p (a d) -> p a d", a=KV)
                dve.reciprocal(rec[0:T, :], po3[:, :, DH]).then_inc(d_rec, 1)
                dve.wait_ge(d_rec, s * 4 + (r + 1))
                wait(dve, t_ot, (s - 1) * 2)
                dve.tensor_tensor(o[t % 2][0:T, r::REP, :], po3[:, :, 0:DH],
                                  rec[0:T, :].unsqueeze(2).to_broadcast([T, KV, DH]), ALU.mult).then_inc(d_o, 1)
            return work

        def residual(s, t):
            if isinstance(s, int):
                dve.wait_ge(loaded[t % 4], 16 * (s // 4 + 1))
            else:
                dve.wait_ge(loaded[t % 4], (s - t % 4) * 4 + 16)
            dve.wait_ge(t_out, s + 1)
            tile = h[t % 4][0:T, :]
            dve.tensor_tensor(tile, tile, pout[0:T, 0:D], ALU.add).then_inc(d_h, 1)

        in_steps(dve, [(0, rope_keys), (CORE, shift(0)), (LATE, normal(2)), (CORE, shift(1)), (OUT, residual),
                       (LATE, normal(3)), (0, rope_queries),
                       (CORE, shift(2)), (CORE, normal(0)), (CORE, shift(3)), (CORE, normal(1))], N, LEAD, UNROLL)

    @block.tensor
    def _(pe):
        pe.wait_ge(weights, 96)
        pe.wait_ge(g_made, 8)

        def project(w, cols):
            for a in (0, 1):
                for k in range(KD):
                    ins = pe.matmul(pq[a][:, 0:C], w[:, k, a, :], xnt[:, k, cols], start=(k == 0), stop=(k == KD - 1))
            return ins

        def project_keys(p, t):
            if t % QUAD:
                return
            wait(pe, d_qm, p)
            project(wk, bass.ds(p * T, C)).then_inc(t_k, 1)

        def project_queries(p, t):
            r = t % QUAD
            if r == 0:
                wait(pe, d_km, per_quad(p, t) + 1)
            wait(pe, d_qm, p)
            project(wq[:, :, r, :, :], bass.ds((p - r) * T, C)).then_inc(t_q, 1)

        def project_values(s, t):
            pe.wait_ge(g_x, s + 1)
            wait(pe, a_v, s)
            for k in range(KD):
                ins = pe.matmul(pv[0:T, 0:KV * DH], xcur[t % 2][:, k, :], wv[:, k, :], start=(k == 0), stop=(k == KD - 1))
            ins.then_inc(t_v, 1)

        def scores(r):
            def work(s, t):
                b, x = t // QUAD, t % QUAD
                if r == 0:
                    if x == 0:
                        wait(pe, a_k, per_quad(s, t) + 1)
                    wait(pe, g_q, (s - x) + 4)
                wait(pe, d_sh, s * 4 + r)
                out = psc[0:T, 0:C]
                for a in (0, 1):
                    pe.matmul(out, turned_q[b][:, r, a, x, :], keys[b][:, a, x, :, :].rearrange("p g t -> p (g t)"),
                              start=(a == 0), stop=False)
                pe.matmul(out, idb[0:T, 0:T], mask[0:T, :, :].rearrange("p g t -> p (g t)"), start=False, stop=True)\
                    .then_inc(t_sc, 1)
            return work

        def turn_weights(r):
            def work(s, t):
                pe.wait_ge(a_ex, s * 4 + (r + 1))
                wait(pe, a_tr, s * 4 + r)
                for g in range(KV):
                    ins = pe.transpose(ptr[0:T, g * T:(g + 1) * T], pr[r % 2][0:T, g, :], idf[0:T, 0:T])
                ins.then_inc(t_tr, 1)
            return work

        def weighted(r):
            def work(s, t):
                pe.wait_ge(a_tr, s * 4 + (r + 1))
                pe.wait_ge(a_v, s + 1)
                wait(pe, d_o, s * 4 + r)
                for g in range(KV):
                    ins = pe.matmul(po[0:T, g * (DH + 1):(g + 1) * (DH + 1)], prt[r % 2][0:T, g, :], v[t % 2][0:T, g, :],
                                    start=True, stop=True)
                ins.then_inc(t_o, 1)
            return work

        def turn_out(x):
            def work(s, t):
                pe.wait_ge(d_o, s * 4 + 4)
                wait(pe, a_ot, s * 2 + x)
                for k in range(4):
                    c = 4 * x + k
                    ins = pe.transpose(pot[:, k * T:(k + 1) * T], o[t % 2][0:T, 2 * c:2 * c + 2, :].rearrange("p a d -> p (a d)"),
                                       idf[0:T, 0:T])
                ins.then_inc(t_ot, 1)
            return work

        def output(s, t):
            pe.wait_ge(a_ot, s * 2 + 2)
            wait(pe, d_h, s)
            for k in range(HEADS // 2):
                ins = pe.matmul(pout[0:T, 0:D], ot[t % 2][:, k, :], wo[:, k, :], start=(k == 0), stop=(k == HEADS // 2 - 1))
            ins.then_inc(t_out, 1)

        in_steps(pe, [(CORE, project_values), (0, project_keys),
                      (CORE, scores(0)), (LATE, turn_weights(3)), (LATE, weighted(2)), (OUT, output),
                      (CORE, scores(1)), (CORE, turn_weights(0)), (LATE, weighted(3)),
                      (0, project_queries),
                      (CORE, scores(2)), (CORE, turn_weights(1)), (CORE, weighted(0)), (LATE, turn_out(0)),
                      (CORE, scores(3)), (CORE, turn_weights(2)), (CORE, weighted(1)), (LATE, turn_out(1))],
                 N, LEAD, UNROLL)


EXPERTS = 8
FFN = 1024
CAP = 128
GROUPS = 8
IN_GROUP = SAMPLES // GROUPS
HALF_GROUPS = GROUPS // 2
CHUNK = HALF_GROUPS * CAP
CHUNKS = 2 * EXPERTS
SLOTS = CHUNKS * CHUNK
SPARE = SLOTS


class RouterNorm(Norm):

    def __init__(self, m, pt, plg, wr, logits, x_out):
        xt = [m.sb(f"rxt{b}", [P, KD, C]) for b in (0, 1)]
        super().__init__(m, xt, pt, plg, None)
        self.wr, self.all_logits, self.x_out = wr, logits, x_out
        self.written = [m.sem(f"written{b}") for b in (0, 1)]
        self.wr_in = m.sem("wr_in")

    def xt_out(self, q, t, k):
        return self.xnt[t % 2][:, k, :]

    def kept(self, q):
        return self.all_logits[0:T, bass.ds(q * QUAD, QUAD), :]

    def source(self, b):
        return self.sums[b][0:T, :, :]

    def sync_and_write(self, sp, h_in):
        def load(q, t):
            wait(sp, self.d_xn, q - 3)
            sp.dma_start(self.h[t][0:T, :, :], h_in[bass.ds(q * QUAD, QUAD), :, :].rearrange("s t d -> t s d"))\
                .then_inc(self.loaded[t], 16)

        def write(q, t):
            b = t % 2
            sp.wait_ge(self.d_xn, q + 1)
            sp.dma_start(self.x_out[bass.ds(q * QUAD, QUAD), :, :].rearrange("s t d -> t s d"), self.xn[b][0:T, :, :])\
                .then_inc(self.written[b], 16)
        in_steps(sp, [(0, load), (2, write)], NQ, 4)
        for b in (0, 1):
            sp.wait_ge(self.written[b], 16 * (NQ // 2))

    def tensor(self, pe, idf):
        pe.wait_ge(self.wr_in, 16)

        def turn(q, t):
            b = t % 2
            pe.wait_ge(self.d_xn, q + 1)
            wait(pe, self.a_xt, (q - 1) * KD)
            for k in range(KD):
                for s in range(QUAD):
                    ins = pe.transpose(self.pt[b][:, k, s * T:(s + 1) * T], self.xn[b][0:T, s, k * P:(k + 1) * P],
                                       idf[0:T, 0:T])
            ins.then_inc(self.t_xt, 1)

        def logits(q, t):
            b = t % 2
            pe.wait_ge(self.a_xt, q * KD + KD)
            wait(pe, self.d_lg, q - 1)
            for s in range(QUAD):
                for k in range(KD):
                    ins = pe.matmul(self.sums[b][0:T, s, :], self.xnt[b][:, k, s * T:(s + 1) * T], self.wr[:, k, :],
                                    start=(k == 0), stop=(k == KD - 1))
            ins.then_inc(self.t_lg, 1)
        in_steps(pe, [(1, logits), (0, turn)], NQ, 4)


def expert_phase(nc, io, idf, h_in, out, x_dram, places, answers):
    with ExitStack() as ctx:
        m = Memory(nc, ctx, "e_")
        logits = m.sb("logits", [P, SAMPLES, EXPERTS])
        gates = m.sb("gates", [P, 2, SAMPLES])
        put = m.sb("put", [P, SAMPLES, 2], I32)
        get = m.sb("get", [P, SAMPLES, 2], I32)
        with ExitStack() as inner:
            n = Memory(nc, inner, "en_")
            wr = n.sb("wr", [P, KD, EXPERTS])
            zero = n.sb("zero", [P, CHUNK * D // P])
            pt = [n.ps(f"pt{b}", [P, KD, 512]) for b in (0, 1)]
            plg = [n.ps(f"plg{b}", [P, QUAD, EXPERTS]) for b in (0, 1)]
            norm = RouterNorm(n, pt, plg, wr, logits, x_dram)
            zeroed = n.sem("zeroed")
            cleared = n.sem("cleared")
            block = inner.enter_context(nc.Block())

            @block.sync
            def _(sp):
                sp.dma_start(wr[:], io["ewr"].rearrange("(k p) n -> p k n", p=P)).then_inc(norm.wr_in, 16)
                norm.sync_and_write(sp, h_in)
                sp.wait_ge(cleared, 16 * CHUNKS)

            @block.gpsimd
            def _(pool):
                norm.gpsimd(pool)

            @block.scalar
            def _(act):
                act.wait_ge(zeroed, 1)
                def clear(q):
                    act.dma_start(places[bass.ds(q * CHUNK, CHUNK), :].rearrange("(p r) d -> p (r d)", p=P), zero[:])\
                        .then_inc(cleared, 16)

                norm.scalar(act, clear)

            @block.tensor
            def _(pe):
                norm.tensor(pe, idf)

            @block.vector
            def _(dve):
                dve.memset(zero[:], 0.0).then_inc(zeroed, 1)
                norm.vector(dve)

        with ExitStack() as inner:
            choose(nc, Memory(nc, inner, "ec_"), inner, logits, gates, put, get)
        with ExitStack() as inner:
            experts(nc, Memory(nc, inner, "ex_"), inner, io, idf, gates, put, get, h_in, out, x_dram, places, answers)


def choose(nc, m, ctx, logits, gates, put, get):
    S, E = SAMPLES, EXPERTS
    FULL = [P, S, E]
    shifted = m.sb("shifted", FULL)
    probs = m.sb("probs", FULL)
    left = m.sb("left", FULL)
    rank = m.sb("rank", FULL)
    order = m.sb("order", FULL, I32)
    orderf = m.sb("orderf", FULL)
    base = m.sb("base", FULL, I32)
    basef = m.sb("basef", FULL)
    spare = m.sb("spare", [P, 2, S], I32)
    sparef = m.sb("sparef", [P, 2, S])
    small = m.sb("small", [P, 8, S])
    mask = [m.sb(f"mask{k}", FULL, BF16) for k in (0, 1)]
    upto = m.sb("upto", [P, T], BF16)
    every = m.sb("every", [P, T], BF16)
    before = m.sb("before", [P, 2, GROUPS, IN_GROUP + 1, E])
    pos = m.sb("pos", FULL)
    work = m.sb("work", FULL)
    keep = m.sb("keep", [P, 2, S])
    row = m.sb("row", [P, 2, S])
    pc = [m.ps(f"pc{k}", [P, 512]) for k in (0, 1)]
    pa = [m.ps(f"pa{k}", [P, 512]) for k in (0, 1)]
    d = m.sem("d")
    g = m.sem("g")
    a = m.sem("a")
    masks = m.sem("masks")
    t_c = m.sem("t_c")
    block = ctx.enter_context(nc.Block())

    @block.gpsimd
    def _(pool):
        pool.iota(order[:], [[0, S], [-1, E]], base=E, channel_multiplier=0).then_inc(g, 1)
        for half in (0, 1):
            part = base[:, half * S // 2:(half + 1) * S // 2, :]
            pool.iota(part, [[CAP, HALF_GROUPS], [0, IN_GROUP], [CHUNK, E]], base=half * EXPERTS * CHUNK - 1,
                      channel_multiplier=0).then_inc(g, 1)
        pool.iota(spare[:], [[P * S, 2], [P, S]], base=SPARE, channel_multiplier=1).then_inc(g, 1)
        pool.memset(upto[:], 1.0).then_inc(g, 1)
        pool.memset(every[:], 1.0).then_inc(g, 1)
        pool.wait_ge(g, 6)
        pool.affine_select(out=upto[:], in_=upto[:], compare_op=ALU.is_ge, fill=0.0, base=0,
                           pattern=[[1, T]], channel_multiplier=-1).then_inc(g, 1)

    @block.scalar
    def _(act):
        act.wait_ge(d, 5)
        act.activation(shifted[0:T, :, :], shifted[0:T, :, :], ACT.Exp).then_inc(a, 1)

    @block.tensor
    def _(pe):
        pe.wait_ge(g, 7)
        for k in (0, 1):
            pe.wait_ge(masks, k + 1)
            flat = mask[k][0:T, :, :].rearrange("p s e -> p (s e)")
            pe.matmul(pc[k][0:T, :], upto[0:T, :], flat, start=True, stop=True)
            pe.matmul(pa[k][0:T, :], every[0:T, :], flat, start=True, stop=True).then_inc(t_c, 1)

    @block.vector
    def _(dve):
        count = [0]

        def then(ins):
            count[0] += 1
            ins.then_inc(d, 1)
            dve.wait_ge(d, count[0])

        def wide(x):
            return x.unsqueeze(2).to_broadcast([T, S, E])

        full = (slice(0, T), slice(None), slice(None))
        dve.wait_ge(g, 7)
        then(dve.tensor_copy(orderf[:], order[:]))
        then(dve.tensor_copy(basef[:], base[:]))
        then(dve.tensor_copy(sparef[:], spare[:]))
        top, total, recip, best = (small[0:T, x, :] for x in range(4))
        then(dve.tensor_reduce(top, logits[full], AX_X, ALU.max))
        then(dve.tensor_tensor(shifted[full], logits[full], wide(top), ALU.subtract))
        dve.wait_ge(a, 1)
        then(dve.tensor_reduce(total, shifted[full], AX_X, ALU.add))
        then(dve.reciprocal(recip, total))
        then(dve.tensor_tensor(probs[full], shifted[full], wide(recip), ALU.mult))
        for k in (0, 1):
            src = (probs, left)[k]
            gate = small[0:T, 4 + k, :]
            then(dve.tensor_reduce(gate, src[full], AX_X, ALU.max))
            then(dve.tensor_tensor(rank[full], src[full], wide(gate), ALU.is_equal))
            then(dve.tensor_tensor(rank[full], rank[full], orderf[full], ALU.mult))
            then(dve.tensor_reduce(best, rank[full], AX_X, ALU.max))
            then(dve.tensor_tensor(work[full], rank[full], wide(best), ALU.is_equal))
            dve.tensor_copy(mask[k][full], work[full]).then_inc(masks, 1)
            if k == 0:
                then(dve.scalar_tensor_tensor(out=left[full], in0=work[full], scalar=-2.0, in1=probs[full],
                                              op0=ALU.mult, op1=ALU.add))
        then(dve.memset(before[0:T, 0, :, 0, :], 0.0))
        for k in (0, 1):
            dve.wait_ge(t_c, k + 1)
            sums = pa[k][0:T, :].rearrange("p (g s e) -> p g s e", g=GROUPS, s=IN_GROUP)
            for s in range(IN_GROUP):
                then(dve.tensor_tensor(before[0:T, k, :, s + 1, :], before[0:T, k, :, s, :], sums[:, :, s, :], ALU.add))
            if k == 0:
                then(dve.tensor_copy(before[0:T, 1, :, 0, :], before[0:T, 0, :, IN_GROUP, :]))
            then(dve.tensor_tensor(pos[full].rearrange("p (g s) e -> p g s e", g=GROUPS),
                                   pc[k][0:T, :].rearrange("p (g s e) -> p g s e", g=GROUPS, s=IN_GROUP),
                                   before[0:T, k, :, 0:IN_GROUP, :], ALU.add))
            then(dve.scalar_tensor_tensor(out=work[full], in0=pos[full], scalar=float(CAP), in1=mask[k][full],
                                          op0=ALU.is_le, op1=ALU.mult))
            then(dve.tensor_reduce(keep[0:T, k, :], work[full], AX_X, ALU.add))
            then(dve.tensor_tensor(pos[full], pos[full], basef[full], ALU.add))
            then(dve.tensor_tensor(work[full], work[full], pos[full], ALU.mult))
            then(dve.tensor_reduce(row[0:T, k, :], work[full], AX_X, ALU.add))
            then(dve.tensor_tensor(gates[0:T, k, :], small[0:T, 4 + k, :], keep[0:T, k, :], ALU.mult))
            S2 = S // 2
            then(dve.tensor_copy(get[0:T, 0:S2, k], row[0:T, k, 0:S2]))
            then(dve.scalar_tensor_tensor(out=small[0:T, 6, S2:S], in0=keep[0:T, k, S2:S], scalar=-float(SLOTS // 2),
                                          in1=row[0:T, k, S2:S], op0=ALU.mult, op1=ALU.add))
            then(dve.tensor_copy(get[0:T, S2:S, k], small[0:T, 6, S2:S]))
            then(dve.tensor_scalar(keep[0:T, k, :], keep[0:T, k, :], -1.0, 1.0, ALU.mult, ALU.add))
            then(dve.tensor_tensor(keep[0:T, k, :], keep[0:T, k, :], sparef[0:T, k, :], ALU.mult))
            then(dve.tensor_tensor(put[0:T, :, k], row[0:T, k, :], keep[0:T, k, :], ALU.add))


def experts(nc, m, ctx, io, idf, gates, put, get, h_in, out, x_dram, places, answers):
    FT = FFN // P
    wi = [m.sb(f"wi{b}", [P, KD, FFN]) for b in (0, 1)]
    wo = [m.sb(f"wo{b}", [P, FT, D]) for b in (0, 1)]
    tok = [m.sb(f"tok{b}", [P, HALF_GROUPS, D]) for b in (0, 1)]
    xt = [m.sb(f"xt{b}", [P, KD, CHUNK]) for b in (0, 1)]
    hid = [m.sb(f"hid{b}", [P, FT, CHUNK]) for b in (0, 1)]
    ans = [m.sb(f"ans{b}", [P, HALF_GROUPS, D]) for b in (0, 1)]
    index = [m.sb(f"index{b}", [P, QUAD, 2], I32) for b in (0, 1)]
    index2 = [m.sb(f"index2{b}", [P, QUAD, 2], I32) for b in (0, 1)]
    x = [m.sb(f"x{b}", [P, QUAD, D]) for b in (0, 1)]
    h = [m.sb(f"h{b}", [P, QUAD, D]) for b in (0, 1)]
    got = [m.sb(f"got{b}", [P, QUAD, 2, D]) for b in (0, 1)]
    pt = m.ps("pt", [P, KD, 512])
    pu = [m.ps(f"pu{b}", [P, 512]) for b in (0, 1)]
    pd = [m.ps(f"pd{b}", [P, 2, D]) for b in (0, 1)]

    idle = m.sb("idle", [1, 6])
    g_idle = m.sem("g_idle")
    g_met = [m.sem(f"g_met{i}") for i in range(5)]
    x_in = [m.sem(f"x_in{b}") for b in (0, 1)]
    sent = [m.sem(f"sent{b}") for b in (0, 1)]
    g_put = m.sem("g_put")
    loaded = [m.sem(f"loaded{b}") for b in (0, 1)]
    kept = [m.sem(f"kept{b}") for b in (0, 1)]
    t_t = m.sem("t_t")
    a_t = m.sem("a_t")
    t_u = m.sem("t_u")
    a_u = m.sem("a_u")
    t_d = m.sem("t_d")
    d_a = m.sem("d_a")
    g_get = m.sem("g_get")
    back = [m.sem(f"back{b}") for b in (0, 1)]
    d_c = m.sem("d_c")
    done = [m.sem(f"done{b}") for b in (0, 1)]
    MOVES = 16 * 2 * QUAD
    HALF = NQ // 2
    block = ctx.enter_context(nc.Block())

    def slot_uses(q, t, each):
        return (q - t % 2) * (each // 2) if not isinstance(q, int) else each * (q // 2)

    def quad_of(tensor, q):
        return tensor[bass.ds(q * QUAD, QUAD), :, :].rearrange("s t d -> t s d")

    @block.gpsimd
    def _(pool):
        pool.memset(idle[:], 0.0).then_inc(g_idle, 1)
        pool.wait_ge(g_idle, 1)

        def met(site, n):
            wait(pool, g_met[site], n)
            pool.tensor_tensor(idle[:, site + 1:site + 2], idle[:, 0:1], idle[:, 0:1], ALU.add).then_inc(g_met[site], 1)

        def take(q, t):
            b = t % 2
            wait(pool, sent[b], slot_uses(q, t, MOVES))
            met(0, q)
            pool.dma_start(x[b][0:T, :, :], quad_of(x_dram, q)).then_inc(x_in[b], 16)
            pool.tensor_copy(index[b][0:T, :, :], put[0:T, bass.ds(q * QUAD, QUAD), :]).then_inc(g_put, 1)

        def send(q, t):
            b = t % 2
            pool.wait_ge(g_put, q + 1)
            pool.wait_ge(x_in[b], slot_uses(q, t, 16) + 16)
            met(1, q)
            for s in range(QUAD):
                for k in (0, 1):
                    pool.indirect_dma_start(out=places[:, :], in_=x[b][0:T, s, :], in_offset=None,
                                            out_offset=bass.IndirectOffsetOnAxis(ap=index[b][0:T, s, k:k + 1], axis=0))\
                        .then_inc(sent[b], 16)

        in_steps(pool, [(0, take), (1, send)], NQ, 4, 2)

        def fetch_from(source):
            def work(q, t):
                b = t % 2
                if isinstance(q, int) and q % HALF == 0:
                    for i in (0, 1):
                        pool.wait_ge(kept[i], 16 * EXPERTS // 2 * (q // HALF + 1))
                wait(pool, done[b], slot_uses(q, t, 16))
                met(2, q)
                pool.dma_start(h[b][0:T, :, :], quad_of(h_in, q)).then_inc(back[b], 16)
                pool.tensor_copy(index2[b][0:T, :, :], get[0:T, bass.ds(q * QUAD, QUAD), :]).then_inc(g_get, 1)
                pool.wait_ge(g_get, q + 1)
                met(3, q)
                for s in range(QUAD):
                    for k in (0, 1):
                        pool.indirect_dma_start(out=got[b][0:T, s, k, :], out_offset=None, in_=source[:, :],
                                                in_offset=bass.IndirectOffsetOnAxis(ap=index2[b][0:T, s, k:k + 1], axis=0))\
                            .then_inc(back[b], 16)
            return work

        def write(q, t):
            pool.wait_ge(d_c, (q + 1) * 2 * QUAD)
            met(4, q)
            pool.dma_start(quad_of(out, q), h[t % 2][0:T, :, :]).then_inc(done[t % 2], 16)

        for half in (0, 1):
            in_steps(pool, [(0, fetch_from(answers[half])), (1, write)], HALF, 4, 2, base=half * HALF)
        for b in (0, 1):
            pool.wait_ge(done[b], 16 * NQ // 2)

    @block.sync
    def _(sp):
        def chunk(half, c, t):
            b = t % 2
            if isinstance(c, int) and c % EXPERTS == 0:
                for i in (0, 1):
                    sp.wait_ge(sent[i], MOVES * HALF // 2 * (c // EXPERTS + 1))
            wait(sp, t_d, (c - 1) * 2)
            e = c - half * EXPERTS
            sp.dma_start(wi[b][:], io["ewi"][bass.ds(e, 1), :, :].rearrange("e (k p) f -> p (e k) f", p=P)).then_inc(loaded[b], 16)
            sp.dma_start(wo[b][:], io["ewo"][bass.ds(e, 1), :, :].rearrange("e (k p) n -> p (e k) n", p=P)).then_inc(loaded[b], 16)
            sp.dma_start(tok[b][:], places[bass.ds(c * CHUNK, CHUNK), :].rearrange("(g p) d -> p g d", p=P))\
                .then_inc(loaded[b], 16)

        def keep(half, c, t):
            b = t % 2
            sp.wait_ge(d_a, c * 2 + 2)
            e = c - half * EXPERTS
            sp.dma_start(answers[half][bass.ds(e * CHUNK, CHUNK), :].rearrange("(g p) d -> p g d", p=P), ans[b][:])\
                .then_inc(kept[b], 16)

        for half in (0, 1):
            in_steps(sp, [(0, partial(chunk, half)), (2, partial(keep, half))], EXPERTS, 4, 2, base=half * EXPERTS)
        for b in (0, 1):
            sp.wait_ge(kept[b], 16 * CHUNKS // 2)

    def halves(eng, stages, second=()):
        for half in (0, 1):
            in_steps(eng, stages + (list(second) if half else []), EXPERTS, 4, 2, base=half * EXPERTS)

    @block.scalar
    def _(act):
        def empty(c, t):
            act.wait_ge(t_t, c + 1)
            for k in range(KD):
                act.activation(xt[t % 2][:, k, :], pt[:, k, :], ACT.Copy).then_inc(a_t, 1)

        def gelu(c, t):
            for f in range(FT):
                act.wait_ge(t_u, c * FT + (f + 1))
                act.activation(hid[t % 2][:, f, :], pu[f % 2][:], ACT.Gelu_apprx_tanh).then_inc(a_u, 1)

        halves(act, [(1, gelu), (0, empty)])

    @block.vector
    def _(dve):
        def answer(c, t):
            b = t % 2
            for r in (0, 1):
                dve.wait_ge(t_d, c * 2 + (r + 1))
                if r == 0:
                    wait(dve, kept[b], 16 * (c // 2) if isinstance(c, int) else (c - b) * 8)
                dve.tensor_copy(ans[b][:, 2 * r:2 * r + 2, :], pd[r][:]).then_inc(d_a, 1)

        def combine(q, t):
            b = t % 2
            dve.wait_ge(back[b], slot_uses(q, t, MOVES + 16) + MOVES + 16)
            for k in (0, 1):
                for s in range(QUAD):
                    if k:
                        dve.wait_ge(d_c, q * 2 * QUAD + (s + 1))
                    tile = h[b][0:T, s, :]
                    dve.scalar_tensor_tensor(out=tile, in0=got[b][0:T, s, k, :],
                                             scalar=gates[0:T, k, bass.ds(q * QUAD + s, 1)], in1=tile,
                                             op0=ALU.mult, op1=ALU.add).then_inc(d_c, 1)

        def combine_first(c, t):
            combine(c - EXPERTS, t)

        halves(dve, [(1, answer)], [(1, combine_first)])
        in_steps(dve, [(0, combine)], HALF, 4, 2, base=HALF)

    @block.tensor
    def _(pe):
        def turn(c, t):
            b = t % 2
            if isinstance(c, int):
                pe.wait_ge(loaded[b], 48 * (c // 2 + 1))
            else:
                pe.wait_ge(loaded[b], (c - b) * 24 + 48)
            wait(pe, a_t, c * 2)
            for k in range(KD):
                for g in range(HALF_GROUPS):
                    ins = pe.transpose(pt[:, k, g * P:(g + 1) * P], tok[b][:, g, k * P:(k + 1) * P], idf[:, :])
            ins.then_inc(t_t, 1)

        def up(c, t):
            b = t % 2
            pe.wait_ge(a_t, c * 2 + 2)
            for f in range(FT):
                wait(pe, a_u, c * FT + (f - 1))
                for k in range(KD):
                    ins = pe.matmul(pu[f % 2][:], wi[b][:, k, f * P:(f + 1) * P], xt[b][:, k, :],
                                    start=(k == 0), stop=(k == KD - 1))
                ins.then_inc(t_u, 1)

        def down(c, t):
            b = t % 2
            pe.wait_ge(a_u, c * FT + FT)
            for r in (0, 1):
                wait(pe, d_a, (c - 1) * 2 + (r + 1))
                for g in (2 * r, 2 * r + 1):
                    for f in range(FT):
                        ins = pe.matmul(pd[r][:, g % 2, :], hid[b][:, f, g * P:(g + 1) * P], wo[b][:, f, :],
                                        start=(f == 0), stop=(f == FT - 1))
                ins.then_inc(t_d, 1)

        halves(pe, [(1, up), (0, turn), (1, down)])


def clear_semaphores(nc, used):
    with ExitStack() as ctx:
        block = ctx.enter_context(nc.Block())

        @block.gpsimd
        def _(pool):
            for semaphore in used:
                pool.sem_clear(semaphore)


def build(nc, io, out, scratch, rows):
    with ExitStack() as ctx:
        idf = ctx.enter_context(nc.sbuf_tensor("idf", [P, P], F32))
        used = make_identity(nc, idf)
        used = used + mixer_phase(nc, io, idf, scratch[0])
        clear_semaphores(nc, used)
        routed_phase(nc, io, idf, scratch[0], scratch[1])
        grouped_phase(nc, io, idf, scratch[1], scratch[2])
        expert_phase(nc, io, idf, scratch[2], out, *rows)


def kernel(**inputs):
    import numpy as _np
    import concourse.bacc as _bacc
    from concourse import mybir as _mybir
    from concourse.bass_utils import run_bass_kernel_spmd as _run

    a = {k: _np.ascontiguousarray(v) for k, v in inputs.items()}
    x = a["x"].reshape(16, 4, 3, 6, 16, 6, 16).transpose(0, 2, 4, 6, 1, 3, 5)
    x = _np.pad(x.reshape(16, 6, 128, 4, 36), ((0, 0),) * 4 + ((0, 28),))
    x = x.reshape(16, 6, 128, 256).transpose(0, 2, 1, 3)

    def cols(v, n):
        return v.reshape(4, 128, n).transpose(1, 0, 2).reshape(128, 4 * n)

    data = {
        "patches": x,
        "txt": a["txt"],
        "tokw": a["L0_tok_W"],
        "w1": a["L0_attn_W1"], "w2": a["L0_attn_W2"],
        "xpw": a["L0_attn_x_proj_w"], "dtw": a["L0_attn_dt_proj_w"], "wo0": a["L0_attn_Wo"],
        "cols": _np.concatenate([cols(a["L0_attn_b1"], 1), cols(a["L0_attn_b2"], 1), cols(a["L0_attn_conv_w"], 4),
                                 cols(a["L0_attn_conv_b"], 1), cols(a["L0_attn_dt_proj_b"], 1),
                                 cols(a["L0_attn_D_skip"], 1), cols(a["L0_attn_A_log"], 16)], axis=1),
        "brow": _np.concatenate([a["L0_tok_b"], a["L0_attn_bo"], a["L0_ffn_bo"]]).reshape(1, 3, 256),
    }
    data["rwqkv"] = _np.stack([a["L0_ffn_W" + w].reshape(256, 16, 64) for w in "qkv"], axis=2).reshape(256, 16, 192)
    data["rbias"] = _np.stack([a["L0_ffn_b" + w].reshape(16, 64) for w in "qkv"], axis=1).reshape(1, 16, 192)
    data["rwr"] = a["L0_ffn_Wr"]
    data["rwo"] = a["L0_ffn_Wo"]
    data["rbr"] = _np.broadcast_to(a["L0_ffn_br"], (64, 16))
    data["gwq"] = a["L1_attn_Wq"].reshape(256, 4, 4, 32, 2).transpose(0, 2, 4, 1, 3).reshape(256, 1024)
    data["gwk"] = a["L1_attn_Wk"].reshape(256, 4, 32, 2).transpose(0, 3, 1, 2).reshape(256, 256)
    data["gwv"], data["gwo"] = a["L1_attn_Wv"], a["L1_attn_Wo"]
    rate = (1.0 / 10000.0 ** (_np.arange(0, 64, 2, dtype=_np.float32) / _np.float32(64))).astype(_np.float32)
    angle = _np.arange(113, dtype=_np.float32)[None, :] * rate[:, None]
    data["cos"] = _np.tile(_np.cos(angle).astype(_np.float32), (4, 1))
    data["sin"] = _np.tile(_np.sin(angle).astype(_np.float32), (4, 1))
    data["ewr"], data["ewi"], data["ewo"] = a["L1_ffn_w_router"], a["L1_ffn_wi"], a["L1_ffn_wo"]
    nc = _bacc.Bacc("TRN2", target_bir_lowering=False, num_devices=1)
    arrays, io = {}, {}
    for name, v in data.items():
        v = _np.ascontiguousarray(v)
        arrays[f"in_{name}"] = v
        io[name] = nc.dram_tensor(f"in_{name}", v.shape, _mybir.dt.from_np(v.dtype), kind="ExternalInput").ap()
    out = nc.dram_tensor("out_h", (64, 113, 256), _mybir.dt.float32, kind="ExternalOutput").ap()
    scratch = [nc.dram_tensor(f"h{i}", (64, 113, 256), _mybir.dt.float32, kind="Internal").ap() for i in range(3)]
    rows = [nc.dram_tensor("normal", (64, 113, 256), _mybir.dt.float32, kind="Internal").ap(),
            nc.dram_tensor("places", (SLOTS + 2 * P * SAMPLES, 256), _mybir.dt.float32, kind="Internal").ap(),
            [nc.dram_tensor(f"answers{i}", (SLOTS // 2, 256), _mybir.dt.float32, kind="Internal").ap() for i in (0, 1)]]
    build(nc, io, out, scratch, rows)
    r = _run(nc, [arrays], core_ids=[0])
    return r.results[0]["out_h"]
```
